# Optimizing a Trainium2 kernel written in Bass

```python
import numpy as np
import jax
import jax.numpy as jnp

def _softmax(x, axis=-1):
    return jax.nn.softmax(x, axis=axis)

def _gelu(x):
    return jax.nn.gelu(x, approximate=True)

def _silu(x):
    return jax.nn.silu(x)

def _sigmoid(x):
    return jax.nn.sigmoid(x)

def _layernorm(x, axis=-1, eps=1e-05):
    m = jnp.mean(x, axis=axis, keepdims=True)
    v = jnp.var(x, axis=axis, keepdims=True)
    return (x - m) / jnp.sqrt(v + eps)

def _scatter_add(tgt, idx, src, axis=0):
    return tgt.at[idx].add(src)

def _segment_sum(src, seg, n):
    return jax.ops.segment_sum(src, seg, n)
kernel_name = 'mk_flamingo_gated_d2_seqx_r8_4375a6'

def setup_inputs(seed: int=0):
    np.random.seed(seed)
    _w = jnp.asarray

    def _rec_inputs():
        import jax
        import jax.numpy as jnp
        _rk = jax.random.key(seed)
        x = -0.0005207 + 1.001 * jax.random.normal(jax.random.fold_in(_rk, 1), (16, 56, 128), jnp.float32)
        _lenS = 56 - jax.random.randint(jax.random.fold_in(_rk, 7), (16,), 0, max(1, 56 // 4) + 1, jnp.int32)
        _lenS2 = 1500 - jax.random.randint(jax.random.fold_in(_rk, 8), (16,), 0, max(1, 1500 // 4) + 1, jnp.int32)
        _ctx_1024P = jax.random.normal(jax.random.fold_in(_rk, 11), (16, 16, 128), jnp.float32)
        _ctx_1024c = jax.random.dirichlet(jax.random.fold_in(_rk, 511), 0.3 * jnp.ones((16,), jnp.float32), (16, 1500))
        _ctx_1024t = jnp.einsum('bsk,bkd->bsd', _ctx_1024c, _ctx_1024P)
        _ctx_1024t = _ctx_1024t * jax.lax.rsqrt(jnp.mean(jnp.square(_ctx_1024t)) + 1e-12) * 0.953939
        ctx_1024 = -5.72187e-05 + 0.999849 * (_ctx_1024t + 0.3 * jax.random.normal(jax.random.fold_in(_rk, 611), (16, 1500, 128), jnp.float32))
        _validS = jnp.arange(56)[None, :] < _lenS[:, None]
        _validS2 = jnp.arange(1500)[None, :] < _lenS2[:, None]
        _causal = jnp.tril(jnp.ones((56, 56), dtype=bool))
        mask_BxS2_bf0 = jnp.logical_not(jnp.ones((16, 1500), dtype=bool))
        _g = jax.random.normal(jax.random.fold_in(_rk, 9001), (2, 2), jnp.float32)
        _g = jnp.sign(_g) * jnp.maximum(jnp.abs(_g), 1.0) + (_g == 0) * 1.0
        g_xattn = _g[0]
        g_ffn = _g[1]
        return (x, ctx_1024, mask_BxS2_bf0, g_xattn, g_ffn)
    x, ctx_1024, mask_BxS2_bf0, g_xattn, g_ffn = _rec_inputs()

    def _L0_xattn_setup():
        import jax, jax.numpy as jnp
        import numpy as np
        key = jax.random.key(seed)
        ks = jax.random.split(key, 5)
        b, n_q, n_kv = (16, 128, 512)
        query_dim, context_dim, heads, dim_head = (128, 128, 16, 64)
        inner = heads * dim_head
        x = jax.random.normal(ks[0], (b, n_q, query_dim), dtype=jnp.float32)
        context = jax.random.normal(ks[1], (b, n_kv, context_dim), dtype=jnp.float32)
        Wq = jax.random.normal(ks[2], (query_dim, inner), dtype=jnp.float32) * query_dim ** (-0.5)
        Wkv = jax.random.normal(ks[3], (context_dim, 2 * inner), dtype=jnp.float32) * context_dim ** (-0.5)
        Wout = jax.random.normal(ks[4], (inner, query_dim), dtype=jnp.float32) * inner ** (-0.5)
        bout = jnp.zeros((query_dim,), dtype=jnp.float32)
        return {'x': x, 'context': context, 'Wq': Wq, 'Wkv': Wkv, 'Wout': Wout, 'bout': bout}
    _L0_xattn_all = _L0_xattn_setup()
    _L0_xattn_in = {k: v for k, v in _L0_xattn_all.items() if k in ('Wq', 'Wkv', 'Wout', 'bout')}
    del _L0_xattn_all

    def _L0_ffn_setup():
        import jax, jax.numpy as jnp
        import numpy as np
        B, S, D, O, E, K = (2, 256, 128, 128, 8, 2)
        key = jax.random.key(seed)
        ks = jax.random.split(key, 6)

        def w(k, shape, fan_in):
            return jax.random.normal(k, shape, jnp.float32) * fan_in ** (-0.5)
        return {'x': jax.random.normal(ks[0], (B, S, D), jnp.float32), 'gate_w': w(ks[1], (E, D), D), 'gate_b': jnp.zeros((E,), jnp.float32), 'w1': w(ks[2], (E, D, O), D), 'b1': jnp.zeros((E, O), jnp.float32), 'w2': w(ks[3], (E, O, O), O), 'b2': jnp.zeros((E, O), jnp.float32), 'w3': w(ks[4], (E, O, O), O), 'b3': jnp.zeros((E, O), jnp.float32)}
    _L0_ffn_all = _L0_ffn_setup()
    _L0_ffn_in = {k: v for k, v in _L0_ffn_all.items() if k in ('gate_w', 'gate_b', 'w1', 'b1', 'w2', 'b2', 'w3', 'b3')}
    del _L0_ffn_all

    def _L1_xattn_setup():
        import jax, jax.numpy as jnp
        import numpy as np
        B, SQ, SKV, D, H = (2, 256, 256, 128, 16)
        HD = D // H

        def cross_attention(query, context, mask, Wq, bq, Wkv, bkv, Wout, bout, num_heads):
            b, sq, d = query.shape
            skv = context.shape[1]
            hd = d // num_heads
            scale = hd ** (-0.5)
            q = query @ Wq + bq
            kv = context @ Wkv + bkv
            kv = kv.reshape(b, skv, 2, num_heads, hd).transpose(2, 0, 3, 1, 4)
            k, v = (kv[0], kv[1])
            q = q.reshape(b, sq, num_heads, hd).transpose(0, 2, 1, 3)
            scores = jnp.einsum('bhid,bhjd->bhij', q, k) * scale
            scores = jnp.where(mask[:, None, None, :], -jnp.inf, scores)
            attn = jax.nn.softmax(scores, axis=-1)
            out = jnp.einsum('bhij,bhjd->bhid', attn, v)
            out = out.transpose(0, 2, 1, 3).reshape(b, sq, d)
            return out @ Wout + bout
        key = jax.random.key(seed)
        ks = jax.random.split(key, 6)
        scale = 1.0 / np.sqrt(D)
        return {'query': jax.random.normal(ks[0], (B, SQ, D), dtype=jnp.float32), 'context': jax.random.normal(ks[1], (B, SKV, D), dtype=jnp.float32), 'mask': jnp.zeros((B, SKV), dtype=bool), 'Wq': jax.random.normal(ks[2], (D, D), dtype=jnp.float32) * scale, 'bq': jnp.zeros((D,), dtype=jnp.float32), 'Wkv': jax.random.normal(ks[3], (D, 2 * D), dtype=jnp.float32) * scale, 'bkv': jnp.zeros((2 * D,), dtype=jnp.float32), 'Wout': jax.random.normal(ks[4], (D, D), dtype=jnp.float32) * scale, 'bout': jnp.zeros((D,), dtype=jnp.float32), 'num_heads': H}
    _L1_xattn_all = _L1_xattn_setup()
    _L1_xattn_in = {k: v for k, v in _L1_xattn_all.items() if k in ('Wq', 'bq', 'Wkv', 'bkv', 'Wout', 'bout')}
    del _L1_xattn_all

    def _L1_ffn_setup():
        import jax, jax.numpy as jnp
        import numpy as np
        TAU = 1.0
        K_ROUTE = 3
        EPS = 1e-08

        def _route_combine_weights(x_addr, U, k, tau):
            z = x_addr @ U.T
            topv, topi = jax.lax.top_k(z, k)
            w = jax.nn.softmax(topv / (tau + EPS), axis=1)
            N, L = z.shape
            rows = jnp.arange(N)[:, None]
            return jnp.zeros((N, L), z.dtype).at[rows, topi].add(w)

        def _mixture(inp, C, W):
            L = W.shape[0]
            y = jnp.zeros((inp.shape[0], W.shape[1]), inp.dtype)
            for e in range(L):
                y = y + C[:, e:e + 1] * (inp @ W[e].T)
            return y
        key = jax.random.key(seed)
        ks = jax.random.split(key, 8)
        B, T, D_in, H, D_out, L, d_addr = (8, 1024, 128, 128, 128, 12, 64)

        def unit_rows(k, L_, d_):
            U = jax.random.normal(k, (L_, d_), dtype=jnp.float32)
            U = U - U.mean(axis=1, keepdims=True)
            return U / (jnp.linalg.norm(U, axis=1, keepdims=True) + EPS)

        def norm_tape(k, shape):
            W = jax.random.normal(k, shape, dtype=jnp.float32)
            n = jnp.sqrt(jnp.sum(W * W, axis=tuple(range(1, W.ndim)), keepdims=True)) + 1e-12
            return W / n
        x = jax.random.normal(ks[0], (B, T, D_in), dtype=jnp.float32)
        P_w = jax.random.normal(ks[1], (d_addr, D_in), dtype=jnp.float32) / np.sqrt(D_in)
        U1 = unit_rows(ks[2], L, d_addr)
        U2 = unit_rows(ks[3], L, d_addr)
        U3 = unit_rows(ks[4], L, d_addr)
        W1 = norm_tape(ks[5], (L, H, D_in))
        W2 = norm_tape(ks[6], (L, D_out, H))
        b2 = norm_tape(ks[7], (L, D_out))
        return {'x': x, 'P_w': P_w, 'U1': U1, 'U2': U2, 'U3': U3, 'W1': W1, 'W2': W2, 'b2': b2}
    _L1_ffn_all = _L1_ffn_setup()
    _L1_ffn_in = {k: v for k, v in _L1_ffn_all.items() if k in ('P_w', 'U1', 'U2', 'U3', 'W1', 'W2', 'b2')}
    del _L1_ffn_all
    return {'x': x, 'ctx_1024': ctx_1024, 'mask_BxS2_bf0': mask_BxS2_bf0, 'g_xattn': g_xattn, 'g_ffn': g_ffn, 'L0_xattn_Wq': _L0_xattn_in['Wq'], 'L0_xattn_Wkv': _L0_xattn_in['Wkv'], 'L0_xattn_Wout': _L0_xattn_in['Wout'], 'L0_xattn_bout': _L0_xattn_in['bout'], 'L0_ffn_gate_w': _L0_ffn_in['gate_w'], 'L0_ffn_gate_b': _L0_ffn_in['gate_b'], 'L0_ffn_w1': _L0_ffn_in['w1'], 'L0_ffn_b1': _L0_ffn_in['b1'], 'L0_ffn_w2': _L0_ffn_in['w2'], 'L0_ffn_b2': _L0_ffn_in['b2'], 'L0_ffn_w3': _L0_ffn_in['w3'], 'L0_ffn_b3': _L0_ffn_in['b3'], 'L1_xattn_Wq': _L1_xattn_in['Wq'], 'L1_xattn_bq': _L1_xattn_in['bq'], 'L1_xattn_Wkv': _L1_xattn_in['Wkv'], 'L1_xattn_bkv': _L1_xattn_in['bkv'], 'L1_xattn_Wout': _L1_xattn_in['Wout'], 'L1_xattn_bout': _L1_xattn_in['bout'], 'L1_ffn_P_w': _L1_ffn_in['P_w'], 'L1_ffn_U1': _L1_ffn_in['U1'], 'L1_ffn_U2': _L1_ffn_in['U2'], 'L1_ffn_U3': _L1_ffn_in['U3'], 'L1_ffn_W1': _L1_ffn_in['W1'], 'L1_ffn_W2': _L1_ffn_in['W2'], 'L1_ffn_b2': _L1_ffn_in['b2']}

def reference(x, ctx_1024, mask_BxS2_bf0, g_xattn, g_ffn, L0_xattn_Wq, L0_xattn_Wkv, L0_xattn_Wout, L0_xattn_bout, L0_ffn_gate_w, L0_ffn_gate_b, L0_ffn_w1, L0_ffn_b1, L0_ffn_w2, L0_ffn_b2, L0_ffn_w3, L0_ffn_b3, L1_xattn_Wq, L1_xattn_bq, L1_xattn_Wkv, L1_xattn_bkv, L1_xattn_Wout, L1_xattn_bout, L1_ffn_P_w, L1_ffn_U1, L1_ffn_U2, L1_ffn_U3, L1_ffn_W1, L1_ffn_W2, L1_ffn_b2):
    import jax
    import jax.numpy as jnp

    def _L0_xattn_ref(x, context, Wq, Wkv, Wout, bout):
        import jax, jax.numpy as jnp
        import numpy as np
        heads, dim_head = (16, 64)
        b, n_q, _ = x.shape
        n_kv = context.shape[1]
        scale = dim_head ** (-0.5)
        q = x @ Wq
        kv = context @ Wkv
        k, v = jnp.split(kv, 2, axis=-1)

        def split_heads(t):
            bb, n, _ = t.shape
            return t.reshape(bb, n, heads, dim_head).transpose(0, 2, 1, 3)
        q, k, v = map(split_heads, (q, k, v))
        i_idx = jnp.arange(n_q)[:, None]
        j_idx = jnp.arange(n_kv)[None, :]
        mask = j_idx % n_q == i_idx
        sim = jnp.einsum('bhid,bhjd->bhij', q, k) * scale
        max_neg = -jnp.finfo(sim.dtype).max
        sim = jnp.where(mask[None, None, :, :], sim, max_neg)
        attn = jax.nn.softmax(sim, axis=-1)
        out = jnp.einsum('bhij,bhjd->bhid', attn, v)
        out = out.transpose(0, 2, 1, 3).reshape(b, n_q, heads * dim_head)
        return out @ Wout + bout

    def _L0_ffn_ref(x, gate_w, gate_b, w1, b1, w2, b2, w3, b3):
        import jax, jax.numpy as jnp
        import numpy as np
        B, S, D, O, E, K = (2, 256, 128, 128, 8, 2)
        probs = jax.nn.softmax(x @ gate_w.T + gate_b, axis=-1)
        _, topi = jax.lax.top_k(probs, K)
        onehot = jax.nn.one_hot(topi, E, dtype=probs.dtype)
        cw = jnp.einsum('bske,bsk->bse', onehot, probs[..., :K])
        out = jnp.zeros(x.shape[:2] + (O,), x.dtype)
        for e in range(E):
            h = jax.nn.relu(x @ w1[e] + b1[e])
            h = jax.nn.relu(h @ w2[e] + b2[e])
            h = h @ w3[e] + b3[e]
            out = out + cw[..., e:e + 1] * h
        return out

    def _L1_xattn_ref(query, context, mask, Wq, bq, Wkv, bkv, Wout, bout, num_heads):
        import jax, jax.numpy as jnp
        import numpy as np
        B, SQ, SKV, D, H = (2, 256, 256, 128, 16)
        HD = D // H

        def cross_attention(query, context, mask, Wq, bq, Wkv, bkv, Wout, bout, num_heads):
            b, sq, d = query.shape
            skv = context.shape[1]
            hd = d // num_heads
            scale = hd ** (-0.5)
            q = query @ Wq + bq
            kv = context @ Wkv + bkv
            kv = kv.reshape(b, skv, 2, num_heads, hd).transpose(2, 0, 3, 1, 4)
            k, v = (kv[0], kv[1])
            q = q.reshape(b, sq, num_heads, hd).transpose(0, 2, 1, 3)
            scores = jnp.einsum('bhid,bhjd->bhij', q, k) * scale
            scores = jnp.where(mask[:, None, None, :], -jnp.inf, scores)
            attn = jax.nn.softmax(scores, axis=-1)
            out = jnp.einsum('bhij,bhjd->bhid', attn, v)
            out = out.transpose(0, 2, 1, 3).reshape(b, sq, d)
            return out @ Wout + bout
        return cross_attention(query, context, mask, Wq, bq, Wkv, bkv, Wout, bout, num_heads)

    def _L1_ffn_ref(x, P_w, U1, U2, U3, W1, W2, b2):
        import jax, jax.numpy as jnp
        import numpy as np
        TAU = 1.0
        K_ROUTE = 3
        EPS = 1e-08

        def _route_combine_weights(x_addr, U, k, tau):
            z = x_addr @ U.T
            topv, topi = jax.lax.top_k(z, k)
            w = jax.nn.softmax(topv / (tau + EPS), axis=1)
            N, L = z.shape
            rows = jnp.arange(N)[:, None]
            return jnp.zeros((N, L), z.dtype).at[rows, topi].add(w)

        def _mixture(inp, C, W):
            L = W.shape[0]
            y = jnp.zeros((inp.shape[0], W.shape[1]), inp.dtype)
            for e in range(L):
                y = y + C[:, e:e + 1] * (inp @ W[e].T)
            return y
        B, T, D = x.shape
        xf = x.reshape(B * T, D)
        xa = xf @ P_w.T
        C1 = _route_combine_weights(xa, U1, K_ROUTE, TAU)
        C2 = _route_combine_weights(xa, U2, K_ROUTE, TAU)
        C3 = _route_combine_weights(xa, U3, K_ROUTE, TAU)
        h = jax.nn.gelu(_mixture(xf, C1, W1), approximate=False)
        y = _mixture(h, C2, W2) + C3 @ b2
        return y.reshape(B, T, -1)
    x = x + jnp.tanh(g_xattn[0]) * _L0_xattn_ref(_layernorm(x, axis=-1), ctx_1024, L0_xattn_Wq, L0_xattn_Wkv, L0_xattn_Wout, L0_xattn_bout)
    x = x + jnp.tanh(g_ffn[0]) * _L0_ffn_ref(_layernorm(x, axis=-1), L0_ffn_gate_w, L0_ffn_gate_b, L0_ffn_w1, L0_ffn_b1, L0_ffn_w2, L0_ffn_b2, L0_ffn_w3, L0_ffn_b3)
    x = x + jnp.tanh(g_xattn[1]) * _L1_xattn_ref(_layernorm(x, axis=-1), ctx_1024, mask_BxS2_bf0, L1_xattn_Wq, L1_xattn_bq, L1_xattn_Wkv, L1_xattn_bkv, L1_xattn_Wout, L1_xattn_bout, 16)
    x = x + jnp.tanh(g_ffn[1]) * _L1_ffn_ref(_layernorm(x, axis=-1), L1_ffn_P_w, L1_ffn_U1, L1_ffn_U2, L1_ffn_U3, L1_ffn_W1, L1_ffn_W2, L1_ffn_b2)
    return x

_drawn_inputs = setup_inputs


def setup_inputs(seed=0):
    import zlib

    import numpy as np

    out = dict(_drawn_inputs(seed))
    spreads = {'g_ffn': (-1.0, 0.6),
     'L0_xattn_bout': (0.0, 0.1),
     'L0_ffn_gate_b': (0.0, 0.283),
     'L0_ffn_b1': (0.0, 0.8),
     'L0_ffn_b2': (0.0, 0.8),
     'L0_ffn_b3': (0.0, 0.565),
     'L1_xattn_bq': (0.0, 0.482),
     'L1_xattn_bkv': (0.0, 0.1),
     'L1_xattn_bout': (0.0, 0.1)}
    factors = {'L1_ffn_U1': 8.0, 'L1_ffn_U2': 8.0, 'L1_ffn_W1': 8.0, 'L1_ffn_W2': 8.0}
    for name, (base, spread) in spreads.items():
        noise = np.random.default_rng([zlib.crc32(name.encode()), seed]).standard_normal(out[name].shape)
        drawn = base * np.exp(spread * noise) if base else spread * noise
        out[name] = jnp.asarray(drawn.astype(out[name].dtype))
    for name, factor in factors.items():
        out[name] = (out[name] * factor).astype(out[name].dtype)
    return out
```

```python
from contextlib import ExitStack

import concourse.bass as bass
from concourse import mybir

F32 = mybir.dt.float32
F32R = mybir.dt.float32r
BF16 = mybir.dt.bfloat16
U8 = mybir.dt.uint8
ALU = mybir.AluOpType
ACT = mybir.ActivationFunctionType
AX = mybir.AxisListType.X

P = 128
B, SQ, SK, D = 16, 56, 1500, 128
TOK = B * SQ
NT = TOK // P
HALVES = ((0, 4), (4, 3))
H = 16
DH0 = 64
DH1 = D // H
EPS = 1e-5
BIG = 1e30

KPQ = -(-SK // SQ)
LASTQ = SK - (KPQ - 1) * SQ
QG = 8
NG = SQ // QG
GK = QG * KPQ
CK = GK // 2
UNITS = ((0, 2), (2, 2), (4, 2), (6, 1))
NU = len(UNITS)
SLOTS = 2

KT = 12
SKP = KT * P
HG = 4
GH = H // HG
GROWS = GH * DH1
MASK_ROW = 3 * GROWS
MAX_ROW = MASK_ROW + 1
QCOLS = GH * SQ
PAIRS = H // 2
PQ = 2 * SQ
KC = 3
VH = DH1 + 1
VW = 168
PG = 6
SCALE1 = float(DH1) ** -0.5

E0, E1 = 8, 12
TOPK1 = 3
PADDR = 64


def raw(ap):
    return ap.bitcast(F32)


def build(nc, a, out):
    ctx = ExitStack()
    with ctx:
        def sem(name):
            return ctx.enter_context(nc.semaphore(name))

        def sb(name, shape, dt=F32, scope=ctx):
            return scope.enter_context(nc.sbuf_tensor(name, shape, dt))

        bank = [ctx.enter_context(nc.psum_tensor(f"bank{i}", [P, 512], F32)) for i in range(4)]
        wide = [ctx.enter_context(nc.psum_tensor(f"wide{i}", [P, 2, 512], F32)) for i in range(2)]
        PS = [bank[0][:, :], bank[1][:, :], bank[2][:, :], bank[3][:, :],
              wide[0][:, 0, :], wide[0][:, 1, :], wide[1][:, 0, :], wide[1][:, 1, :]]

        x = sb("x", [P, NT, D])
        xn = sb("xn", [P, NT, D])
        xT = sb("xT", [P, TOK])
        ident = sb("ident", [P, P])
        gates = sb("gates", [P, 4])
        tg = sb("tg", [P, 4])
        eps = sb("eps", [P, 1])
        ones_row = sb("ones_row", [1, P])
        stats = sb("stats", [P, NT, 6])
        mv = sb("mv", [P, NT, 2])
        sd = sb("sd", [P, NT])
        rstd = sb("rstd", [P, NT])
        ctxT = [sb(f"ctxT{s}", [P, SKP]) for s in range(SLOTS)]
        rows = sb("rows", [1, 2 * D + E0])
        wq1 = sb("wq1", [P, D])
        wk1 = sb("wk1", [P, D])
        wv1 = sb("wv1", [P, D])
        wo1 = sb("wo1", [P, D])
        spread = sb("spread", [H, P])
        bcol = sb("bcol", [P, 3])
        mask8 = sb("mask8", [B, SK], U8)
        qstack = sb("qstack", [P, B, HG, GH, SQ], F32R)
        order_0 = sb("order_0", [P, NT, E0])
        order_1 = sb("order_1", [P, NT * 3, E1])

        one = ExitStack()
        qk = sb("qk", [P, TOK * H], scope=one)
        G = sb("G", [P, H, D], scope=one)
        M = sb("M", [P, H, D], scope=one)
        pick_f = sb("pick_f", [QG, P], scope=one)
        pick = sb("pick", [QG, P], BF16, scope=one)
        block_f = sb("block_f", [QG, 3, GK], scope=one)
        blockm = sb("blockm", [QG, 3, GK], BF16, scope=one)
        w1 = sb("w1", [P, E0, D], scope=one)
        w2 = sb("w2", [P, E0, D], scope=one)
        w3 = sb("w3", [P, E0, D], scope=one)
        gwT = sb("gwT", [P, E0], scope=one)
        b12 = sb("b12", [P, 2, E0], scope=one)
        b3 = sb("b3", [E0, D], scope=one)
        attn = ExitStack()
        ctxn = [sb(f"ctxn{s}", [CK, 2 * NG, D], scope=attn) for s in range(SLOTS)]
        qslot = [sb(f"qslot{s}", [P, SQ * H], scope=attn) for s in range(SLOTS)]
        p0 = [sb(f"p0_{s}", [P, 2, GK], scope=attn) for s in range(SLOTS)]
        p0T = [sb(f"p0T_{s}", [CK, 2, 2, P], scope=attn) for s in range(SLOTS)]
        nmax0 = sb("nmax0", [P, SLOTS, 2], scope=attn)
        psum0 = sb("psum0", [P, SLOTS, 2], scope=attn)
        rsum0 = sb("rsum0", [P, SLOTS, 2], scope=attn)
        attn.close()
        moe = ExitStack()
        h1 = [sb(f"h1_{s}", [P, 512], scope=moe) for s in range(2)]
        h2 = [sb(f"h2_{s}", [P, 512], scope=moe) for s in range(2)]
        acc0 = sb("acc0", [P, NT, D], scope=moe)
        probs = sb("probs", [P, NT, E0], scope=moe)
        left = sb("left", [P, NT, E0], scope=moe)
        pick0 = sb("pick0", [P, NT, E0], scope=moe)
        cw = sb("cw", [P, NT, E0], scope=moe)
        top0 = sb("top0", [P, NT], scope=moe)
        cwT = sb("cwT", [E0, TOK], scope=moe)
        moe.close()
        one.close()
        early = ExitStack()
        wq0 = sb("wq0", [DH0, H, D], scope=early)
        wk0 = sb("wk0", [DH0, H, D], scope=early)
        wv0 = sb("wv0", [DH0, H, D], scope=early)
        wo0 = sb("wo0", [DH0, H, D], scope=early)
        early.close()

        two = ExitStack()
        kstack = [sb(f"kstack{s}", [P, HG, SKP], F32R, scope=two) for s in range(SLOTS)]
        qs = [sb(f"qs{s}", [P, HG, GH, SQ], F32R, scope=two) for s in range(SLOTS)]
        maskr = sb("maskr", [B, SKP], F32R, scope=two)
        k1 = sb("k1", [P, SKP], F32R, scope=two)
        k2 = sb("k2", [P, SKP], F32R, scope=two)
        V = [sb(f"V{s}", [P, KT, VW], scope=two) for s in range(SLOTS)]
        p1 = [sb(f"p1_{s}", [P, 2, 2 * QCOLS], scope=two) for s in range(3)]
        mx3 = sb("mx3", [PQ, PAIRS, KC], scope=two)
        negm = sb("negm", [P, 32], scope=two)
        negmT = sb("negmT", [P, 32], scope=two)
        three = ExitStack()
        q1 = sb("q1", [P, TOK], F32R, scope=three)
        q2 = sb("q2", [P, TOK], F32R, scope=three)
        three.close()
        pv = sb("pv", [P, B, 336], scope=two)
        two.close()

        four = ExitStack()
        f1 = sb("f1", [P, E1, D], scope=four)
        f2 = sb("f2", [P, E1, D], scope=four)
        pwT = sb("pwT", [P, PADDR], scope=four)
        uT = sb("uT", [PADDR, 3 * E1], scope=four)
        fb2 = sb("fb2", [E1, D], scope=four)
        oT = sb("oT", [P, TOK], scope=four)
        den = sb("den", [H, TOK], scope=four)
        rden = sb("rden", [H, TOK], scope=four)
        xaT = sb("xaT", [PADDR, TOK], scope=four)
        z = sb("z", [P, NT * 3, E1], scope=four)
        zl = sb("zl", [P, NT * 3, E1], scope=four)
        ez = sb("ez", [P, NT * 3, E1], scope=four)
        sel = sb("sel", [P, NT * 3, E1], scope=four)
        pk = sb("pk", [P, NT * 3, E1], scope=four)
        C = sb("C", [P, NT * 3, E1], scope=four)
        top1 = sb("top1", [P, NT * 3], scope=four)
        top2 = sb("top2", [P, NT * 3], scope=four)
        c3T = sb("c3T", [E1, TOK], scope=four)
        y1 = sb("y1", [P, NT, D], scope=four)
        hg = sb("hg", [P, NT, D], scope=four)
        hT = sb("hT", [P, TOK], scope=four)
        y2 = sb("y2", [P, NT, D], scope=four)
        four.close()

        x_loaded = sem("x_loaded")
        w0_loaded = sem("w0_loaded")
        small_loaded = sem("small_loaded")
        ffn0_loaded = sem("ffn0_loaded")
        ffn1_loaded = sem("ffn1_loaded")
        ctxT_loaded = [sem(f"ctxT_loaded{s}") for s in range(SLOTS)]
        ctxn_loaded = [sem(f"ctxn_loaded{s}") for s in range(SLOTS)]
        v_step = sem("v_step")
        a_step = sem("a_step")
        pool_done = sem("pool_done")
        const_done = sem("const_done")
        var_done = sem("var_done")
        sd_done = sem("sd_done")
        xn_done = sem("xn_done")
        xnT_done = sem("xnT_done")
        xT_done = sem("xT_done")
        g_done, g_kept = sem("g_done"), sem("g_kept")
        m_done, m_kept = sem("m_done"), sem("m_kept")
        qk_done = sem("qk_done")
        qk_kept = [sem("qk_kept_first_half"), sem("qk_kept_second_half")]
        qslot_done = sem("qslot_done")
        s0_done, max0_done, exp0_done, norm0_done = sem("s0_done"), sem("max0_done"), sem("exp0_done"), sem("norm0_done")
        recip0_done, order_done = sem("recip0_done"), sem("order_done")
        p0T_done, p0T_kept = sem("p0T_done"), sem("p0T_kept")
        ac_done, ac_kept = sem("ac_done"), sem("ac_kept")
        o_done = sem("o_done")
        x_new = sem("x_new")
        gate_done, gate_sub, gate_exp = sem("gate_done"), sem("gate_sub"), sem("gate_exp")
        cw_done, cwT_done, cwT_kept = sem("cw_done"), sem("cwT_done"), sem("cwT_kept")
        b3_done, b3_kept = sem("b3_done"), sem("b3_kept")
        l1_done, l1_kept = sem("l1_done"), sem("l1_kept")
        l2_done, l2_kept = sem("l2_done"), sem("l2_kept")
        l3_done, l3_kept = sem("l3_done"), sem("l3_kept")
        q_done, q1_kept, q2_kept = sem("q_done"), sem("q1_kept"), sem("q2_kept")
        qstack_done = sem("qstack_done")
        maskr_done, mask_stored = sem("maskr_done"), sem("mask_stored")
        k_done, k1_kept, k2_kept = sem("k_done"), sem("k1_kept"), sem("k2_kept")
        v_done, v_kept = sem("v_done"), sem("v_kept")
        kst_loaded = [[sem(f"kst_loaded{s}_{c}") for c in range(KC)] for s in range(SLOTS)]
        qs_loaded = [sem(f"qs_loaded{s}") for s in range(SLOTS)]
        m1_done, m1_kept = sem("m1_done"), sem("m1_kept")
        negm_done, negmT_done = sem("negm_done"), sem("negmT_done")
        c_loaded = [sem(f"c_loaded{s}") for s in range(SLOTS)]
        st_done, exp1_done = sem("st_done"), sem("exp1_done")
        pv_done, pv_bank_free = sem("pv_done"), sem("pv_bank_free")
        oT_loaded, oT_done = sem("oT_loaded"), sem("oT_done")
        rden_done, spread_done = sem("rden_done"), sem("spread_done")
        xa_done, xa_kept = sem("xa_done"), sem("xa_kept")
        z_done, zsub_done, ez_done = sem("z_done"), sem("zsub_done"), sem("ez_done")
        C_done, c3T_done, c3T_kept = sem("C_done"), sem("c3T_done"), sem("c3T_kept")
        fb_done, fb_kept = sem("fb_done"), sem("fb_kept")
        mix_done, mix_kept = sem("mix_done"), sem("mix_kept")
        hg_done, hT_done, hT_kept = sem("hg_done"), sem("hT_done"), sem("hT_kept")
        out_done = sem("out_done")

        NUNITS = B * NU
        NTILES = B * KT
        NM = PAIRS * KC
        KDMA = 13

        mask_rows = nc.dram_tensor("mask_rows", (B, SKP), F32).ap()

        block = ctx.enter_context(nc.Block())

        @block.sync
        def _(sp):
            sp.dma_start(x[:, :, :], a["x"]).then_inc(x_loaded, 16)
            sp.dma_start(ident[:, :], a["ident"]).then_inc(x_loaded, 16)
            for name, t in (("wq0", wq0), ("wk0", wk0), ("wv0", wv0), ("wo0", wo0)):
                sp.dma_start(t[:, :, :], a[name]).then_inc(w0_loaded, 16)
            for s in range(SLOTS):
                sp.dma_start(ctxT[s][:, :], a["ctxT"][s]).then_inc(ctxT_loaded[s], 16)
                sp.dma_start(ctxn[s][:, :, :], a["ctxn"][s]).then_inc(ctxn_loaded[s], 16)
            for name, t in (("pick", pick_f[:, :]), ("block", block_f[:, :, :]), ("rows", rows[:, :]),
                            ("gates", gates[:, :]), ("wq1", wq1[:, :]), ("wk1", wk1[:, :]), ("wv1", wv1[:, :]),
                            ("wo1", wo1[:, :]), ("bcol", bcol[:, :]), ("spread", spread[:, :]), ("mask", mask8[:, :])):
                sp.dma_start(t, a[name]).then_inc(small_loaded, 16)
            for name, t in (("w1", w1[:, :, :]), ("w2", w2[:, :, :]), ("w3", w3[:, :, :]), ("gwT", gwT[:, :]),
                            ("b12", b12[:, :, :]), ("b3", b3[:, :])):
                sp.dma_start(t, a[name]).then_inc(ffn0_loaded, 16)

            with sp.Fori(0, B // SLOTS - 1) as i:
                for s in range(SLOTS):
                    b = i * SLOTS + s
                    sp.wait_ge(s0_done, (b + 1) * NU)
                    sp.dma_start(ctxT[s][:, :], a["ctxT"][bass.ds(b + SLOTS, 1)].rearrange("o p n -> (o p) n")).then_inc(ctxT_loaded[s], 16)
                    sp.wait_ge(ac_done, (b + 1) * NU)
                    sp.dma_start(ctxn[s][:, :, :], a["ctxn"][bass.ds(b + SLOTS, 1)].rearrange("o p c d -> (o p) c d")).then_inc(ctxn_loaded[s], 16)
            for s in range(SLOTS):
                sp.wait_ge(s0_done, (B - SLOTS + s + 1) * NU)
                sp.dma_start(ctxT[s][:, :], a["ctxT"][s]).then_inc(ctxT_loaded[s], 16)

            sp.wait_ge(pool_done, 2)
            sp.wait_ge(q1_kept, 2)
            sp.wait_ge(q2_kept, 2)
            for part, src in enumerate((q1, q2, q1)):
                for g in range(HG):
                    for hh in range(GH):
                        row = part * GROWS + hh * DH1
                        frm = g * GROWS + hh * DH1
                        sp.dma_start(raw(qstack[row:row + DH1, :, g, hh, :]),
                                     raw(src[frm:frm + DH1, :].rearrange("p (b q) -> p b q", b=B))).then_inc(qstack_done, 16)
            sp.wait_ge(qstack_done, 16 * 3 * HG * GH)
            sp.wait_ge(maskr_done, 1)
            sp.dma_start(mask_rows, raw(maskr[:, :])).then_inc(mask_stored, 16)
            sp.wait_ge(mask_stored, 16)
            sp.wait_ge(const_done, 4)

            def load_queries(b, s):
                sp.dma_start(raw(qs[s][:, :, :, :]), raw(qstack[:, bass.ds(b, 1), :, :, :]).rearrange("p o g h q -> p (o g) h q")).then_inc(qs_loaded[s], 16)

            def stack_keys(b, s, c):
                cols = slice(c * 512, (c + 1) * 512)
                sp.dma_start(raw(kstack[s][MASK_ROW:MASK_ROW + 1, :, cols]),
                             mask_rows[bass.ds(b, 1), cols].unsqueeze(1).to_broadcast([1, HG, 512])).then_inc(kst_loaded[s][c], 16)
                sp.wait_ge(k2_kept, b * KC + c + 1)
                for part, src in enumerate((k1, k1, k2)):
                    for g in range(HG):
                        sp.dma_start(raw(kstack[s][part * GROWS:(part + 1) * GROWS, g, cols]),
                                     raw(src[g * GROWS:(g + 1) * GROWS, cols])).then_inc(kst_loaded[s][c], 16)

            def load_max(b, s):
                sp.wait_ge(negmT_done, b + 1)
                for r in range(4):
                    n = min(32, PQ - 32 * r)
                    dst = qs[s][MAX_ROW:MAX_ROW + 1, :, :, :].rearrange("o g (k h) q -> o (g k) (h q)", k=2)
                    sp.dma_start(raw(dst[:, :, 32 * r:32 * r + n]), negmT[32 * r:32 * r + PAIRS, 0:n]).then_inc(c_loaded[s], 16)

            for s in range(SLOTS):
                load_queries(s, s)
                for c in range(KC):
                    stack_keys(s, s, c)
            load_max(0, 0)

            def sample(b, s, last):
                if not last:
                    sp.wait_ge(v_done, (b + 1) * KC)
                    sp.dma_start(ctxT[s][:, :], a["ctxT"][bass.ds(b + SLOTS, 1)].rearrange("o p n -> (o p) n")).then_inc(ctxT_loaded[s], 16)
                for c in range(KC):
                    if c == KC - 1 and not (last and s == 1):
                        load_max(b + 1, 1 - s)
                    if not last:
                        sp.wait_ge(st_done, b * KT + 4 * (c + 1))
                        stack_keys(b + SLOTS, s, c)
                if not last:
                    load_queries(b + SLOTS, s)

            with sp.Fori(0, B // SLOTS - 1) as i:
                for s in range(SLOTS):
                    sample(i * SLOTS + s, s, False)
            for s in range(SLOTS):
                sample(B - SLOTS + s, s, True)

            sp.wait_ge(st_done, NTILES - KT)
            for name, t in (("f1", f1[:, :, :]), ("f2", f2[:, :, :]), ("pwT", pwT[:, :]), ("uT", uT[:, :]), ("fb2", fb2[:, :])):
                sp.dma_start(t, a[name]).then_inc(ffn1_loaded, 16)
            sp.wait_ge(pv_bank_free, B + 1)
            for h in range(H):
                g, hh = h // 3, h % 3
                row = 32 * (g % 4) + hh * VH
                col = 168 * (g // 4) + hh * SQ
                dst = oT[h * DH1:(h + 1) * DH1, :].rearrange("p (b q) -> p b q", b=B)
                ddn = den[h:h + 1, :].rearrange("p (b q) -> p b q", b=B)
                sp.dma_start(dst, pv[row:row + DH1, :, col:col + SQ]).then_inc(oT_loaded, 16)
                sp.dma_start(ddn, pv[row + DH1:row + VH, :, col:col + SQ]).then_inc(oT_loaded, 16)

            for n, (t0, nt) in enumerate(HALVES):
                sp.wait_ge(x_new, 3 * 2 + n + 1)
                sp.dma_start(out[:, t0:t0 + nt, :], x[:, t0:t0 + nt, :]).then_inc(out_done, 16)
            sp.wait_ge(out_done, 32)

        @block.gpsimd
        def _(pool):
            nc.gpsimd.memset(qstack[:, :, :, :, :].bitcast(F32), 0.0).then_inc(pool_done, 1)
            pool.wait_ge(pool_done, 1)
            nc.gpsimd.memset(qstack[MASK_ROW:MASK_ROW + 1, :, :, :, :].bitcast(F32), 1.0).then_inc(pool_done, 1)

            pool.wait_ge(pool_done, 2)
            nc.gpsimd.iota(order_0[:, :, :], [[0, NT], [-1, E0]], base=E0, channel_multiplier=0,
                           allow_small_or_imprecise_dtypes=True).then_inc(order_done, 1)
            nc.gpsimd.iota(order_1[:, :, :], [[0, NT * 3], [-1, E1]], base=E1, channel_multiplier=0,
                           allow_small_or_imprecise_dtypes=True).then_inc(order_done, 1)

            pool.wait_ge(qk_kept[0], H)
            pool.wait_ge(qk_kept[1], H)
            for s in range(SLOTS):
                nc.gpsimd.tensor_copy(qslot[s][:, :], qk[:, s * SQ * H:(s + 1) * SQ * H]).then_inc(qslot_done, 1)
            with pool.Fori(0, B // SLOTS - 1) as i:
                for s in range(SLOTS):
                    b = i * SLOTS + s
                    pool.wait_ge(s0_done, (b + 1) * NU)
                    nc.gpsimd.tensor_copy(qslot[s][:, :], qk[:, bass.ds((b + SLOTS) * (SQ * H), SQ * H)]).then_inc(qslot_done, 1)

        @block.tensor
        def _(pe):
            def transpose_x(n):
                pe.wait_ge(xn_done, n + 1)
                for j, (t0, nt) in enumerate(HALVES):
                    for t in range(nt):
                        mm = pe.transpose(PS[4 + j][:, t * P:(t + 1) * P], xn[:, t0 + t, :], ident[:, :])
                    mm.then_inc(xnT_done, 1)

            def add_row(psum, row, n, stop=True):
                return pe.matmul(psum, ones_row[:, :], row, start=False, stop=stop)

            pe.wait_ge(w0_loaded, 64)
            for j in range(4):
                if j >= 2:
                    pe.wait_ge(g_kept, j - 1)
                for h in range(4):
                    mm = pe.matmul(PS[j % 2][:, h * D:(h + 1) * D], wq0[:, 4 * j + h, :], wk0[:, 4 * j + h, :], start=True, stop=True)
                mm.then_inc(g_done, 1)
            for j in range(4):
                if j >= 2:
                    pe.wait_ge(m_kept, j - 1)
                for h in range(4):
                    mm = pe.matmul(PS[2 + j % 2][:, h * D:(h + 1) * D], wv0[:, 4 * j + h, :], wo0[:, 4 * j + h, :], start=True, stop=True)
                mm.then_inc(m_done, 1)
            pe.wait_ge(x_loaded, 32)
            transpose_x(0)
            pe.wait_ge(g_kept, 4)
            pe.wait_ge(m_kept, 4)
            pe.wait_ge(xT_done, 2)
            for n in range(2 * H):
                h, half = divmod(n, 2)
                if n >= 4:
                    pe.wait_ge(qk_kept[half], h - 1)
                pe.matmul(PS[n % 4][:, 0:448], G[:, h, :], xT[:, half * 448:(half + 1) * 448], start=True, stop=True).then_inc(qk_done, 1)

            def scores0(n, u, s):
                first, cnt = UNITS[u]
                for g in range(cnt):
                    grp = first + g
                    i0 = grp * QG
                    kind = 0 if i0 + QG <= LASTQ else (1 if i0 < LASTQ else 2)
                    dst = PS[n % 2][:, g * 256:g * 256 + GK]
                    keys = ctxT[s][:, 0:KPQ * SQ].rearrange("p (t i) -> p i t", i=SQ)[:, i0:i0 + QG, :]
                    pe.matmul(dst, qslot[s][:, i0 * H:(i0 + QG) * H], keys, start=True, stop=False)
                    mm = pe.matmul(dst, pick[:, :], blockm[:, kind, :], start=False, stop=True)
                mm.then_inc(s0_done, 1)

            def transposes0(u, par):
                first, cnt = UNITS[u]
                for g in range(cnt):
                    for c in range(2):
                        mm = pe.transpose(PS[2 + par][0:CK, (2 * g + c) * P:(2 * g + c + 1) * P],
                                          p0[par][:, g, c * CK:(c + 1) * CK], ident[:, :])
                mm.then_inc(p0T_done, 1)

            def values0(u, par, s):
                first, cnt = UNITS[u]
                for g in range(cnt):
                    for c in range(2):
                        mm = pe.matmul(PS[4 + 2 * par][:, g * P:(g + 1) * P], ctxn[s][:, 2 * (first + g) + c, :],
                                       p0T[par][:, g, c, :], start=(c == 0), stop=(c == 1))
                mm.then_inc(ac_done, 1)

            def body0(i, last):
                for k in range(SLOTS * NU):
                    n = i * (SLOTS * NU) + k
                    k2_, k1_ = k + 2, k + 1
                    if not (last and k2_ >= SLOTS * NU):
                        s2, u2 = (k2_ // NU) % SLOTS, k2_ % NU
                        if u2 == 0:
                            nxt = i + k2_ // (SLOTS * NU)
                            pe.wait_ge(ctxT_loaded[s2], 16 * (nxt + 1))
                            pe.wait_ge(qslot_done, nxt * SLOTS + s2 + 1)
                        pe.wait_ge(exp0_done, n + 1)
                        scores0(k2_, u2, s2)
                    if not (last and k1_ >= SLOTS * NU):
                        pe.wait_ge(norm0_done, n + 2)
                        transposes0(k1_ % NU, k1_ % 2)
                    s0, u0 = k // NU, k % NU
                    if u0 == 0:
                        pe.wait_ge(ctxn_loaded[s0], 16 * (i + 1))
                    pe.wait_ge(p0T_kept, n + 1)
                    if k >= 1:
                        pe.wait_ge(ac_kept, n - 1)
                    values0(u0, k % 2, s0)

            pe.wait_ge(const_done, 1)
            pe.wait_ge(qk_kept[0], H)
            pe.wait_ge(qk_kept[1], H)
            pe.wait_ge(ctxT_loaded[0], 16)
            pe.wait_ge(qslot_done, 1)
            scores0(0, 0, 0)
            scores0(1, 1, 0)
            pe.wait_ge(norm0_done, 1)
            transposes0(0, 0)
            with pe.Fori(0, B // SLOTS - 1) as i:
                body0(i, False)
            body0(B // SLOTS - 1, True)

            def project_out(n, weight_of, lhs_of, count, row):
                for j, (t0, nt) in enumerate(HALVES):
                    for t in range(nt):
                        dst = PS[j][:, t * P:(t + 1) * P]
                        for h in range(count):
                            pe.matmul(dst, lhs_of(t0 + t, h), weight_of(h), start=(h == 0), stop=False)
                        mm = add_row(dst, row, D)
                    mm.then_inc(o_done, 1)

            pe.wait_ge(ac_kept, NUNITS)
            qk_v = qk[:, :].rearrange("p (t h) -> p h t", h=H)
            project_out(0, lambda h: M[:, h, :], lambda t, h: qk_v[:, h, t * P:(t + 1) * P], H, rows[:, 0:D])

            transpose_x(1)
            pe.wait_ge(xT_done, 4)
            pe.wait_ge(ffn0_loaded, 96)
            for t in range(NT):
                pe.matmul(PS[6][:, t * E0:(t + 1) * E0], xT[:, t * P:(t + 1) * P], gwT[:, :], start=True, stop=False)
                mm = add_row(PS[6][:, t * E0:(t + 1) * E0], rows[:, 2 * D:2 * D + E0], E0)
            mm.then_inc(gate_done, 1)

            def width(s):
                return HALVES[s % 2][0] * P, HALVES[s % 2][1] * P

            def layer1(s):
                t0, w = width(s)
                if s >= 2:
                    pe.wait_ge(l1_kept, s - 1)
                pe.matmul(PS[s % 2][:, 0:w], w1[:, s // 2, :], xT[:, t0:t0 + w], start=True, stop=True).then_inc(l1_done, 1)

            def layer2(s):
                t0, w = width(s)
                pe.wait_ge(l1_kept, s + 1)
                if s >= 2:
                    pe.wait_ge(l2_kept, s - 1)
                pe.matmul(PS[2 + s % 2][:, 0:w], w2[:, s // 2, :], h1[s % 2][:, 0:w], start=True, stop=True).then_inc(l2_done, 1)

            def layer3(s):
                t0, w = width(s)
                pe.wait_ge(l2_kept, s + 1)
                if s >= 2:
                    pe.wait_ge(l3_kept, s - 1)
                for t in range(w // P):
                    mm = pe.matmul(PS[4 + s % 2][:, t * P:(t + 1) * P], h2[s % 2][:, t * P:(t + 1) * P], w3[:, s // 2, :], start=True, stop=True)
                mm.then_inc(l3_done, 1)

            NS = 2 * E0
            pe.wait_ge(x_new, 2)
            layer1(0)
            layer1(1)
            layer2(0)
            pe.wait_ge(cw_done, 1)
            for j, (t0, nt) in enumerate(HALVES):
                for t in range(nt):
                    mm = pe.transpose(PS[6 + j][0:E0, t * P:(t + 1) * P], cw[:, t0 + t, :], ident[:, :])
                mm.then_inc(cwT_done, 1)
            pe.wait_ge(cwT_kept, 2)
            for j, (t0, nt) in enumerate(HALVES):
                for t in range(nt):
                    mm = pe.matmul(PS[6 + j][:, t * P:(t + 1) * P], cwT[:, (t0 + t) * P:(t0 + t + 1) * P], b3[:, :], start=True, stop=True)
                mm.then_inc(b3_done, 1)
            for s in range(NS):
                if s + 2 < NS:
                    layer1(s + 2)
                if s + 1 < NS:
                    layer2(s + 1)
                layer3(s)

            transpose_x(2)
            pe.wait_ge(xT_done, 6)
            for j in range(2):
                pe.matmul(PS[j][:, 0:448], wq1[:, :], xT[:, j * 448:(j + 1) * 448], start=True, stop=True).then_inc(q_done, 1)

            KV, MB, PVB = PS[0], (PS[1], PS[2]), PS[3]

            def keys(b, s, c):
                if c == 0:
                    pe.wait_ge(v_kept, b * KC)
                else:
                    pe.wait_ge(k2_kept, b * KC + c)
                pe.matmul(KV, wk1[:, :], ctxT[s][:, c * 512:(c + 1) * 512], start=True, stop=True).then_inc(k_done, 1)

            def values(b, s, c):
                if c == 0:
                    pe.wait_ge(k2_kept, (b + 1) * KC)
                else:
                    pe.wait_ge(v_kept, b * KC + c)
                for t in range(4):
                    mm = pe.matmul(KV[:, t * P:(t + 1) * P], ctxT[s][:, (4 * c + t) * P:(4 * c + t + 1) * P], wv1[:, :], start=True, stop=True)
                mm.then_inc(v_done, 1)

            def maximum(b, s, n, m):
                c, pair = divmod(m, PAIRS)
                if pair == 0:
                    pe.wait_ge(kst_loaded[s][c], 16 * KDMA * (n + 1))
                if not (type(b) is int and b == 0 and m < 2):
                    pe.wait_ge(m1_kept, b * NM + (m - 1))
                q = qs[s][0:MAX_ROW, pair // 2, 2 * (pair % 2):2 * (pair % 2) + 2, :]
                pe.matmul(MB[m % 2][0:PQ, :], q, kstack[s][0:MAX_ROW, pair // 2, c * 512:(c + 1) * 512],
                          start=True, stop=True).then_inc(m1_done, 1)

            def scores1(s, t):
                for g in range(HG):
                    mm = pe.matmul(wide[t % 2][:, g // 2, (g % 2) * QCOLS:(g % 2 + 1) * QCOLS],
                                   kstack[s][:, g, t * P:(t + 1) * P], qs[s][:, g, :, :], start=True, stop=True)
                mm.then_inc(st_done, 1)

            def values1(s, t):
                for g in range(PG):
                    heads = 3 if g < 5 else 1
                    pcols = p1[t % 3][:, :, :].rearrange("p a c -> p (a c)")[:, 3 * g * SQ:(3 * g + heads) * SQ]
                    mm = pe.matmul(PVB[32 * (g % 4):32 * (g % 4) + 32, 168 * (g // 4):168 * (g // 4) + heads * SQ],
                                   V[s][:, t, 3 * VH * g:3 * VH * g + 32], pcols,
                                   start=(t == 0 and g < 4), stop=(t == KT - 1), skip_group_check=True)
                mm.then_inc(pv_done, 1)

            for s in range(SLOTS):
                pe.wait_ge(ctxT_loaded[s], 16 * (B // SLOTS + 1))
                if s == 0:
                    pe.wait_ge(q1_kept, 2)
                    pe.wait_ge(q2_kept, 2)
                for c in range(KC):
                    keys(s, s, c)
                for c in range(KC):
                    values(s, s, c)
            pe.wait_ge(qs_loaded[0], 16)
            for m in range(NM):
                maximum(0, 0, 0, m)
            pe.wait_ge(const_done, 4)
            pe.wait_ge(c_loaded[0], 64)
            scores1(0, 0)
            scores1(0, 1)

            def body1(i, last):
                for s in range(SLOTS):
                    b = i * SLOTS + s
                    for t in range(KT):
                        tile = b * KT + t
                        nb = b + 1
                        final = last and s == 1
                        pe.wait_ge(exp1_done, tile + 1)
                        if t + 2 < KT:
                            scores1(s, t + 2)
                        elif not final:
                            if t + 2 == KT:
                                pe.wait_ge(c_loaded[1 - s], 64 * (i + s + 1))
                            scores1(1 - s, t + 2 - KT)
                        if t == 0:
                            pe.wait_ge(v_kept, (b + 1) * KC)
                            pe.wait_ge(pv_bank_free, b + 1)
                        values1(s, t)
                        if not final and t < 8:
                            if t == 0:
                                pe.wait_ge(qs_loaded[1 - s], 16 * (i + s + 1))
                            for m in range(3 * t, 3 * t + 3):
                                maximum(nb, 1 - s, i + s, m)
                        if not last:
                            if t == 0:
                                pe.wait_ge(ctxT_loaded[s], 16 * (B // SLOTS + 2) + 16 * i)
                            if t in (1, 3, 5):
                                keys(b + SLOTS, s, (t - 1) // 2)
                            if t in (7, 9, 11):
                                values(b + SLOTS, s, (t - 7) // 2)

            with pe.Fori(0, B // SLOTS - 1) as i:
                body1(i, False)
            body1(B // SLOTS - 1, True)

            pe.wait_ge(rden_done, 1)
            for j in range(2):
                pe.matmul(PS[2 + j][:, 0:448], spread[:, :], rden[:, j * 448:(j + 1) * 448], start=True, stop=True).then_inc(spread_done, 1)
            pe.wait_ge(oT_done, 1)
            project_out(1, lambda h: wo1[:, :], lambda t, h: oT[:, t * P:(t + 1) * P], 1, rows[:, D:2 * D])

            transpose_x(3)
            pe.wait_ge(xT_done, 8)
            pe.wait_ge(ffn1_loaded, 80)
            for j in range(2):
                pe.matmul(PS[2 + j][0:PADDR, 0:448], pwT[:, :], xT[:, j * 448:(j + 1) * 448], start=True, stop=True).then_inc(xa_done, 1)
            pe.wait_ge(xa_kept, 2)
            for t in range(NT):
                mm = pe.matmul(PS[2][:, t * 3 * E1:(t + 1) * 3 * E1], xaT[:, t * P:(t + 1) * P], uT[:, :], start=True, stop=True)
            mm.then_inc(z_done, 1)

            def mixture(which, src, w):
                for n in range(NT * 3):
                    t, e4 = divmod(n, 3)
                    m = which * NT * 3 + n
                    if m >= 4:
                        pe.wait_ge(mix_kept, m - 3)
                    pe.matmul(PS[4 + m % 4][:, :], src[:, t * P:(t + 1) * P],
                              w[:, 4 * e4:4 * e4 + 4, :].rearrange("p e d -> p (e d)"), start=True, stop=True).then_inc(mix_done, 1)

            pe.wait_ge(x_new, 6)
            mixture(0, xT, f1)
            pe.wait_ge(C_done, 1)
            for j, (t0, nt) in enumerate(HALVES):
                for t in range(nt):
                    mm = pe.transpose(PS[j][0:E1, t * P:(t + 1) * P], C[:, 3 * (t0 + t) + 2, :], ident[:, :])
                mm.then_inc(c3T_done, 1)
            pe.wait_ge(c3T_kept, 2)
            for j, (t0, nt) in enumerate(HALVES):
                for t in range(nt):
                    mm = pe.matmul(PS[j][:, t * P:(t + 1) * P], c3T[:, (t0 + t) * P:(t0 + t + 1) * P], fb2[:, :], start=True, stop=True)
                mm.then_inc(fb_done, 1)
            pe.wait_ge(hg_done, 1)
            for j, (t0, nt) in enumerate(HALVES):
                for t in range(nt):
                    mm = pe.transpose(PS[2 + j][:, t * P:(t + 1) * P], hg[:, t0 + t, :], ident[:, :])
                mm.then_inc(hT_done, 1)
            pe.wait_ge(hT_kept, 2)
            mixture(1, hT, f2)

        @block.scalar
        def _(act):
            def norm_parts(n):
                act.wait_ge(var_done, n + 1)
                nc.scalar.activation(sd[:, :], mv[:, :, 1], ACT.Sqrt, bias=eps[:, 0:1]).then_inc(sd_done, 1)
                act.wait_ge(xnT_done, 2 * n + 2)
                nc.scalar.copy(xT[:, 512:TOK], PS[5][:, 0:TOK - 512]).then_inc(xT_done, 1)

            for j in range(4):
                act.wait_ge(g_done, j + 1)
                nc.scalar.mul(G[:, 4 * j:4 * j + 4, :].rearrange("p h d -> p (h d)"), PS[j % 2], DH0 ** -0.5).then_inc(g_kept, 1)
            norm_parts(0)
            act.wait_ge(small_loaded, 176)
            nc.scalar.activation(tg[:, :], gates[:, :], ACT.Tanh).then_inc(a_step, 1)
            qk_t = qk[:, :].rearrange("p (t h) -> p h t", h=H)
            for h in range(H):
                act.wait_ge(qk_done, 2 * h + 1)
                nc.scalar.copy(qk_t[:, h, 0:448], PS[2 * h % 4][:, 0:448]).then_inc(qk_kept[0], 1)

            def exp0(u, par, n):
                first, cnt = UNITS[u]
                act.wait_ge(max0_done, n + 1)
                for g in range(cnt):
                    ins = nc.scalar.activation(p0[par][:, g, :], PS[par][:, g * 256:g * 256 + GK], ACT.Exp,
                                               bias=nmax0[:, par, g:g + 1], accum_out=psum0[:, par, g:g + 1])
                ins.then_inc(exp0_done, 1)

            def body0(i, last):
                for k in range(SLOTS * NU):
                    n = i * (SLOTS * NU) + k
                    if not (last and k + 2 >= SLOTS * NU):
                        act.wait_ge(p0T_done, n + 1)
                        exp0((k + 2) % NU, k % 2, n + 2)
                    act.wait_ge(ac_done, n + 1)
                    first, cnt = UNITS[k % NU]
                    start = (i * SLOTS + k // NU) * (SQ * H) + first * P
                    nc.scalar.copy(qk[:, bass.ds(start, cnt * P)], PS[4 + 2 * (k % 2)][:, 0:cnt * P]).then_inc(ac_kept, 1)

            exp0(0, 0, 0)
            exp0(1, 1, 1)
            with act.Fori(0, B // SLOTS - 1) as i:
                body0(i, False)
            body0(B // SLOTS - 1, True)

            norm_parts(1)
            act.wait_ge(gate_sub, 1)
            nc.scalar.activation(left[:, :, :], probs[:, :, :], ACT.Exp).then_inc(gate_exp, 1)

            def relu1(s):
                w = HALVES[s % 2][1] * P
                act.wait_ge(l1_done, s + 1)
                if s >= 2:
                    act.wait_ge(l2_done, s - 1)
                nc.scalar.activation(h1[s % 2][:, 0:w], PS[s % 2][:, 0:w], ACT.Relu, bias=b12[:, 0, s // 2:s // 2 + 1]).then_inc(l1_kept, 1)

            def relu2(s):
                w = HALVES[s % 2][1] * P
                act.wait_ge(l2_done, s + 1)
                if s >= 2:
                    act.wait_ge(l3_done, s - 1)
                nc.scalar.activation(h2[s % 2][:, 0:w], PS[2 + s % 2][:, 0:w], ACT.Relu, bias=b12[:, 1, s // 2:s // 2 + 1]).then_inc(l2_kept, 1)

            NS = 2 * E0
            relu1(0)
            relu1(1)
            relu2(0)
            for s in range(NS):
                if s + 2 < NS:
                    relu1(s + 2)
                if s + 1 < NS:
                    relu2(s + 1)

            norm_parts(2)
            for j in range(2):
                act.wait_ge(q_done, j + 1)
                nc.scalar.activation(q1[:, j * 448:(j + 1) * 448], PS[j][:, 0:448], ACT.Identity, bias=bcol[:, 0:1]).then_inc(q1_kept, 1)

            def keep_k1(b, n, s, c):
                act.wait_ge(k_done, b * KC + c + 1)
                if not (type(b) is int and b == 0):
                    act.wait_ge(kst_loaded[1 - s][c], 16 * KDMA * (n + 1))
                nc.scalar.activation(k1[:, c * 512:(c + 1) * 512], PS[0], ACT.Identity, bias=bcol[:, 1:2]).then_inc(k1_kept, 1)

            for s in range(SLOTS):
                for c in range(KC):
                    keep_k1(s, 0, s, c)

            def body1(i, last):
                for s in range(SLOTS):
                    b = i * SLOTS + s
                    for t in range(KT):
                        act.wait_ge(st_done, b * KT + t + 1)
                        nc.scalar.activation(p1[t % 3][:, :, :], wide[t % 2][:, :, 0:2 * QCOLS], ACT.Exp, scale=SCALE1).then_inc(exp1_done, 1)
                        if not last and t in (1, 3, 5):
                            keep_k1(b + SLOTS, i + s, s, (t - 1) // 2)

            with act.Fori(0, B // SLOTS - 1) as i:
                body1(i, False)
            body1(B // SLOTS - 1, True)

            norm_parts(3)
            for j in range(2):
                act.wait_ge(xa_done, j + 1)
                nc.scalar.copy(xaT[:, j * 448:(j + 1) * 448], PS[2 + j][0:PADDR, 0:448]).then_inc(xa_kept, 1)
            act.wait_ge(zsub_done, 1)
            nc.scalar.activation(ez[:, :, :], zl[:, :, :], ACT.Exp).then_inc(ez_done, 1)
            for j, (t0, nt) in enumerate(HALVES):
                act.wait_ge(c3T_done, j + 1)
                nc.scalar.copy(c3T[:, t0 * P:(t0 + nt) * P], PS[j][0:E1, 0:nt * P]).then_inc(c3T_kept, 1)
            for j, (t0, nt) in enumerate(HALVES):
                act.wait_ge(fb_done, j + 1)
                nc.scalar.copy(y2[:, t0:t0 + nt, :].rearrange("p t d -> p (t d)"), PS[j][:, 0:nt * P]).then_inc(fb_kept, 1)
            act.wait_ge(mix_kept, NT * 3)
            nc.scalar.activation(hg[:, :, :], y1[:, :, :], ACT.Gelu).then_inc(hg_done, 1)
            for j, (t0, nt) in enumerate(HALVES):
                act.wait_ge(hT_done, j + 1)
                nc.scalar.copy(hT[:, t0 * P:(t0 + nt) * P], PS[2 + j][:, 0:nt * P]).then_inc(hT_kept, 1)

        @block.vector
        def _(dve):
            steps = [0]

            def link(ins):
                steps[0] += 1
                ins.then_inc(v_step, 1)
                dve.wait_ge(v_step, steps[0])

            def layernorm(n):
                for t in range(NT):
                    ins = nc.vector.bn_stats(stats[:, t, :], x[:, t, :])
                link(ins)
                for t in range(NT):
                    ins = nc.vector.bn_aggr(mv[:, t, :], stats[:, t, :])
                ins.then_inc(var_done, 1)
                dve.wait_ge(sd_done, n + 1)
                link(nc.vector.reciprocal(rstd[:, :], sd[:, :]))
                for t in range(NT):
                    ins = nc.vector.tensor_scalar(xn[:, t, :], x[:, t, :], mv[:, t, 0:1], rstd[:, t:t + 1], ALU.subtract, ALU.mult)
                ins.then_inc(xn_done, 1)

            def keep_xT(n):
                dve.wait_ge(xnT_done, 2 * n + 1)
                nc.vector.tensor_copy(xT[:, 0:512], PS[4]).then_inc(xT_done, 1)

            def bc(ap, n):
                return ap.unsqueeze(2).to_broadcast([P, ap.shape[1], n])

            link(nc.vector.memset(eps[:, :], EPS))
            nc.vector.memset(ones_row[:, :], 1.0)
            dve.wait_ge(x_loaded, 32)
            layernorm(0)
            for j in range(4):
                dve.wait_ge(m_done, j + 1)
                nc.vector.tensor_copy(M[:, 4 * j:4 * j + 4, :].rearrange("p h d -> p (h d)"), PS[2 + j % 2]).then_inc(m_kept, 1)
            keep_xT(0)
            dve.wait_ge(small_loaded, 176)
            nc.vector.tensor_copy(pick[:, :], pick_f[:, :])
            nc.vector.tensor_copy(blockm[:, :, :], block_f[:, :, :]).then_inc(const_done, 1)
            qk_t = qk[:, :].rearrange("p (t h) -> p h t", h=H)
            for h in range(H):
                dve.wait_ge(qk_done, 2 * h + 2)
                nc.vector.tensor_copy(qk_t[:, h, 448:TOK], PS[(2 * h + 1) % 4][:, 0:448]).then_inc(qk_kept[1], 1)

            def max0(u, par, n):
                cnt = UNITS[u][1]
                dve.wait_ge(s0_done, n + 1)
                nc.vector.tensor_reduce(nmax0[:, par, 0:cnt], PS[par].rearrange("p (g k) -> p g k", g=2)[:, 0:cnt, 0:GK],
                                        AX, ALU.max, negate=True).then_inc(max0_done, 1)

            def norm0(u, par, n):
                cnt = UNITS[u][1]
                dve.wait_ge(exp0_done, n + 1)
                nc.vector.reciprocal(rsum0[:, par, 0:cnt], psum0[:, par, 0:cnt]).then_inc(recip0_done, 1)
                dve.wait_ge(recip0_done, n + 1)
                for g in range(cnt):
                    ins = nc.vector.tensor_scalar(p0[par][:, g, :], p0[par][:, g, :], rsum0[:, par, g:g + 1], None, ALU.mult)
                ins.then_inc(norm0_done, 1)

            def keep_p0T(u, par, n):
                cnt = UNITS[u][1]
                dve.wait_ge(p0T_done, n + 1)
                nc.vector.tensor_copy(p0T[par][:, 0:cnt, :, :].rearrange("p g c q -> p (g c q)"),
                                      PS[2 + par][0:CK, 0:cnt * 256]).then_inc(p0T_kept, 1)

            def body0(i, last):
                for k in range(SLOTS * NU):
                    n = i * (SLOTS * NU) + k
                    if not (last and k + 1 >= SLOTS * NU):
                        norm0((k + 1) % NU, (k + 1) % 2, n + 1)
                    keep_p0T(k % NU, k % 2, n)
                    if not (last and k + 2 >= SLOTS * NU):
                        max0((k + 2) % NU, k % 2, n + 2)

            max0(0, 0, 0)
            max0(1, 1, 1)
            norm0(0, 0, 0)
            with dve.Fori(0, B // SLOTS - 1) as i:
                body0(i, False)
            body0(B // SLOTS - 1, True)

            def residual(src_of, n, gate):
                for j, (t0, nt) in enumerate(HALVES):
                    ins = nc.vector.scalar_tensor_tensor(out=x[:, t0:t0 + nt, :].rearrange("p t d -> p (t d)"),
                                                         in0=src_of(j, t0, nt), scalar=tg[:, gate:gate + 1],
                                                         in1=x[:, t0:t0 + nt, :].rearrange("p t d -> p (t d)"),
                                                         op0=ALU.mult, op1=ALU.add)
                    ins.then_inc(x_new, 1)
                dve.wait_ge(x_new, 2 * n + 2)

            dve.wait_ge(a_step, 1)
            dve.wait_ge(o_done, 2)
            residual(lambda j, t0, nt: PS[j][:, 0:nt * P], 0, 0)

            layernorm(1)
            keep_xT(1)
            dve.wait_ge(gate_done, 1)
            logits = PS[6][:, 0:NT * E0].rearrange("p (t e) -> p t e", e=E0)
            link(nc.vector.tensor_reduce(top0[:, :], logits, AX, ALU.max))
            nc.vector.tensor_tensor(probs[:, :, :], logits, bc(top0[:, :], E0), ALU.subtract).then_inc(gate_sub, 1)
            dve.wait_ge(gate_exp, 1)
            link(nc.vector.tensor_reduce(top0[:, :], left[:, :, :], AX, ALU.add))
            link(nc.vector.reciprocal(top0[:, :], top0[:, :]))
            link(nc.vector.tensor_tensor(probs[:, :, :], left[:, :, :], bc(top0[:, :], E0), ALU.mult))
            link(nc.vector.tensor_copy(left[:, :, :], probs[:, :, :]))

            def first_largest(vals, pick_, top, n, order):
                link(nc.vector.tensor_reduce(top, vals, AX, ALU.max))
                link(nc.vector.tensor_tensor(pick_, vals, bc(top, n), ALU.is_equal))
                link(nc.vector.tensor_tensor(pick_, pick_, order, ALU.mult))
                link(nc.vector.tensor_reduce(top, pick_, AX, ALU.max))
                link(nc.vector.tensor_tensor(pick_, pick_, bc(top, n), ALU.is_equal))

            dve.wait_ge(order_done, 2)
            order0 = order_0[:, :, :]
            first_largest(left[:, :, :], pick0[:, :, :], top0[:, :], E0, order0)
            link(nc.vector.tensor_tensor(cw[:, :, :], pick0[:, :, :], probs[:, :, 0:1].to_broadcast([P, NT, E0]), ALU.mult))
            link(nc.vector.scalar_tensor_tensor(out=left[:, :, :], in0=pick0[:, :, :], scalar=-2.0, in1=left[:, :, :], op0=ALU.mult, op1=ALU.add))
            first_largest(left[:, :, :], pick0[:, :, :], top0[:, :], E0, order0)
            link(nc.vector.tensor_tensor(pick0[:, :, :], pick0[:, :, :], probs[:, :, 1:2].to_broadcast([P, NT, E0]), ALU.mult))
            nc.vector.tensor_tensor(cw[:, :, :], cw[:, :, :], pick0[:, :, :], ALU.add).then_inc(cw_done, 1)
            for j, (t0, nt) in enumerate(HALVES):
                dve.wait_ge(cwT_done, j + 1)
                nc.vector.tensor_copy(cwT[:, t0 * P:(t0 + nt) * P], PS[6 + j][0:E0, 0:nt * P]).then_inc(cwT_kept, 1)
            for j, (t0, nt) in enumerate(HALVES):
                dve.wait_ge(b3_done, j + 1)
                link(nc.vector.tensor_copy(acc0[:, t0:t0 + nt, :].rearrange("p t d -> p (t d)"), PS[6 + j][:, 0:nt * P]))
            for s in range(2 * E0):
                t0, nt = HALVES[s % 2]
                dve.wait_ge(l3_done, s + 1)
                if s >= 2:
                    dve.wait_ge(l3_kept, s - 1)
                for t in range(nt):
                    ins = nc.vector.scalar_tensor_tensor(out=acc0[:, t0 + t, :], in0=PS[4 + s % 2][:, t * P:(t + 1) * P],
                                                         scalar=cw[:, t0 + t, s // 2:s // 2 + 1], in1=acc0[:, t0 + t, :],
                                                         op0=ALU.mult, op1=ALU.add)
                ins.then_inc(l3_kept, 1)
            dve.wait_ge(l3_kept, 2 * E0)
            residual(lambda j, t0, nt: acc0[:, t0:t0 + nt, :].rearrange("p t d -> p (t d)"), 1, 1)

            layernorm(2)
            nc.vector.memset(maskr[:, SK:SKP].bitcast(F32), -BIG)
            nc.vector.tensor_scalar(maskr[:, 0:SK], mask8[:, :], -BIG, None, ALU.mult).then_inc(maskr_done, 1)
            for s in range(SLOTS):
                link(nc.vector.memset(kstack[s][MASK_ROW:P, :, :].bitcast(F32), 0.0))
                nc.vector.memset(kstack[s][MASK_ROW:MASK_ROW + 2, :, :].bitcast(F32), 1.0).then_inc(const_done, 1)
                link(nc.vector.memset(V[s][:, :, :], 1.0))
            nc.vector.memset(negmT[:, :], 0.0).then_inc(pv_bank_free, 1)
            nc.vector.memset(negm[:, :], 0.0).then_inc(const_done, 1)
            keep_xT(2)
            for j in range(2):
                dve.wait_ge(q1_kept, j + 1)
                nc.vector.scalar_tensor_tensor(out=q2[:, j * 448:(j + 1) * 448], in0=PS[j][:, 0:448], scalar=bcol[:, 0:1],
                                               in1=q1[:, j * 448:(j + 1) * 448].bitcast(F32), op0=ALU.add, op1=ALU.subtract).then_inc(q2_kept, 1)

            def keep_k2(b, c):
                dve.wait_ge(k1_kept, b * KC + c + 1)
                cols = slice(c * 512, (c + 1) * 512)
                nc.vector.scalar_tensor_tensor(out=k2[:, cols], in0=PS[0], scalar=bcol[:, 1:2], in1=k1[:, cols].bitcast(F32),
                                               op0=ALU.add, op1=ALU.subtract).then_inc(k2_kept, 1)

            def keep_v(b, s, c):
                dve.wait_ge(v_done, b * KC + c + 1)
                nc.vector.tensor_copy(V[s][:, 4 * c:4 * c + 4, 0:H * VH].rearrange("p t (h e) -> p t h e", e=VH)[:, :, :, 0:DH1],
                                      PS[0].rearrange("p (t h e) -> p t h e", t=4, e=DH1)).then_inc(v_kept, 1)

            def keep_max(b, m):
                c, pair = divmod(m, PAIRS)
                dve.wait_ge(m1_done, b * NM + m + 1)
                nc.vector.tensor_reduce(mx3[:, pair, c:c + 1], (PS[1], PS[2])[m % 2][0:PQ, :], AX, ALU.max).then_inc(m1_kept, 1)

            def turn_max(b):
                dve.wait_ge(m1_kept, (b + 1) * NM)
                nc.vector.tensor_reduce(negm[0:PQ, 0:PAIRS].bitcast(F32R), mx3[:, :, :], AX, ALU.max, negate=True).then_inc(negm_done, 1)
                dve.wait_ge(negm_done, b + 1)
                nc.vector.transpose(negmT[:, :], negm[:, :]).then_inc(negmT_done, 1)

            def keep_pv(b):
                dve.wait_ge(pv_done, (b + 1) * KT)
                nc.vector.tensor_copy(pv[:, bass.ds(b, 1), 0:168], PS[3][:, 0:168].unsqueeze(1))
                nc.vector.tensor_copy(pv[0:32, bass.ds(b, 1), 168:336], PS[3][0:32, 168:336].unsqueeze(1))
                nc.vector.tensor_copy(pv[32:64, bass.ds(b, 1), 168:168 + SQ], PS[3][32:64, 168:168 + SQ].unsqueeze(1)).then_inc(pv_bank_free, 1)

            for s in range(SLOTS):
                for c in range(KC):
                    keep_k2(s, c)
                for c in range(KC):
                    keep_v(s, s, c)
            for m in range(NM):
                keep_max(0, m)
            turn_max(0)

            def body1(i, last):
                for s in range(SLOTS):
                    b = i * SLOTS + s
                    final = last and s == 1
                    for t in range(KT):
                        if not final and t < 8:
                            for m in range(3 * t, 3 * t + 3):
                                keep_max(b + 1, m)
                        if not final and t == 7:
                            turn_max(b + 1)
                        if not last:
                            if t in (1, 3, 5):
                                keep_k2(b + SLOTS, (t - 1) // 2)
                            if t in (9, 11):
                                keep_v(b + SLOTS, s, (t - 9) // 2)
                    keep_pv(b)
                    if not last:
                        keep_v(b + SLOTS, s, 2)

            with dve.Fori(0, B // SLOTS - 1) as i:
                body1(i, False)
            body1(B // SLOTS - 1, True)

            dve.wait_ge(oT_loaded, 16 * H * 2)
            nc.vector.reciprocal(rden[:, :], den[:, :]).then_inc(rden_done, 1)
            for j in range(2):
                dve.wait_ge(spread_done, j + 1)
                half = oT[:, j * 448:(j + 1) * 448]
                link(nc.vector.tensor_tensor(half, half, PS[2 + j][:, 0:448], ALU.mult))
            nc.vector.tensor_scalar(oT[:, :], oT[:, :], bcol[:, 2:3], None, ALU.add).then_inc(oT_done, 1)
            dve.wait_ge(o_done, 4)
            residual(lambda j, t0, nt: PS[j][:, 0:nt * P], 2, 2)

            layernorm(3)
            keep_xT(3)
            dve.wait_ge(z_done, 1)
            link(nc.vector.tensor_copy(z[:, :, :].rearrange("p a e -> p (a e)"), PS[2][:, 0:NT * 3 * E1]))
            link(nc.vector.tensor_reduce(top2[:, :], z[:, :, :], AX, ALU.max))
            nc.vector.tensor_tensor(zl[:, :, :], z[:, :, :], bc(top2[:, :], E1), ALU.subtract).then_inc(zsub_done, 1)
            for k in range(TOPK1):
                first_largest(z[:, :, :], pk[:, :, :], top1[:, :], E1, order_1[:, :, :])
                if k == 0:
                    link(nc.vector.tensor_copy(sel[:, :, :], pk[:, :, :]))
                else:
                    link(nc.vector.tensor_tensor(sel[:, :, :], sel[:, :, :], pk[:, :, :], ALU.add))
                if k < TOPK1 - 1:
                    link(nc.vector.scalar_tensor_tensor(out=z[:, :, :], in0=pk[:, :, :], scalar=-BIG, in1=z[:, :, :], op0=ALU.mult, op1=ALU.add))
            dve.wait_ge(ez_done, 1)
            link(nc.vector.tensor_tensor(C[:, :, :], ez[:, :, :], sel[:, :, :], ALU.mult))
            link(nc.vector.tensor_reduce(top1[:, :], C[:, :, :], AX, ALU.add))
            link(nc.vector.reciprocal(top1[:, :], top1[:, :]))
            nc.vector.tensor_tensor(C[:, :, :], C[:, :, :], bc(top1[:, :], E1), ALU.mult).then_inc(C_done, 1)
            dve.wait_ge(C_done, 1)

            def mix(which, dst):
                for n in range(NT * 3):
                    t, e4 = divmod(n, 3)
                    m = which * NT * 3 + n
                    dve.wait_ge(mix_done, m + 1)
                    for e in range(4):
                        first = which == 0 and e4 == 0 and e == 0
                        coef = C[:, 3 * t + which, 4 * e4 + e:4 * e4 + e + 1]
                        src = PS[4 + m % 4][:, e * D:(e + 1) * D]
                        if first:
                            ins = nc.vector.tensor_scalar(dst[:, t, :], src, coef, None, ALU.mult)
                        else:
                            ins = nc.vector.scalar_tensor_tensor(out=dst[:, t, :], in0=src, scalar=coef, in1=dst[:, t, :], op0=ALU.mult, op1=ALU.add)
                        if e < 3:
                            link(ins)
                    ins.then_inc(mix_kept, 1)
                    dve.wait_ge(mix_kept, m + 1)

            mix(0, y1)
            dve.wait_ge(fb_kept, 2)
            mix(1, y2)
            residual(lambda j, t0, nt: y2[:, t0:t0 + nt, :].rearrange("p t d -> p (t d)"), 3, 3)


def kernel(**inputs):
    import numpy as np
    import concourse.bacc as bacc
    from concourse.bass_utils import run_bass_kernel_spmd

    v = {k: np.asarray(t) for k, t in inputs.items()}
    ctx = v["ctx_1024"]
    ctxT = np.zeros((B, P, SKP), ctx.dtype)
    ctxT[:, :, :SK] = ctx.transpose(0, 2, 1)
    ctxn = np.zeros((B, KPQ * SQ, D), ctx.dtype)
    ctxn[:, :SK] = ctx
    ctxn = ctxn.reshape(B, KPQ, 2 * NG, 4, D).transpose(0, 3, 1, 2, 4).reshape(B, CK, 2 * NG, D)
    pick = np.zeros((QG, QG, H), np.float32)
    block = np.full((QG, 3, QG, KPQ), -BIG, np.float32)
    for i in range(QG):
        pick[i, i] = 1
        for kind, whole in enumerate((QG, LASTQ % QG, 0)):
            block[i, kind, i, :KPQ - (i >= whole)] = 0

    def heads(w, transposed):
        w = w.T if transposed else w
        return w.reshape(H, DH0, D).transpose(1, 0, 2)

    wkv0, wkv1 = v["L0_xattn_Wkv"], v["L1_xattn_Wkv"]
    inner = H * DH0
    arrays = {
        "x": v["x"].reshape(NT, P, D).transpose(1, 0, 2),
        "ident": np.eye(P, dtype=np.float32),
        "wq0": heads(v["L0_xattn_Wq"], True),
        "wk0": heads(wkv0[:, :inner], True),
        "wv0": heads(wkv0[:, inner:], True),
        "wo0": heads(v["L0_xattn_Wout"], False),
        "ctxT": ctxT,
        "ctxn": ctxn,
        "pick": pick.reshape(QG, P),
        "block": block.reshape(QG, 3, GK),
        "rows": np.concatenate([v["L0_xattn_bout"], v["L1_xattn_bout"], v["L0_ffn_gate_b"]])[None],
        "gates": np.broadcast_to(np.stack([v["g_xattn"][0], v["g_ffn"][0], v["g_xattn"][1], v["g_ffn"][1]])[None], (P, 4)),
        "wq1": v["L1_xattn_Wq"],
        "wk1": wkv1[:, :D],
        "wv1": wkv1[:, D:],
        "wo1": v["L1_xattn_Wout"],
        "bcol": np.stack([v["L1_xattn_bq"], v["L1_xattn_bkv"][:D], v["L1_xattn_bkv"][D:]], 1),
        "spread": np.repeat(np.eye(H, dtype=np.float32), DH1, axis=1),
        "mask": v["mask_BxS2_bf0"],
        "w1": v["L0_ffn_w1"].transpose(1, 0, 2),
        "w2": v["L0_ffn_w2"].transpose(1, 0, 2),
        "w3": v["L0_ffn_w3"].transpose(1, 0, 2),
        "gwT": v["L0_ffn_gate_w"].T,
        "b12": np.stack([v["L0_ffn_b1"].T, v["L0_ffn_b2"].T], 1),
        "b3": v["L0_ffn_b3"],
        "f1": v["L1_ffn_W1"].transpose(2, 0, 1),
        "f2": v["L1_ffn_W2"].transpose(2, 0, 1),
        "pwT": v["L1_ffn_P_w"].T,
        "uT": np.concatenate([v["L1_ffn_U1"], v["L1_ffn_U2"], v["L1_ffn_U3"]]).T,
        "fb2": v["L1_ffn_b2"],
    }
    arrays = {k: np.ascontiguousarray(t) for k, t in arrays.items()}
    nc = bacc.Bacc("TRN2", target_bir_lowering=False, num_devices=1)
    aps = {k: nc.dram_tensor(f"in_{k}", t.shape, mybir.dt.from_np(t.dtype), kind="ExternalInput").ap()
           for k, t in arrays.items()}
    out = nc.dram_tensor("out", (TOK, D), F32, kind="ExternalOutput").ap()
    build(nc, aps, out.rearrange("(n p) d -> p n d", p=P))
    got = run_bass_kernel_spmd(nc, [{f"in_{k}": t for k, t in arrays.items()}], core_ids=[0])
    return got.results[0]["out"].reshape(B, SQ, D)
```

```python
from contextlib import ExitStack

import concourse.bass as bass
from concourse import mybir

F32 = mybir.dt.float32
F32R = mybir.dt.float32r
BF16 = mybir.dt.bfloat16
U8 = mybir.dt.uint8
ALU = mybir.AluOpType
ACT = mybir.ActivationFunctionType
AX = mybir.AxisListType.X

P = 128
B, SQ, SK, D = 16, 56, 1500, 128
TOK = B * SQ
NT = TOK // P
HALVES = ((0, 4), (4, 3))
H = 16
DH0 = 64
DH1 = D // H
EPS = 1e-5
BIG = 1e30

KPQ = -(-SK // SQ)
LASTQ = SK - (KPQ - 1) * SQ
QG = 8
NG = SQ // QG
GK = QG * KPQ
CK = GK // 2
UNITS = ((0, 2), (2, 2), (4, 2), (6, 1))
NU = len(UNITS)
SLOTS = 2
AHEAD = 3

KT = 12
SKP = KT * P
HG = 4
GH = H // HG
GROWS = GH * DH1
MASK_ROW = 3 * GROWS
MAX_ROW = MASK_ROW + 1
QCOLS = GH * SQ
PAIRS = H // 2
PQ = 2 * SQ
KC = 3
VH = DH1 + 1
VW = 168
PG = 6
SCALE1 = float(DH1) ** -0.5

E0, E1 = 8, 12
TOPK1 = 3
PADDR = 64


def raw(ap):
    return ap.bitcast(F32)


def build(nc, a, out):
    ctx = ExitStack()
    with ctx:
        def sem(name):
            return ctx.enter_context(nc.semaphore(name))

        def sb(name, shape, dt=F32, scope=ctx):
            return scope.enter_context(nc.sbuf_tensor(name, shape, dt))

        bank = [ctx.enter_context(nc.psum_tensor(f"bank{i}", [P, 512], F32)) for i in range(4)]
        wide = [ctx.enter_context(nc.psum_tensor(f"wide{i}", [P, 2, 512], F32)) for i in range(2)]
        PS = [bank[0][:, :], bank[1][:, :], bank[2][:, :], bank[3][:, :],
              wide[0][:, 0, :], wide[0][:, 1, :], wide[1][:, 0, :], wide[1][:, 1, :]]

        x = sb("x", [P, NT, D])
        xn = sb("xn", [P, NT, D])
        xT = sb("xT", [P, TOK])
        ident = sb("ident", [P, P])
        gates = sb("gates", [P, 4])
        tg = sb("tg", [P, 4])
        eps = sb("eps", [P, 1])
        ones_row = sb("ones_row", [1, P])
        stats = sb("stats", [P, NT, 6])
        mv = sb("mv", [P, NT, 2])
        sd = sb("sd", [P, NT])
        rstd = sb("rstd", [P, NT])
        ctxT = [sb(f"ctxT{s}", [P, SKP]) for s in range(SLOTS)]
        rows = sb("rows", [1, 2 * D + E0])
        wq1 = sb("wq1", [P, HG, MASK_ROW])
        wk1 = sb("wk1", [P, D])
        wv1 = sb("wv1", [P, D])
        wo1 = sb("wo1", [P, D])
        spread = sb("spread", [H, P])
        bcol = sb("bcol", [P, 2])
        bq1 = sb("bq1", [MASK_ROW, HG])
        own_head = sb("own_head", [MASK_ROW, GH])
        q96 = sb("q96", [MASK_ROW, HG, TOK], F32R)
        qs = [sb(f"qs{s}", [P, HG, GH, SQ], F32R) for s in range(SLOTS)]
        qm = [sb(f"qm{s}", [P, HG, GH, SQ], F32R) for s in range(SLOTS)]
        order_0 = sb("order_0", [P, NT, E0])
        order_1 = sb("order_1", [P, NT * 3, E1])

        one = ExitStack()
        qk = sb("qk", [P, TOK * H], scope=one)
        G = sb("G", [P, H, D], scope=one)
        M = sb("M", [P, H, D], scope=one)
        pick_f = sb("pick_f", [QG, P], scope=one)
        pick = sb("pick", [QG, P], BF16, scope=one)
        block_f = sb("block_f", [QG, 3, GK], scope=one)
        blockm = sb("blockm", [QG, 3, GK], BF16, scope=one)
        w1 = sb("w1", [P, E0, D], scope=one)
        w2 = sb("w2", [P, E0, D], scope=one)
        w3 = sb("w3", [P, E0, D], scope=one)
        gwT = sb("gwT", [P, E0], scope=one)
        b12 = sb("b12", [P, 2, E0], scope=one)
        b3 = sb("b3", [E0, D], scope=one)
        attn = ExitStack()
        ctxn = [sb(f"ctxn{s}", [CK, 2 * NG, D], scope=attn) for s in range(SLOTS)]
        qslot = [sb(f"qslot{s}", [P, SQ * H], scope=attn) for s in range(SLOTS)]
        p0 = [sb(f"p0_{s}", [P, 2, GK], scope=attn) for s in range(SLOTS)]
        p0T = [sb(f"p0T_{s}", [CK, 2, 2, P], scope=attn) for s in range(SLOTS)]
        nmax0 = sb("nmax0", [P, SLOTS, 2], scope=attn)
        psum0 = sb("psum0", [P, SLOTS, 2], scope=attn)
        rsum0 = sb("rsum0", [P, SLOTS, 2], scope=attn)
        attn.close()
        moe = ExitStack()
        h1 = [sb(f"h1_{s}", [P, 512], scope=moe) for s in range(2)]
        h2 = [sb(f"h2_{s}", [P, 512], scope=moe) for s in range(2)]
        acc0 = sb("acc0", [P, NT, D], scope=moe)
        probs = sb("probs", [P, NT, E0], scope=moe)
        left = sb("left", [P, NT, E0], scope=moe)
        pick0 = sb("pick0", [P, NT, E0], scope=moe)
        cw = sb("cw", [P, NT, E0], scope=moe)
        top0 = sb("top0", [P, NT], scope=moe)
        cwT = sb("cwT", [E0, TOK], scope=moe)
        moe.close()
        one.close()
        early = ExitStack()
        wq0 = sb("wq0", [DH0, H, D], scope=early)
        wk0 = sb("wk0", [DH0, H, D], scope=early)
        wv0 = sb("wv0", [DH0, H, D], scope=early)
        wo0 = sb("wo0", [DH0, H, D], scope=early)
        mask8 = sb("mask8", [B, SK], U8, scope=early)
        maskr = sb("maskr", [B, SKP], F32R, scope=early)
        early.close()

        two = ExitStack()
        kstack = [sb(f"kstack{s}", [P, HG, SKP], F32R, scope=two) for s in range(SLOTS)]
        k12 = sb("k12", [P, 2, SKP], F32R, scope=two)
        V = [sb(f"V{s}", [P, KT, VW], scope=two) for s in range(SLOTS)]
        p1 = [sb(f"p1_{s}", [P, 2, 2 * QCOLS], scope=two) for s in range(3)]
        mx3 = sb("mx3", [PQ, PAIRS, KC], scope=two)
        negm = sb("negm", [P, 32], scope=two)
        negmT = sb("negmT", [P, 32], scope=two)
        pv = sb("pv", [P, B, 336], scope=two)
        two.close()

        four = ExitStack()
        f1 = sb("f1", [P, E1, D], scope=four)
        f2 = sb("f2", [P, E1, D], scope=four)
        pwT = sb("pwT", [P, PADDR], scope=four)
        uT = sb("uT", [PADDR, 3 * E1], scope=four)
        fb2 = sb("fb2", [E1, D], scope=four)
        oT = sb("oT", [P, TOK], scope=four)
        den = sb("den", [H, TOK], scope=four)
        rden = sb("rden", [H, TOK], scope=four)
        xaT = sb("xaT", [PADDR, TOK], scope=four)
        z = sb("z", [P, NT * 3, E1], scope=four)
        zl = sb("zl", [P, NT * 3, E1], scope=four)
        ez = sb("ez", [P, NT * 3, E1], scope=four)
        sel = sb("sel", [P, NT * 3, E1], scope=four)
        pk = sb("pk", [P, NT * 3, E1], scope=four)
        C = sb("C", [P, NT * 3, E1], scope=four)
        top1 = sb("top1", [P, NT * 3], scope=four)
        top2 = sb("top2", [P, NT * 3], scope=four)
        c3T = sb("c3T", [E1, TOK], scope=four)
        y1 = sb("y1", [P, NT, D], scope=four)
        hg = sb("hg", [P, NT, D], scope=four)
        hT = sb("hT", [P, TOK], scope=four)
        y2 = sb("y2", [P, NT, D], scope=four)
        four.close()

        x_loaded = sem("x_loaded")
        w0_loaded = sem("w0_loaded")
        small_loaded = sem("small_loaded")
        ffn0_loaded = sem("ffn0_loaded")
        ffn1_loaded = sem("ffn1_loaded")
        ctxT_loaded = [sem(f"ctxT_loaded{s}") for s in range(SLOTS)]
        ctxn_loaded = [sem(f"ctxn_loaded{s}") for s in range(SLOTS)]
        v_step = sem("v_step")
        pool_done = sem("pool_done")
        const_done = sem("const_done")
        var_done = sem("var_done")
        sd_done = sem("sd_done")
        xn_done = sem("xn_done")
        xnT_done = sem("xnT_done")
        xT_done = sem("xT_done")
        g_done, g_kept = sem("g_done"), sem("g_kept")
        m_done, m_kept = sem("m_done"), sem("m_kept")
        qk_done = sem("qk_done")
        qk_kept = [sem("qk_kept_first_half"), sem("qk_kept_second_half")]
        qslot_done = sem("qslot_done")
        s0_done, max0_done, exp0_done, norm0_done = sem("s0_done"), sem("max0_done"), sem("exp0_done"), sem("norm0_done")
        recip0_done, order_done = sem("recip0_done"), sem("order_done")
        p0T_done, p0T_kept = sem("p0T_done"), sem("p0T_kept")
        ac_done, ac_bank_free = sem("ac_done"), sem("ac_bank_free")
        o_done = sem("o_done")
        x_new = sem("x_new")
        gate_done, gate_sub, gate_exp = sem("gate_done"), sem("gate_sub"), sem("gate_exp")
        cw_done, cwT_done, cwT_kept = sem("cw_done"), sem("cwT_done"), sem("cwT_kept")
        b3_done, b3_kept = sem("b3_done"), sem("b3_kept")
        l1_done, l1_kept = sem("l1_done"), sem("l1_kept")
        l2_done, l2_kept = sem("l2_done"), sem("l2_kept")
        l3_done, l3_kept = sem("l3_done"), sem("l3_kept")
        k12_stored = [sem(f"k12_stored{c}") for c in range(KC)]
        q_done, q1_kept, q2_kept = sem("q_done"), sem("q1_kept"), sem("q2_kept")
        mask_loaded, maskr_done, mask_stored = sem("mask_loaded"), sem("maskr_done"), sem("mask_stored")
        k_done, k1_kept, k2_kept = sem("k_done"), sem("k1_kept"), sem("k2_kept")
        v_done, v_kept = sem("v_done"), sem("v_kept")
        kst_loaded = [[sem(f"kst_loaded{s}_{c}") for c in range(KC)] for s in range(SLOTS)]
        qs_done, qm_done = sem("qs_done"), sem("qm_done")
        kones_done, vones_done = sem("kones_done"), sem("vones_done")
        m1_done, m1_kept = sem("m1_done"), sem("m1_kept")
        negm_done, negmT_done = sem("negm_done"), sem("negmT_done")
        c_loaded = [sem(f"c_loaded{s}") for s in range(SLOTS)]
        st_done, exp1_done = sem("st_done"), sem("exp1_done")
        pv_done, pv_bank_free = sem("pv_done"), sem("pv_bank_free")
        oT_loaded, oT_done = sem("oT_loaded"), sem("oT_done")
        rden_done, spread_done = sem("rden_done"), sem("spread_done")
        xa_done, xa_kept = sem("xa_done"), sem("xa_kept")
        z_done, zsub_done, ez_done = sem("z_done"), sem("zsub_done"), sem("ez_done")
        C_done, c3T_done, c3T_kept = sem("C_done"), sem("c3T_done"), sem("c3T_kept")
        fb_done, fb_kept = sem("fb_done"), sem("fb_kept")
        mix_done, mix_kept = sem("mix_done"), sem("mix_kept")
        hg_done, hT_done, hT_kept = sem("hg_done"), sem("hT_done"), sem("hT_kept")
        out_done = sem("out_done")

        NUNITS = B * NU
        NTILES = B * KT
        NM = PAIRS * KC
        KDMA = 4

        mask_rows = nc.dram_tensor("mask_rows", (B, SKP), F32).ap()
        k12_rows = nc.dram_tensor("k12_rows", (B, P, 2, SKP), F32).ap()

        block = ctx.enter_context(nc.Block())

        @block.sync
        def _(sp):
            sp.dma_start(x[:, :, :], a["x"]).then_inc(x_loaded, 16)
            sp.dma_start(ident[:, :], a["ident"]).then_inc(x_loaded, 16)
            for name, t in (("wq0", wq0), ("wk0", wk0), ("wv0", wv0), ("wo0", wo0)):
                sp.dma_start(t[:, :, :], a[name]).then_inc(w0_loaded, 16)
            sp.dma_start(mask8[:, :], a["mask"]).then_inc(mask_loaded, 16)
            for s in range(SLOTS):
                sp.dma_start(ctxT[s][:, :], a["ctxT"][s]).then_inc(ctxT_loaded[s], 16)
                sp.dma_start(ctxn[s][:, :, :], a["ctxn"][s]).then_inc(ctxn_loaded[s], 16)
            for name, t in (("pick", pick_f[:, :]), ("block", block_f[:, :, :]), ("rows", rows[:, :]),
                            ("gates", gates[:, :]), ("wq1", wq1[:, :, :]), ("bq1", bq1[:, :]), ("own_head", own_head[:, :]), ("wk1", wk1[:, :]), ("wv1", wv1[:, :]),
                            ("wo1", wo1[:, :]), ("bcol", bcol[:, :]), ("spread", spread[:, :])):
                sp.dma_start(t, a[name]).then_inc(small_loaded, 16)
            sp.wait_ge(maskr_done, 1)
            sp.dma_start(mask_rows, raw(maskr[:, :])).then_inc(mask_stored, 16)
            for name, t in (("w1", w1[:, :, :]), ("w2", w2[:, :, :]), ("w3", w3[:, :, :]), ("gwT", gwT[:, :]),
                            ("b12", b12[:, :, :]), ("b3", b3[:, :])):
                sp.dma_start(t, a[name]).then_inc(ffn0_loaded, 16)

            with sp.Fori(0, B // SLOTS - 1) as i:
                for s in range(SLOTS):
                    b = i * SLOTS + s
                    sp.wait_ge(s0_done, (b + 1) * NU)
                    sp.dma_start(ctxT[s][:, :], a["ctxT"][bass.ds(b + SLOTS, 1)].rearrange("o p n -> (o p) n")).then_inc(ctxT_loaded[s], 16)
                    sp.wait_ge(ac_done, (b + 1) * NU)
                    sp.dma_start(ctxn[s][:, :, :], a["ctxn"][bass.ds(b + SLOTS, 1)].rearrange("o p c d -> (o p) c d")).then_inc(ctxn_loaded[s], 16)
            for s in range(SLOTS):
                sp.wait_ge(s0_done, (B - SLOTS + s + 1) * NU)
                sp.dma_start(ctxT[s][:, :], a["ctxT"][s]).then_inc(ctxT_loaded[s], 16)

            def stack_keys(b, s, c):
                cols = slice(c * 512, (c + 1) * 512)
                sp.dma_start(raw(kstack[s][MASK_ROW:MASK_ROW + 1, :, cols]),
                             mask_rows[bass.ds(b, 1), cols].unsqueeze(1).to_broadcast([1, HG, 512])).then_inc(kst_loaded[s][c], 16)
                sp.wait_ge(k12_stored[c], (b + 1) * 16)
                for part, src in enumerate((0, 0, 1)):
                    sp.dma_start(raw(kstack[s][part * GROWS:(part + 1) * GROWS, :, cols]),
                                 k12_rows[bass.ds(b, 1), :, src, cols].rearrange("o (g r) n -> r (o g) n", r=GROWS)).then_inc(kst_loaded[s][c], 16)

            def load_max(b, s):
                sp.wait_ge(negmT_done, b + 1)
                dst = qs[s][MAX_ROW:MAX_ROW + 1, :, :, :].rearrange("o g (k h) q -> o (g k) (h q)", k=2)
                for r in range(4):
                    n = min(32, PQ - 32 * r)
                    sp.dma_start(raw(dst[:, :, 32 * r:32 * r + n]), negmT[32 * r:32 * r + PAIRS, 0:n]).then_inc(c_loaded[s], 16)

            sp.wait_ge(mask_stored, 16)
            for s in range(SLOTS):
                sp.wait_ge(kones_done, s + 1)
                for c in range(KC):
                    stack_keys(s, s, c)
            sp.wait_ge(v_done, KC)
            sp.dma_start(ctxT[0][:, :], a["ctxT"][SLOTS]).then_inc(ctxT_loaded[0], 16)

            load_max(0, 0)

            def sample(i, s, last):
                b = i * SLOTS + s
                if not (last or (s == 1 and type(b) is int)):
                    sp.wait_ge(v_done, (b + 2) * KC)
                    sp.dma_start(ctxT[1 - s][:, :], a["ctxT"][bass.ds(b + 3, 1)].rearrange("o p n -> (o p) n")).then_inc(ctxT_loaded[1 - s], 16)
                for c in range(KC):
                    if c == KC - 1 and not (last and s == 1):
                        load_max(b + 1, 1 - s)
                    if not last:
                        sp.wait_ge(st_done, b * KT + 4 * (c + 1))
                        stack_keys(b + SLOTS, s, c)

            with sp.Fori(0, B // SLOTS - 2) as i:
                for s in range(SLOTS):
                    sample(i, s, False)
            for s in range(SLOTS):
                sample(B // SLOTS - 2, s, False)
            for s in range(SLOTS):
                sample(B // SLOTS - 1, s, True)

            sp.wait_ge(st_done, NTILES - KT)
            for name, t in (("f1", f1[:, :, :]), ("f2", f2[:, :, :]), ("pwT", pwT[:, :]), ("uT", uT[:, :]), ("fb2", fb2[:, :])):
                sp.dma_start(t, a[name]).then_inc(ffn1_loaded, 16)
            sp.wait_ge(pv_bank_free, B + 1)
            for h in range(H):
                g, hh = h // 3, h % 3
                row = 32 * (g % 4) + hh * VH
                col = 168 * (g // 4) + hh * SQ
                dst = oT[h * DH1:(h + 1) * DH1, :].rearrange("p (b q) -> p b q", b=B)
                ddn = den[h:h + 1, :].rearrange("p (b q) -> p b q", b=B)
                sp.dma_start(dst, pv[row:row + DH1, :, col:col + SQ]).then_inc(oT_loaded, 16)
                sp.dma_start(ddn, pv[row + DH1:row + VH, :, col:col + SQ]).then_inc(oT_loaded, 16)

            for n, (t0, nt) in enumerate(HALVES):
                sp.wait_ge(x_new, 3 * 2 + n + 1)
                sp.dma_start(out[:, t0:t0 + nt, :], x[:, t0:t0 + nt, :]).then_inc(out_done, 16)
            sp.wait_ge(out_done, 32)

        @block.gpsimd
        def _(pool):
            for s in range(SLOTS):
                for m, buf in enumerate((qs[s], qm[s])):
                    nc.gpsimd.memset(buf[MASK_ROW:P, :, :, :].bitcast(F32), 0.0).then_inc(pool_done, 1)
                    pool.wait_ge(pool_done, 4 * s + 2 * m + 1)
                    nc.gpsimd.memset(buf[MASK_ROW:MASK_ROW + 1, :, :, :].bitcast(F32), 1.0).then_inc(pool_done, 1)
            pool.wait_ge(pool_done, 4 * SLOTS)
            nc.gpsimd.iota(order_0[:, :, :], [[0, NT], [-1, E0]], base=E0, channel_multiplier=0,
                           allow_small_or_imprecise_dtypes=True).then_inc(order_done, 1)
            nc.gpsimd.iota(order_1[:, :, :], [[0, NT * 3], [-1, E1]], base=E1, channel_multiplier=0,
                           allow_small_or_imprecise_dtypes=True).then_inc(order_done, 1)

            pool.wait_ge(qk_kept[0], H)
            pool.wait_ge(qk_kept[1], H)
            for s in range(SLOTS):
                nc.gpsimd.tensor_copy(qslot[s][:, :], qk[:, s * SQ * H:(s + 1) * SQ * H]).then_inc(qslot_done, 1)
            with pool.Fori(0, B // SLOTS - 1) as i:
                for s in range(SLOTS):
                    b = i * SLOTS + s
                    pool.wait_ge(s0_done, (b + 1) * NU)
                    nc.gpsimd.tensor_copy(qslot[s][:, :], qk[:, bass.ds((b + SLOTS) * (SQ * H), SQ * H)]).then_inc(qslot_done, 1)

            def store_keys(b, c):
                cols = slice(c * 512, (c + 1) * 512)
                pool.wait_ge(k2_kept, b * KC + c + 1)
                pool.dma_start(k12_rows[bass.ds(b, 1), :, :, cols].rearrange("o p k n -> (o p) k n"),
                               raw(k12[:, :, cols])).then_inc(k12_stored[c], 16)

            pool.wait_ge(x_new, 2)
            for s in range(SLOTS):
                nc.gpsimd.memset(kstack[s][MASK_ROW:P, :, :].bitcast(F32), 1.0).then_inc(kones_done, 1)
                pool.wait_ge(kones_done, s + 1)
                nc.gpsimd.memset(V[s][:, :, 0:H * VH].rearrange("p t (h e) -> p t h e", e=VH)[:, :, :, DH1:VH], 1.0).then_inc(vones_done, 1)
                pool.wait_ge(vones_done, 2 * s + 1)
                nc.gpsimd.memset(V[s][:, :, H * VH:VW], 1.0).then_inc(vones_done, 1)
                pool.wait_ge(vones_done, 2 * s + 2)
            for b in range(SLOTS):
                for c in range(KC):
                    store_keys(b, c)

            def expand(dst, b, signal):
                src = q96[:, :, bass.ds(b * SQ, SQ)].bitcast(F32)
                nc.gpsimd.tensor_tensor(dst[0:MASK_ROW, :, :, :], src.unsqueeze(2).to_broadcast([MASK_ROW, HG, GH, SQ]),
                                        own_head[:, :].unsqueeze(1).unsqueeze(3).to_broadcast([MASK_ROW, HG, GH, SQ]),
                                        ALU.mult).then_inc(signal, 1)

            pool.wait_ge(small_loaded, 192)
            pool.wait_ge(q1_kept, 2 * HG)
            pool.wait_ge(q2_kept, 2 * HG)
            expand(qm[0], 0, qm_done)
            expand(qs[0], 0, qs_done)
            expand(qm[1], 1, qm_done)
            with pool.Fori(0, B // SLOTS - 1) as i:
                for s in range(SLOTS):
                    b = i * SLOTS + s
                    store_keys(b + SLOTS, 0)
                    expand(qs[1 - s], b + 1, qs_done)
                    expand(qm[s], b + SLOTS, qm_done)
                    for c in range(1, KC):
                        store_keys(b + SLOTS, c)
            pool.wait_ge(st_done, (B - SLOTS) * KT)
            expand(qs[1], B - 1, qs_done)

        @block.tensor
        def _(pe):
            def transpose_x(n):
                pe.wait_ge(xn_done, n + 1)
                for j, (t0, nt) in enumerate(HALVES):
                    for t in range(nt):
                        mm = pe.transpose(PS[4 + j][:, t * P:(t + 1) * P], xn[:, t0 + t, :], ident[:, :])
                    mm.then_inc(xnT_done, 1)

            def add_row(psum, row, n, stop=True):
                return pe.matmul(psum, ones_row[:, :], row, start=False, stop=stop)

            pe.wait_ge(w0_loaded, 64)
            for j in range(4):
                if j >= 2:
                    pe.wait_ge(g_kept, j - 1)
                for h in range(4):
                    mm = pe.matmul(PS[j % 2][:, h * D:(h + 1) * D], wq0[:, 4 * j + h, :], wk0[:, 4 * j + h, :], start=True, stop=True)
                mm.then_inc(g_done, 1)
            for j in range(4):
                if j >= 2:
                    pe.wait_ge(m_kept, j - 1)
                for h in range(4):
                    mm = pe.matmul(PS[2 + j % 2][:, h * D:(h + 1) * D], wv0[:, 4 * j + h, :], wo0[:, 4 * j + h, :], start=True, stop=True)
                mm.then_inc(m_done, 1)
            pe.wait_ge(x_loaded, 32)
            transpose_x(0)
            pe.wait_ge(g_kept, 4)
            pe.wait_ge(m_kept, 4)
            pe.wait_ge(xT_done, 2)
            for n in range(2 * H):
                h, half = divmod(n, 2)
                if n >= 4:
                    pe.wait_ge(qk_kept[half], h - 1)
                pe.matmul(PS[n % 4][:, 0:448], G[:, h, :], xT[:, half * 448:(half + 1) * 448], start=True, stop=True).then_inc(qk_done, 1)

            def scores0(par, u, s):
                first, cnt = UNITS[u]
                for g in range(cnt):
                    grp = first + g
                    i0 = grp * QG
                    kind = 0 if i0 + QG <= LASTQ else (1 if i0 < LASTQ else 2)
                    dst = PS[par][:, g * 256:g * 256 + GK]
                    keys = ctxT[s][:, 0:KPQ * SQ].rearrange("p (t i) -> p i t", i=SQ)[:, i0:i0 + QG, :]
                    pe.matmul(dst, qslot[s][:, i0 * H:(i0 + QG) * H], keys, start=True, stop=False)
                    mm = pe.matmul(dst, pick[:, :], blockm[:, kind, :], start=False, stop=True)
                mm.then_inc(s0_done, 1)

            def transposes0(u, par):
                first, cnt = UNITS[u]
                for g in range(cnt):
                    for c in range(2):
                        mm = pe.transpose(PS[2 + par][0:CK, (2 * g + c) * P:(2 * g + c + 1) * P],
                                          p0[par][:, g, c * CK:(c + 1) * CK], ident[:, :])
                mm.then_inc(p0T_done, 1)

            def values0(u, par, s):
                first, cnt = UNITS[u]
                for g in range(cnt):
                    for c in range(2):
                        mm = pe.matmul(PS[4 + 2 * par][:, g * P:(g + 1) * P], ctxn[s][:, 2 * (first + g) + c, :],
                                       p0T[par][:, g, c, :], start=(c == 0), stop=(c == 1))
                mm.then_inc(ac_done, 1)

            def next_sample(s, nxt):
                pe.wait_ge(ctxT_loaded[s], 16 * (nxt + 1))
                pe.wait_ge(qslot_done, nxt * SLOTS + s + 1)

            def body0(i, last):
                for k in range(SLOTS * NU):
                    n = i * (SLOTS * NU) + k
                    k3, k1 = k + AHEAD, k + 1
                    if not (last and k3 >= SLOTS * NU):
                        s3, u3 = (k3 // NU) % SLOTS, k3 % NU
                        if u3 == 0:
                            next_sample(s3, i + k3 // (SLOTS * NU))
                        pe.wait_ge(exp0_done, n + 2)
                        scores0(k3 % 2, u3, s3)
                    if not (last and k1 >= SLOTS * NU):
                        pe.wait_ge(norm0_done, n + 2)
                        transposes0(k1 % NU, k1 % 2)
                    s0, u0 = k // NU, k % NU
                    if u0 == 0:
                        pe.wait_ge(ctxn_loaded[s0], 16 * (i + 1))
                    pe.wait_ge(p0T_kept, n + 1)
                    pe.wait_ge(ac_bank_free, n + 1)
                    values0(u0, k % 2, s0)

            pe.wait_ge(const_done, 1)
            pe.wait_ge(qk_kept[0], H)
            pe.wait_ge(qk_kept[1], H)
            next_sample(0, 0)
            scores0(0, 0, 0)
            scores0(1, 1, 0)
            pe.wait_ge(exp0_done, 1)
            scores0(0, 2, 0)
            pe.wait_ge(norm0_done, 1)
            transposes0(0, 0)
            with pe.Fori(0, B // SLOTS - 1) as i:
                body0(i, False)
            body0(B // SLOTS - 1, True)

            def project_out(n, weight_of, lhs_of, count, row):
                for j, (t0, nt) in enumerate(HALVES):
                    for t in range(nt):
                        dst = PS[j][:, t * P:(t + 1) * P]
                        for h in range(count):
                            pe.matmul(dst, lhs_of(t0 + t, h), weight_of(h), start=(h == 0), stop=False)
                        mm = add_row(dst, row, D)
                    mm.then_inc(o_done, 1)

            pe.wait_ge(ac_bank_free, NUNITS + 2)
            qk_v = qk[:, :].rearrange("p (t h) -> p h t", h=H)
            project_out(0, lambda h: M[:, h, :], lambda t, h: qk_v[:, h, t * P:(t + 1) * P], H, rows[:, 0:D])

            transpose_x(1)
            pe.wait_ge(xT_done, 4)
            pe.wait_ge(ffn0_loaded, 96)
            for t in range(NT):
                pe.matmul(PS[6][:, t * E0:(t + 1) * E0], xT[:, t * P:(t + 1) * P], gwT[:, :], start=True, stop=False)
                mm = add_row(PS[6][:, t * E0:(t + 1) * E0], rows[:, 2 * D:2 * D + E0], E0)
            mm.then_inc(gate_done, 1)

            def width(s):
                return HALVES[s % 2][0] * P, HALVES[s % 2][1] * P

            def layer1(s):
                t0, w = width(s)
                if s >= 2:
                    pe.wait_ge(l1_kept, s - 1)
                pe.matmul(PS[s % 2][:, 0:w], w1[:, s // 2, :], xT[:, t0:t0 + w], start=True, stop=True).then_inc(l1_done, 1)

            def layer2(s):
                t0, w = width(s)
                pe.wait_ge(l1_kept, s + 1)
                if s >= 2:
                    pe.wait_ge(l2_kept, s - 1)
                pe.matmul(PS[2 + s % 2][:, 0:w], w2[:, s // 2, :], h1[s % 2][:, 0:w], start=True, stop=True).then_inc(l2_done, 1)

            def layer3(s):
                t0, w = width(s)
                pe.wait_ge(l2_kept, s + 1)
                if s >= 2:
                    pe.wait_ge(l3_kept, s - 1)
                for t in range(w // P):
                    mm = pe.matmul(PS[4 + s % 2][:, t * P:(t + 1) * P], h2[s % 2][:, t * P:(t + 1) * P], w3[:, s // 2, :], start=True, stop=True)
                mm.then_inc(l3_done, 1)

            def keys(b, s, c, psum):
                if c == 0:
                    if not (type(b) is int and b == 0):
                        pe.wait_ge(v_kept, b * KC)
                else:
                    pe.wait_ge(k2_kept, b * KC + c)
                pe.matmul(psum, wk1[:, :], ctxT[s][:, c * 512:(c + 1) * 512], start=True, stop=True).then_inc(k_done, 1)

            def values(b, s, c, psum):
                if c == 0:
                    pe.wait_ge(k2_kept, (b + 1) * KC)
                else:
                    pe.wait_ge(v_kept, b * KC + c)
                for t in range(4):
                    mm = pe.matmul(psum[:, t * P:(t + 1) * P], ctxT[s][:, (4 * c + t) * P:(4 * c + t + 1) * P], wv1[:, :], start=True, stop=True)
                mm.then_inc(v_done, 1)

            NS = 2 * E0
            pe.wait_ge(x_new, 2)
            layer1(0)
            layer1(1)
            layer2(0)
            pe.wait_ge(cw_done, 1)
            for j, (t0, nt) in enumerate(HALVES):
                for t in range(nt):
                    mm = pe.transpose(PS[6 + j][0:E0, t * P:(t + 1) * P], cw[:, t0 + t, :], ident[:, :])
                mm.then_inc(cwT_done, 1)
            pe.wait_ge(cwT_kept, 2)
            for j, (t0, nt) in enumerate(HALVES):
                for t in range(nt):
                    mm = pe.matmul(PS[6 + j][:, t * P:(t + 1) * P], cwT[:, (t0 + t) * P:(t0 + t + 1) * P], b3[:, :], start=True, stop=True)
                mm.then_inc(b3_done, 1)
            for s in range(NS):
                if s + 2 < NS:
                    layer1(s + 2)
                if s + 1 < NS:
                    layer2(s + 1)
                layer3(s)
                if s == 0:
                    pe.wait_ge(b3_kept, 2)
                    for b in range(SLOTS):
                        pe.wait_ge(ctxT_loaded[b], 16 * (B // SLOTS + 1))
                if 1 <= s <= SLOTS * 2 * KC:
                    b, piece = divmod(s - 1, 2 * KC)
                    (keys if piece < KC else values)(b, b, piece % KC, PS[7])

            transpose_x(2)
            pe.wait_ge(xT_done, 6)
            for m in range(2 * HG):
                g, j = divmod(m, 2)
                if m >= 4:
                    pe.wait_ge(q2_kept, m - 3)
                pe.matmul(PS[m % 4][0:MASK_ROW, 0:448], wq1[:, g, :], xT[:, j * 448:(j + 1) * 448], start=True, stop=True).then_inc(q_done, 1)
            pe.wait_ge(q2_kept, 2 * HG)

            MB, PVB = (PS[1], PS[2]), PS[3]

            def maximum(b, s, n, m):
                c, pair = divmod(m, PAIRS)
                if m == 0:
                    pe.wait_ge(qm_done, b + 1)
                if pair == 0:
                    pe.wait_ge(kst_loaded[s][c], 16 * KDMA * (n + 1))
                if not (type(b) is int and b == 0 and m < 2):
                    pe.wait_ge(m1_kept, b * NM + (m - 1))
                q = qm[s][0:MAX_ROW, pair // 2, 2 * (pair % 2):2 * (pair % 2) + 2, :]
                pe.matmul(MB[m % 2][0:PQ, :], q, kstack[s][0:MAX_ROW, pair // 2, c * 512:(c + 1) * 512],
                          start=True, stop=True).then_inc(m1_done, 1)

            def scores1(s, t):
                for g in range(HG):
                    mm = pe.matmul(wide[t % 2][:, g // 2, (g % 2) * QCOLS:(g % 2 + 1) * QCOLS],
                                   kstack[s][:, g, t * P:(t + 1) * P], qs[s][:, g, :, :], start=True, stop=True)
                mm.then_inc(st_done, 1)

            def values1(s, t):
                for g in range(PG):
                    heads = 3 if g < 5 else 1
                    pcols = p1[t % 3][:, :, :].rearrange("p a c -> p (a c)")[:, 3 * g * SQ:(3 * g + heads) * SQ]
                    mm = pe.matmul(PVB[32 * (g % 4):32 * (g % 4) + 32, 168 * (g // 4):168 * (g // 4) + heads * SQ],
                                   V[s][:, t, 3 * VH * g:3 * VH * g + 32], pcols,
                                   start=(t == 0 and g < 4), stop=(t == KT - 1), skip_group_check=True)
                mm.then_inc(pv_done, 1)

            for m in range(NM):
                maximum(0, 0, 0, m)
            for m in range(PAIRS):
                maximum(1, 1, 0, m)
            pe.wait_ge(v_kept, SLOTS * KC)
            pe.wait_ge(c_loaded[0], 64)
            pe.wait_ge(qs_done, 1)
            scores1(0, 0)
            scores1(0, 1)

            def body1(i, last):
                for s in range(SLOTS):
                    b = i * SLOTS + s
                    final = last and s == 1
                    for t in range(KT):
                        pe.wait_ge(exp1_done, b * KT + t + 1)
                        if t + 2 < KT:
                            scores1(s, t + 2)
                        elif not final:
                            if t + 2 == KT:
                                pe.wait_ge(c_loaded[1 - s], 64 * (i + s + 1))
                                pe.wait_ge(qs_done, b + 2)
                            scores1(1 - s, t + 2 - KT)
                        if t == 0:
                            pe.wait_ge(v_kept, (b + 1) * KC)
                            pe.wait_ge(pv_bank_free, b + 1)
                        values1(s, t)
                        for m in (2 * t, 2 * t + 1):
                            if t < KT - 4 and not final:
                                maximum(b + 1, 1 - s, i + s, PAIRS + m)
                            if t >= KT - 4 and not last:
                                maximum(b + SLOTS, s, i + 1, m - 2 * (KT - 4))
                        if not last:
                            if t == 0:
                                pe.wait_ge(ctxT_loaded[s], 16 * (B // SLOTS + 2) + 16 * i)
                            if t in (1, 3, 5):
                                keys(b + SLOTS, s, (t - 1) // 2, PS[0])
                            if t in (7, 9, 11):
                                values(b + SLOTS, s, (t - 7) // 2, PS[0])

            with pe.Fori(0, B // SLOTS - 1) as i:
                body1(i, False)
            body1(B // SLOTS - 1, True)

            pe.wait_ge(rden_done, 1)
            for j in range(2):
                pe.matmul(PS[2 + j][:, 0:448], spread[:, :], rden[:, j * 448:(j + 1) * 448], start=True, stop=True).then_inc(spread_done, 1)
            pe.wait_ge(oT_done, 1)
            project_out(1, lambda h: wo1[:, :], lambda t, h: oT[:, t * P:(t + 1) * P], 1, rows[:, D:2 * D])

            transpose_x(3)
            pe.wait_ge(xT_done, 8)
            pe.wait_ge(ffn1_loaded, 80)
            for j in range(2):
                pe.matmul(PS[2 + j][0:PADDR, 0:448], pwT[:, :], xT[:, j * 448:(j + 1) * 448], start=True, stop=True).then_inc(xa_done, 1)
            pe.wait_ge(xa_kept, 2)
            for t in range(NT):
                mm = pe.matmul(PS[2][:, t * 3 * E1:(t + 1) * 3 * E1], xaT[:, t * P:(t + 1) * P], uT[:, :], start=True, stop=True)
            mm.then_inc(z_done, 1)

            def mixture(which, src, w):
                for n in range(NT * 3):
                    t, e4 = divmod(n, 3)
                    m = which * NT * 3 + n
                    if m >= 4:
                        pe.wait_ge(mix_kept, m - 3)
                    pe.matmul(PS[4 + m % 4][:, :], src[:, t * P:(t + 1) * P],
                              w[:, 4 * e4:4 * e4 + 4, :].rearrange("p e d -> p (e d)"), start=True, stop=True).then_inc(mix_done, 1)

            pe.wait_ge(x_new, 6)
            mixture(0, xT, f1)
            pe.wait_ge(C_done, 1)
            for j, (t0, nt) in enumerate(HALVES):
                for t in range(nt):
                    mm = pe.transpose(PS[j][0:E1, t * P:(t + 1) * P], C[:, 3 * (t0 + t) + 2, :], ident[:, :])
                mm.then_inc(c3T_done, 1)
            pe.wait_ge(c3T_kept, 2)
            for j, (t0, nt) in enumerate(HALVES):
                for t in range(nt):
                    mm = pe.matmul(PS[j][:, t * P:(t + 1) * P], c3T[:, (t0 + t) * P:(t0 + t + 1) * P], fb2[:, :], start=True, stop=True)
                mm.then_inc(fb_done, 1)
            pe.wait_ge(hg_done, 1)
            for j, (t0, nt) in enumerate(HALVES):
                for t in range(nt):
                    mm = pe.transpose(PS[2 + j][:, t * P:(t + 1) * P], hg[:, t0 + t, :], ident[:, :])
                mm.then_inc(hT_done, 1)
            pe.wait_ge(hT_kept, 2)
            mixture(1, hT, f2)

        @block.scalar
        def _(act):
            def norm_parts(n):
                act.wait_ge(var_done, n + 1)
                nc.scalar.activation(sd[:, :], mv[:, :, 1], ACT.Sqrt, bias=eps[:, 0:1]).then_inc(sd_done, 1)
                act.wait_ge(xnT_done, 2 * n + 2)
                nc.scalar.copy(xT[:, 512:TOK], PS[5][:, 0:TOK - 512]).then_inc(xT_done, 1)

            for j in range(4):
                act.wait_ge(g_done, j + 1)
                nc.scalar.mul(G[:, 4 * j:4 * j + 4, :].rearrange("p h d -> p (h d)"), PS[j % 2], DH0 ** -0.5).then_inc(g_kept, 1)
            norm_parts(0)
            act.wait_ge(small_loaded, 192)
            nc.scalar.activation(tg[:, 0:2], gates[:, 0:2], ACT.Tanh).then_inc(ac_bank_free, 1)
            nc.scalar.activation(tg[:, 2:4], gates[:, 2:4], ACT.Tanh).then_inc(ac_bank_free, 1)
            qk_t = qk[:, :].rearrange("p (t h) -> p h t", h=H)
            act.wait_ge(mask_stored, 16)
            for h in range(H):
                act.wait_ge(qk_done, 2 * h + 1)
                nc.scalar.copy(qk_t[:, h, 0:448], PS[2 * h % 4][:, 0:448]).then_inc(qk_kept[0], 1)

            def exp0(u, par, n):
                first, cnt = UNITS[u]
                act.wait_ge(max0_done, n + 1)
                for g in range(cnt):
                    ins = nc.scalar.activation(p0[par][:, g, :], PS[par][:, g * 256:g * 256 + GK], ACT.Exp,
                                               bias=nmax0[:, par, g:g + 1], accum_out=psum0[:, par, g:g + 1])
                ins.then_inc(exp0_done, 1)

            def body0(i, last):
                for k in range(SLOTS * NU):
                    n = i * (SLOTS * NU) + k
                    if not (last and k + AHEAD >= SLOTS * NU):
                        act.wait_ge(p0T_done, n + 2)
                        exp0((k + AHEAD) % NU, (k + AHEAD) % 2, n + AHEAD)
                    act.wait_ge(ac_done, n + 1)
                    first, cnt = UNITS[k % NU]
                    start = (i * SLOTS + k // NU) * (SQ * H) + first * P
                    nc.scalar.copy(qk[:, bass.ds(start, cnt * P)], PS[4 + 2 * (k % 2)][:, 0:cnt * P]).then_inc(ac_bank_free, 1)

            exp0(0, 0, 0)
            exp0(1, 1, 1)
            act.wait_ge(p0T_done, 1)
            exp0(2, 0, 2)
            with act.Fori(0, B // SLOTS - 1) as i:
                body0(i, False)
            body0(B // SLOTS - 1, True)

            norm_parts(1)
            act.wait_ge(gate_sub, 1)
            nc.scalar.activation(left[:, :, :], probs[:, :, :], ACT.Exp).then_inc(gate_exp, 1)

            def relu1(s):
                w = HALVES[s % 2][1] * P
                act.wait_ge(l1_done, s + 1)
                if s >= 2:
                    act.wait_ge(l2_done, s - 1)
                nc.scalar.activation(h1[s % 2][:, 0:w], PS[s % 2][:, 0:w], ACT.Relu, bias=b12[:, 0, s // 2:s // 2 + 1]).then_inc(l1_kept, 1)

            def relu2(s):
                w = HALVES[s % 2][1] * P
                act.wait_ge(l2_done, s + 1)
                if s >= 2:
                    act.wait_ge(l3_done, s - 1)
                nc.scalar.activation(h2[s % 2][:, 0:w], PS[2 + s % 2][:, 0:w], ACT.Relu, bias=b12[:, 1, s // 2:s // 2 + 1]).then_inc(l2_kept, 1)

            def keep_k1(b, c, psum):
                act.wait_ge(k_done, b * KC + c + 1)
                if not (type(b) is int and b == 0):
                    act.wait_ge(k12_stored[c], b * 16)
                nc.scalar.activation(k12[:, 0, c * 512:(c + 1) * 512], psum, ACT.Identity, bias=bcol[:, 0:1]).then_inc(k1_kept, 1)

            NS = 2 * E0
            relu1(0)
            relu1(1)
            relu2(0)
            for s in range(NS):
                if s + 2 < NS:
                    relu1(s + 2)
                if s + 1 < NS:
                    relu2(s + 1)
                if 1 <= s <= SLOTS * 2 * KC and (s - 1) % (2 * KC) < KC:
                    keep_k1((s - 1) // (2 * KC), (s - 1) % (2 * KC), PS[7])

            norm_parts(2)
            for m in range(2 * HG):
                g, j = divmod(m, 2)
                act.wait_ge(q_done, m + 1)
                nc.scalar.activation(q96[:, g, j * 448:(j + 1) * 448], PS[m % 4][0:MASK_ROW, 0:448], ACT.Identity, bias=bq1[:, g:g + 1]).then_inc(q1_kept, 1)

            def body1(i, last):
                for s in range(SLOTS):
                    b = i * SLOTS + s
                    for t in range(KT):
                        act.wait_ge(st_done, b * KT + t + 1)
                        nc.scalar.activation(p1[t % 3][:, :, :], wide[t % 2][:, :, 0:2 * QCOLS], ACT.Exp, scale=SCALE1).then_inc(exp1_done, 1)
                        if not last and t in (2, 4, 6):
                            keep_k1(b + SLOTS, (t - 2) // 2, PS[0])

            with act.Fori(0, B // SLOTS - 1) as i:
                body1(i, False)
            body1(B // SLOTS - 1, True)

            norm_parts(3)
            for j in range(2):
                act.wait_ge(xa_done, j + 1)
                nc.scalar.copy(xaT[:, j * 448:(j + 1) * 448], PS[2 + j][0:PADDR, 0:448]).then_inc(xa_kept, 1)
            act.wait_ge(zsub_done, 1)
            nc.scalar.activation(ez[:, :, :], zl[:, :, :], ACT.Exp).then_inc(ez_done, 1)
            for j, (t0, nt) in enumerate(HALVES):
                act.wait_ge(c3T_done, j + 1)
                nc.scalar.copy(c3T[:, t0 * P:(t0 + nt) * P], PS[j][0:E1, 0:nt * P]).then_inc(c3T_kept, 1)
            for j, (t0, nt) in enumerate(HALVES):
                act.wait_ge(fb_done, j + 1)
                nc.scalar.copy(y2[:, t0:t0 + nt, :].rearrange("p t d -> p (t d)"), PS[j][:, 0:nt * P]).then_inc(fb_kept, 1)
            act.wait_ge(mix_kept, NT * 3)
            nc.scalar.activation(hg[:, :, :], y1[:, :, :], ACT.Gelu).then_inc(hg_done, 1)
            for j, (t0, nt) in enumerate(HALVES):
                act.wait_ge(hT_done, j + 1)
                nc.scalar.copy(hT[:, t0 * P:(t0 + nt) * P], PS[2 + j][:, 0:nt * P]).then_inc(hT_kept, 1)

        @block.vector
        def _(dve):
            steps = [0]

            def link(ins):
                steps[0] += 1
                ins.then_inc(v_step, 1)
                dve.wait_ge(v_step, steps[0])

            def layernorm(n):
                for t in range(NT):
                    ins = nc.vector.bn_stats(stats[:, t, :], x[:, t, :])
                link(ins)
                for t in range(NT):
                    ins = nc.vector.bn_aggr(mv[:, t, :], stats[:, t, :])
                ins.then_inc(var_done, 1)
                dve.wait_ge(sd_done, n + 1)
                link(nc.vector.reciprocal(rstd[:, :], sd[:, :]))
                for t in range(NT):
                    ins = nc.vector.tensor_scalar(xn[:, t, :], x[:, t, :], mv[:, t, 0:1], rstd[:, t:t + 1], ALU.subtract, ALU.mult)
                ins.then_inc(xn_done, 1)

            def keep_xT(n):
                dve.wait_ge(xnT_done, 2 * n + 1)
                nc.vector.tensor_copy(xT[:, 0:512], PS[4]).then_inc(xT_done, 1)

            def bc(ap, n):
                return ap.unsqueeze(2).to_broadcast([P, ap.shape[1], n])

            link(nc.vector.memset(eps[:, :], EPS))
            nc.vector.memset(ones_row[:, :], 1.0)
            dve.wait_ge(x_loaded, 32)
            layernorm(0)
            dve.wait_ge(mask_loaded, 16)
            nc.vector.memset(maskr[:, SK:SKP].bitcast(F32), -BIG)
            nc.vector.tensor_scalar(maskr[:, 0:SK], mask8[:, :], -BIG, None, ALU.mult).then_inc(maskr_done, 1)
            for j in range(4):
                dve.wait_ge(m_done, j + 1)
                nc.vector.tensor_copy(M[:, 4 * j:4 * j + 4, :].rearrange("p h d -> p (h d)"), PS[2 + j % 2]).then_inc(m_kept, 1)
            keep_xT(0)
            dve.wait_ge(small_loaded, 192)
            nc.vector.tensor_copy(pick[:, :], pick_f[:, :])
            nc.vector.tensor_copy(blockm[:, :, :], block_f[:, :, :]).then_inc(const_done, 1)
            qk_t = qk[:, :].rearrange("p (t h) -> p h t", h=H)
            dve.wait_ge(mask_stored, 16)
            for h in range(H):
                dve.wait_ge(qk_done, 2 * h + 2)
                nc.vector.tensor_copy(qk_t[:, h, 448:TOK], PS[(2 * h + 1) % 4][:, 0:448]).then_inc(qk_kept[1], 1)

            def max0(u, par, n):
                cnt = UNITS[u][1]
                dve.wait_ge(s0_done, n + 1)
                nc.vector.tensor_reduce(nmax0[:, par, 0:cnt], PS[par].rearrange("p (g k) -> p g k", g=2)[:, 0:cnt, 0:GK],
                                        AX, ALU.max, negate=True).then_inc(max0_done, 1)

            def norm0(u, par, n):
                cnt = UNITS[u][1]
                dve.wait_ge(exp0_done, n + 1)
                nc.vector.reciprocal(rsum0[:, par, 0:cnt], psum0[:, par, 0:cnt]).then_inc(recip0_done, 1)
                dve.wait_ge(recip0_done, n + 1)
                for g in range(cnt):
                    ins = nc.vector.tensor_scalar(p0[par][:, g, :], p0[par][:, g, :], rsum0[:, par, g:g + 1], None, ALU.mult)
                ins.then_inc(norm0_done, 1)

            def keep_p0T(u, par, n):
                cnt = UNITS[u][1]
                dve.wait_ge(p0T_done, n + 1)
                nc.vector.tensor_copy(p0T[par][:, 0:cnt, :, :].rearrange("p g c q -> p (g c q)"),
                                      PS[2 + par][0:CK, 0:cnt * 256]).then_inc(p0T_kept, 1)

            def body0(i, last):
                for k in range(SLOTS * NU):
                    n = i * (SLOTS * NU) + k
                    keep_p0T(k % NU, k % 2, n)
                    if not (last and k + 2 >= SLOTS * NU):
                        norm0((k + 2) % NU, k % 2, n + 2)
                    if not (last and k + AHEAD >= SLOTS * NU):
                        max0((k + AHEAD) % NU, (k + AHEAD) % 2, n + AHEAD)

            max0(0, 0, 0)
            max0(1, 1, 1)
            norm0(0, 0, 0)
            max0(2, 0, 2)
            norm0(1, 1, 1)
            with dve.Fori(0, B // SLOTS - 1) as i:
                body0(i, False)
            body0(B // SLOTS - 1, True)

            def residual(src_of, n, gate):
                for j, (t0, nt) in enumerate(HALVES):
                    ins = nc.vector.scalar_tensor_tensor(out=x[:, t0:t0 + nt, :].rearrange("p t d -> p (t d)"),
                                                         in0=src_of(j, t0, nt), scalar=tg[:, gate:gate + 1],
                                                         in1=x[:, t0:t0 + nt, :].rearrange("p t d -> p (t d)"),
                                                         op0=ALU.mult, op1=ALU.add)
                    ins.then_inc(x_new, 1)
                dve.wait_ge(x_new, 2 * n + 2)

            dve.wait_ge(ac_bank_free, 2)
            dve.wait_ge(o_done, 2)
            residual(lambda j, t0, nt: PS[j][:, 0:nt * P], 0, 0)

            layernorm(1)
            keep_xT(1)
            dve.wait_ge(gate_done, 1)
            logits = PS[6][:, 0:NT * E0].rearrange("p (t e) -> p t e", e=E0)
            link(nc.vector.tensor_reduce(top0[:, :], logits, AX, ALU.max))
            nc.vector.tensor_tensor(probs[:, :, :], logits, bc(top0[:, :], E0), ALU.subtract).then_inc(gate_sub, 1)
            dve.wait_ge(gate_exp, 1)
            link(nc.vector.tensor_reduce(top0[:, :], left[:, :, :], AX, ALU.add))
            link(nc.vector.reciprocal(top0[:, :], top0[:, :]))
            link(nc.vector.tensor_tensor(probs[:, :, :], left[:, :, :], bc(top0[:, :], E0), ALU.mult))
            link(nc.vector.tensor_copy(left[:, :, :], probs[:, :, :]))

            def first_largest(vals, pick_, top, n, order):
                link(nc.vector.tensor_reduce(top, vals, AX, ALU.max))
                link(nc.vector.tensor_tensor(pick_, vals, bc(top, n), ALU.is_equal))
                link(nc.vector.tensor_tensor(pick_, pick_, order, ALU.mult))
                link(nc.vector.tensor_reduce(top, pick_, AX, ALU.max))
                link(nc.vector.tensor_tensor(pick_, pick_, bc(top, n), ALU.is_equal))

            dve.wait_ge(order_done, 2)
            order0 = order_0[:, :, :]
            first_largest(left[:, :, :], pick0[:, :, :], top0[:, :], E0, order0)
            link(nc.vector.tensor_tensor(cw[:, :, :], pick0[:, :, :], probs[:, :, 0:1].to_broadcast([P, NT, E0]), ALU.mult))
            link(nc.vector.scalar_tensor_tensor(out=left[:, :, :], in0=pick0[:, :, :], scalar=-2.0, in1=left[:, :, :], op0=ALU.mult, op1=ALU.add))
            first_largest(left[:, :, :], pick0[:, :, :], top0[:, :], E0, order0)
            link(nc.vector.tensor_tensor(pick0[:, :, :], pick0[:, :, :], probs[:, :, 1:2].to_broadcast([P, NT, E0]), ALU.mult))
            nc.vector.tensor_tensor(cw[:, :, :], cw[:, :, :], pick0[:, :, :], ALU.add).then_inc(cw_done, 1)
            for j, (t0, nt) in enumerate(HALVES):
                dve.wait_ge(cwT_done, j + 1)
                nc.vector.tensor_copy(cwT[:, t0 * P:(t0 + nt) * P], PS[6 + j][0:E0, 0:nt * P]).then_inc(cwT_kept, 1)
            for j, (t0, nt) in enumerate(HALVES):
                dve.wait_ge(b3_done, j + 1)
                nc.vector.tensor_copy(acc0[:, t0:t0 + nt, :].rearrange("p t d -> p (t d)"), PS[6 + j][:, 0:nt * P]).then_inc(b3_kept, 1)
            dve.wait_ge(b3_kept, 2)
            def keep_k2(b, c, psum):
                dve.wait_ge(k1_kept, b * KC + c + 1)
                cols = slice(c * 512, (c + 1) * 512)
                nc.vector.scalar_tensor_tensor(out=k12[:, 1, cols], in0=psum, scalar=bcol[:, 0:1], in1=k12[:, 0, cols].bitcast(F32),
                                               op0=ALU.add, op1=ALU.subtract).then_inc(k2_kept, 1)

            def keep_v(b, s, c, psum):
                dve.wait_ge(v_done, b * KC + c + 1)
                nc.vector.tensor_copy(V[s][:, 4 * c:4 * c + 4, 0:H * VH].rearrange("p t (h e) -> p t h e", e=VH)[:, :, :, 0:DH1],
                                      psum.rearrange("p (t h e) -> p t h e", t=4, e=DH1)).then_inc(v_kept, 1)

            for s in range(2 * E0):
                t0, nt = HALVES[s % 2]
                dve.wait_ge(l3_done, s + 1)
                if s >= 2:
                    dve.wait_ge(l3_kept, s - 1)
                for t in range(nt):
                    ins = nc.vector.scalar_tensor_tensor(out=acc0[:, t0 + t, :], in0=PS[4 + s % 2][:, t * P:(t + 1) * P],
                                                         scalar=cw[:, t0 + t, s // 2:s // 2 + 1], in1=acc0[:, t0 + t, :],
                                                         op0=ALU.mult, op1=ALU.add)
                ins.then_inc(l3_kept, 1)
                if 1 <= s <= SLOTS * 2 * KC:
                    b, piece = divmod(s - 1, 2 * KC)
                    if piece == KC:
                        dve.wait_ge(vones_done, 2 * b + 2)
                    if piece < KC:
                        keep_k2(b, piece, PS[7])
                    else:
                        keep_v(b, b, piece - KC, PS[7])
            dve.wait_ge(l3_kept, 2 * E0)
            residual(lambda j, t0, nt: acc0[:, t0:t0 + nt, :].rearrange("p t d -> p (t d)"), 1, 1)

            layernorm(2)
            nc.vector.memset(negm[:, :], 0.0).then_inc(const_done, 1)
            nc.vector.memset(negmT[:, :], 0.0).then_inc(pv_bank_free, 1)
            keep_xT(2)
            for m in range(2 * HG):
                g, j = divmod(m, 2)
                dve.wait_ge(q1_kept, m + 1)
                part = q96[GROWS:2 * GROWS, g, j * 448:(j + 1) * 448]
                nc.vector.scalar_tensor_tensor(out=part, in0=PS[m % 4][GROWS:2 * GROWS, 0:448], scalar=bq1[GROWS:2 * GROWS, g:g + 1],
                                               in1=part.bitcast(F32), op0=ALU.add, op1=ALU.subtract).then_inc(q2_kept, 1)

            def keep_max(b, m):
                c, pair = divmod(m, PAIRS)
                dve.wait_ge(m1_done, b * NM + m + 1)
                nc.vector.tensor_reduce(mx3[:, pair, c:c + 1], (PS[1], PS[2])[m % 2][0:PQ, :], AX, ALU.max).then_inc(m1_kept, 1)

            def turn_max(b):
                dve.wait_ge(m1_kept, (b + 1) * NM)
                nc.vector.tensor_reduce(negm[0:PQ, 0:PAIRS].bitcast(F32R), mx3[:, :, :], AX, ALU.max, negate=True).then_inc(negm_done, 1)
                dve.wait_ge(negm_done, b + 1)
                nc.vector.transpose(negmT[:, :], negm[:, :]).then_inc(negmT_done, 1)

            def keep_pv(b):
                dve.wait_ge(pv_done, (b + 1) * KT)
                nc.vector.tensor_copy(pv[:, bass.ds(b, 1), 0:168], PS[3][:, 0:168].unsqueeze(1))
                nc.vector.tensor_copy(pv[0:32, bass.ds(b, 1), 168:336], PS[3][0:32, 168:336].unsqueeze(1))
                nc.vector.tensor_copy(pv[32:64, bass.ds(b, 1), 168:168 + SQ], PS[3][32:64, 168:168 + SQ].unsqueeze(1)).then_inc(pv_bank_free, 1)

            for m in range(NM):
                keep_max(0, m)
            turn_max(0)
            for m in range(PAIRS):
                keep_max(1, m)

            def body1(i, last):
                for s in range(SLOTS):
                    b = i * SLOTS + s
                    final = last and s == 1
                    for t in range(KT):
                        for m in (2 * t, 2 * t + 1):
                            if t < KT - 4 and not final:
                                keep_max(b + 1, PAIRS + m)
                            if t >= KT - 4 and not last:
                                keep_max(b + SLOTS, m - 2 * (KT - 4))
                        if t == KT - 5 and not final:
                            turn_max(b + 1)
                        if not last:
                            if t in (2, 4, 6):
                                keep_k2(b + SLOTS, (t - 2) // 2, PS[0])
                            if t in (8, 10):
                                keep_v(b + SLOTS, s, (t - 8) // 2, PS[0])
                    keep_pv(b)
                    if not last:
                        keep_v(b + SLOTS, s, 2, PS[0])

            with dve.Fori(0, B // SLOTS - 1) as i:
                body1(i, False)
            body1(B // SLOTS - 1, True)

            dve.wait_ge(oT_loaded, 16 * H * 2)
            nc.vector.reciprocal(rden[:, :], den[:, :]).then_inc(rden_done, 1)
            for j in range(2):
                dve.wait_ge(spread_done, j + 1)
                half = oT[:, j * 448:(j + 1) * 448]
                link(nc.vector.tensor_tensor(half, half, PS[2 + j][:, 0:448], ALU.mult))
            nc.vector.tensor_scalar(oT[:, :], oT[:, :], bcol[:, 1:2], None, ALU.add).then_inc(oT_done, 1)
            dve.wait_ge(o_done, 4)
            residual(lambda j, t0, nt: PS[j][:, 0:nt * P], 2, 2)

            layernorm(3)
            keep_xT(3)
            dve.wait_ge(z_done, 1)
            link(nc.vector.tensor_copy(z[:, :, :].rearrange("p a e -> p (a e)"), PS[2][:, 0:NT * 3 * E1]))
            link(nc.vector.tensor_reduce(top2[:, :], z[:, :, :], AX, ALU.max))
            nc.vector.tensor_tensor(zl[:, :, :], z[:, :, :], bc(top2[:, :], E1), ALU.subtract).then_inc(zsub_done, 1)
            for k in range(TOPK1):
                first_largest(z[:, :, :], pk[:, :, :], top1[:, :], E1, order_1[:, :, :])
                if k == 0:
                    link(nc.vector.tensor_copy(sel[:, :, :], pk[:, :, :]))
                else:
                    link(nc.vector.tensor_tensor(sel[:, :, :], sel[:, :, :], pk[:, :, :], ALU.add))
                if k < TOPK1 - 1:
                    link(nc.vector.scalar_tensor_tensor(out=z[:, :, :], in0=pk[:, :, :], scalar=-BIG, in1=z[:, :, :], op0=ALU.mult, op1=ALU.add))
            dve.wait_ge(ez_done, 1)
            link(nc.vector.tensor_tensor(C[:, :, :], ez[:, :, :], sel[:, :, :], ALU.mult))
            link(nc.vector.tensor_reduce(top1[:, :], C[:, :, :], AX, ALU.add))
            link(nc.vector.reciprocal(top1[:, :], top1[:, :]))
            nc.vector.tensor_tensor(C[:, :, :], C[:, :, :], bc(top1[:, :], E1), ALU.mult).then_inc(C_done, 1)
            dve.wait_ge(C_done, 1)

            def mix(which, dst):
                for n in range(NT * 3):
                    t, e4 = divmod(n, 3)
                    m = which * NT * 3 + n
                    dve.wait_ge(mix_done, m + 1)
                    for e in range(4):
                        first = which == 0 and e4 == 0 and e == 0
                        coef = C[:, 3 * t + which, 4 * e4 + e:4 * e4 + e + 1]
                        src = PS[4 + m % 4][:, e * D:(e + 1) * D]
                        if first:
                            ins = nc.vector.tensor_scalar(dst[:, t, :], src, coef, None, ALU.mult)
                        else:
                            ins = nc.vector.scalar_tensor_tensor(out=dst[:, t, :], in0=src, scalar=coef, in1=dst[:, t, :], op0=ALU.mult, op1=ALU.add)
                        if e < 3:
                            link(ins)
                    ins.then_inc(mix_kept, 1)
                    dve.wait_ge(mix_kept, m + 1)

            mix(0, y1)
            dve.wait_ge(fb_kept, 2)
            mix(1, y2)
            residual(lambda j, t0, nt: y2[:, t0:t0 + nt, :].rearrange("p t d -> p (t d)"), 3, 3)


def kernel(**inputs):
    import numpy as np
    import concourse.bacc as bacc
    from concourse.bass_utils import run_bass_kernel_spmd

    v = {k: np.asarray(t) for k, t in inputs.items()}
    ctx = v["ctx_1024"]
    ctxT = np.zeros((B, P, SKP), ctx.dtype)
    ctxT[:, :, :SK] = ctx.transpose(0, 2, 1)
    ctxn = np.zeros((B, KPQ * SQ, D), ctx.dtype)
    ctxn[:, :SK] = ctx
    ctxn = ctxn.reshape(B, KPQ, 2 * NG, 4, D).transpose(0, 3, 1, 2, 4).reshape(B, CK, 2 * NG, D)
    pick = np.zeros((QG, QG, H), np.float32)
    block = np.full((QG, 3, QG, KPQ), -BIG, np.float32)
    for i in range(QG):
        pick[i, i] = 1
        for kind, whole in enumerate((QG, LASTQ % QG, 0)):
            block[i, kind, i, :KPQ - (i >= whole)] = 0

    def heads(w, transposed):
        w = w.T if transposed else w
        return w.reshape(H, DH0, D).transpose(1, 0, 2)

    wkv0, wkv1 = v["L0_xattn_Wkv"], v["L1_xattn_Wkv"]
    inner = H * DH0
    arrays = {
        "x": v["x"].reshape(NT, P, D).transpose(1, 0, 2),
        "ident": np.eye(P, dtype=np.float32),
        "wq0": heads(v["L0_xattn_Wq"], True),
        "wk0": heads(wkv0[:, :inner], True),
        "wv0": heads(wkv0[:, inner:], True),
        "wo0": heads(v["L0_xattn_Wout"], False),
        "ctxT": ctxT,
        "ctxn": ctxn,
        "pick": pick.reshape(QG, P),
        "block": block.reshape(QG, 3, GK),
        "rows": np.concatenate([v["L0_xattn_bout"], v["L1_xattn_bout"], v["L0_ffn_gate_b"]])[None],
        "gates": np.broadcast_to(np.stack([v["g_xattn"][0], v["g_ffn"][0], v["g_xattn"][1], v["g_ffn"][1]])[None], (P, 4)),
        "wq1": np.tile(v["L1_xattn_Wq"].reshape(D, HG, 1, GROWS), (1, 1, 3, 1)).reshape(D, HG, MASK_ROW),
        "bq1": np.tile(v["L1_xattn_bq"].reshape(HG, GROWS).T, (3, 1)),
        "own_head": np.tile(np.repeat(np.eye(GH, dtype=np.float32), DH1, axis=0), (3, 1)),
        "wk1": wkv1[:, :D],
        "wv1": wkv1[:, D:],
        "wo1": v["L1_xattn_Wout"],
        "bcol": np.stack([v["L1_xattn_bkv"][:D], v["L1_xattn_bkv"][D:]], 1),
        "spread": np.repeat(np.eye(H, dtype=np.float32), DH1, axis=1),
        "mask": v["mask_BxS2_bf0"],
        "w1": v["L0_ffn_w1"].transpose(1, 0, 2),
        "w2": v["L0_ffn_w2"].transpose(1, 0, 2),
        "w3": v["L0_ffn_w3"].transpose(1, 0, 2),
        "gwT": v["L0_ffn_gate_w"].T,
        "b12": np.stack([v["L0_ffn_b1"].T, v["L0_ffn_b2"].T], 1),
        "b3": v["L0_ffn_b3"],
        "f1": v["L1_ffn_W1"].transpose(2, 0, 1),
        "f2": v["L1_ffn_W2"].transpose(2, 0, 1),
        "pwT": v["L1_ffn_P_w"].T,
        "uT": np.concatenate([v["L1_ffn_U1"], v["L1_ffn_U2"], v["L1_ffn_U3"]]).T,
        "fb2": v["L1_ffn_b2"],
    }
    arrays = {k: np.ascontiguousarray(t) for k, t in arrays.items()}
    nc = bacc.Bacc("TRN2", target_bir_lowering=False, num_devices=1)
    aps = {k: nc.dram_tensor(f"in_{k}", t.shape, mybir.dt.from_np(t.dtype), kind="ExternalInput").ap()
           for k, t in arrays.items()}
    out = nc.dram_tensor("out", (TOK, D), F32, kind="ExternalOutput").ap()
    build(nc, aps, out.rearrange("(n p) d -> p n d", p=P))
    got = run_bass_kernel_spmd(nc, [{f"in_{k}": t for k, t in arrays.items()}], core_ids=[0])
    return got.results[0]["out"].reshape(B, SQ, D)
```

```python
from contextlib import ExitStack

import concourse.bass as bass
from concourse import mybir

F32 = mybir.dt.float32
F32R = mybir.dt.float32r
BF16 = mybir.dt.bfloat16
U8 = mybir.dt.uint8
ALU = mybir.AluOpType
ACT = mybir.ActivationFunctionType
AX = mybir.AxisListType.X

P = 128
B, SQ, SK, D = 16, 56, 1500, 128
TOK = B * SQ
NT = TOK // P
HALVES = ((0, 4), (4, 3))
H = 16
DH0 = 64
DH1 = D // H
EPS = 1e-5
BIG = 1e30

KPQ = -(-SK // SQ)
LASTQ = SK - (KPQ - 1) * SQ
QG = 8
NG = SQ // QG
GK = QG * KPQ
CK = GK // 2
UNITS = ((0, 2), (2, 2), (4, 2), (6, 1))
NU = len(UNITS)
SLOTS = 2
AHEAD = 4

KT = 12
SKP = KT * P
HG = 4
GH = H // HG
GROWS = GH * DH1
MASK_ROW = 3 * GROWS
MAX_ROW = MASK_ROW + 1
QCOLS = GH * SQ
PAIRS = H // 2
PQ = 2 * SQ
KC = 3
VH = DH1 + 1
VW = 160
PGROUPS = ((0, 3, 0, 0), (3, 3, 32, 0), (6, 3, 64, 0), (9, 3, 96, 0), (12, 2, 0, 3 * SQ), (14, 2, 32, 3 * SQ))
PBLOCKS = 5
PROWS = (P, P, P, 64, 64)
SCALE1 = float(DH1) ** -0.5

E0, E1 = 8, 12
TOPK1 = 3
PADDR = 64
MIX_TILES = ((0, 1), (2, 3), (4, 5, 6))
ON_DVE = 8
MIX = [(t, e4) for tiles in MIX_TILES for e4 in (2, 0, 1) for t in tiles]


def raw(ap):
    return ap.bitcast(F32)


def build(nc, a, out):
    ctx = ExitStack()
    with ctx:
        def sem(name):
            return ctx.enter_context(nc.semaphore(name))

        def sb(name, shape, dt=F32, scope=ctx):
            return scope.enter_context(nc.sbuf_tensor(name, shape, dt))

        bank = [ctx.enter_context(nc.psum_tensor(f"bank{i}", [P, 512], F32)) for i in range(4)]
        wide = [ctx.enter_context(nc.psum_tensor(f"wide{i}", [P, 2, 512], F32)) for i in range(2)]
        PS = [bank[0][:, :], bank[1][:, :], bank[2][:, :], bank[3][:, :],
              wide[0][:, 0, :], wide[0][:, 1, :], wide[1][:, 0, :], wide[1][:, 1, :]]

        x = sb("x", [P, NT, D])
        xn = sb("xn", [P, NT, D])
        xT = sb("xT", [P, TOK])
        ident = sb("ident", [P, P])
        gates = sb("gates", [P, 4])
        tg = sb("tg", [P, 4])
        eps = sb("eps", [P, 1])
        ones_row = sb("ones_row", [1, P])
        stats = sb("stats", [P, NT, 6])
        mv = sb("mv", [P, NT, 2])
        sd = sb("sd", [P, NT])
        rstd = sb("rstd", [P, NT])
        ctxT = [sb(f"ctxT{s}", [P, SKP]) for s in range(SLOTS)]
        rows = sb("rows", [1, 2 * D + E0])
        wq1 = sb("wq1", [P, HG, MASK_ROW])
        wk1 = sb("wk1", [P, D])
        wv1 = sb("wv1", [P, D])
        wo1 = sb("wo1", [P, D])
        pick_out = sb("pick_out", [P, 2, PBLOCKS, P])
        rden = sb("rden", [P, TOK])
        oT = sb("oT", [P, TOK])
        bcol = sb("bcol", [P, 2])
        bq1 = sb("bq1", [MASK_ROW, HG])
        own_head = sb("own_head", [MASK_ROW, GH])
        q96 = sb("q96", [MASK_ROW, HG, TOK], F32R)
        qs = [sb(f"qs{s}", [P, HG, GH, SQ], F32R) for s in range(SLOTS)]
        qm = [sb(f"qm{s}", [P, HG, GH, SQ], F32R) for s in range(SLOTS)]
        order_0 = sb("order_0", [P, NT, E0])
        order_1 = sb("order_1", [P, NT * 3, E1])

        one = ExitStack()
        qk = sb("qk", [P, TOK * H], scope=one)
        G = sb("G", [P, H, D], scope=one)
        M = sb("M", [P, H, D], scope=one)
        pick_f = sb("pick_f", [QG, P], scope=one)
        pick = sb("pick", [QG, P], BF16, scope=one)
        block_f = sb("block_f", [QG, 3, GK], scope=one)
        blockm = sb("blockm", [QG, 3, GK], BF16, scope=one)
        w1 = sb("w1", [P, E0, D], scope=one)
        w2 = sb("w2", [P, E0, D], scope=one)
        w3 = sb("w3", [P, E0, D], scope=one)
        gwT = sb("gwT", [P, E0], scope=one)
        b12 = sb("b12", [P, 2, E0], scope=one)
        b3 = sb("b3", [E0, D], scope=one)
        attn = ExitStack()
        ctxn = [sb(f"ctxn{s}", [CK, 2 * NG, D], scope=attn) for s in range(SLOTS)]
        qslot = [sb(f"qslot{s}", [P, SQ * H], scope=attn) for s in range(SLOTS)]
        p0 = [sb(f"p0_{s}", [P, 2, GK], scope=attn) for s in range(SLOTS)]
        own = [sb(f"own_{s}", [P, 2, CK], scope=attn) for s in range(SLOTS)]
        p0T = [sb(f"p0T_{s}", [CK, 2, 2, P], scope=attn) for s in range(SLOTS)]
        nmax0 = sb("nmax0", [P, SLOTS, 2], scope=attn)
        psum0 = sb("psum0", [P, SLOTS, 2], scope=attn)
        rsum0 = sb("rsum0", [P, SLOTS, 2], scope=attn)
        attn.close()
        moe = ExitStack()
        h1 = [sb(f"h1_{s}", [P, 512], scope=moe) for s in range(2)]
        h2 = [sb(f"h2_{s}", [P, 512], scope=moe) for s in range(2)]
        acc0 = sb("acc0", [P, NT, D], scope=moe)
        probs = sb("probs", [P, NT, E0], scope=moe)
        left = sb("left", [P, NT, E0], scope=moe)
        pick0 = sb("pick0", [P, NT, E0], scope=moe)
        cw = sb("cw", [P, NT, E0], scope=moe)
        top0 = sb("top0", [P, NT], scope=moe)
        cwT = sb("cwT", [E0, TOK], scope=moe)
        moe.close()
        one.close()
        early = ExitStack()
        wq0 = sb("wq0", [DH0, H, D], scope=early)
        wk0 = sb("wk0", [DH0, H, D], scope=early)
        wv0 = sb("wv0", [DH0, H, D], scope=early)
        wo0 = sb("wo0", [DH0, H, D], scope=early)
        mask8 = sb("mask8", [B, SK], U8, scope=early)
        maskr = sb("maskr", [B, SKP], F32R, scope=early)
        early.close()

        two = ExitStack()
        kstack = [sb(f"kstack{s}", [P, HG, SKP], F32R, scope=two) for s in range(SLOTS)]
        k12 = sb("k12", [P, 2, SKP], F32R, scope=two)
        V = [sb(f"V{s}", [P, KT, VW], scope=two) for s in range(SLOTS)]
        p1 = [sb(f"p1_{s}", [P, 2, 2 * QCOLS], scope=two) for s in range(3)]
        mx3 = sb("mx3", [PQ, PAIRS, KC], scope=two)
        negm = sb("negm", [P, 32], scope=two)
        negmT = sb("negmT", [P, 32], scope=two)
        pv = sb("pv", [P, PBLOCKS, TOK], scope=two)
        two.close()

        four = ExitStack()
        f1 = sb("f1", [P, E1, D], scope=four)
        f2 = sb("f2", [P, E1, D], scope=four)
        pwT = sb("pwT", [P, PADDR], scope=four)
        uT = sb("uT", [PADDR, 3 * E1], scope=four)
        fb2 = sb("fb2", [E1, D], scope=four)
        xaT = sb("xaT", [PADDR, TOK], scope=four)
        z = sb("z", [P, NT * 3, E1], scope=four)
        zl = sb("zl", [P, NT * 3, E1], scope=four)
        ez = sb("ez", [P, NT * 3, E1], scope=four)
        sel = sb("sel", [P, NT * 3, E1], scope=four)
        pk = sb("pk", [P, NT * 3, E1], scope=four)
        C = sb("C", [P, NT * 3, E1], scope=four)
        top1 = sb("top1", [P, NT * 3], scope=four)
        top2 = sb("top2", [P, NT * 3], scope=four)
        c3T = sb("c3T", [E1, TOK], scope=four)
        rest = sb("rest", [P, NT, E1 - ON_DVE, D], scope=four)
        y1 = sb("y1", [P, NT, D], scope=four)
        hg = sb("hg", [P, NT, D], scope=four)
        hT = sb("hT", [P, TOK], scope=four)
        y2 = sb("y2", [P, NT, D], scope=four)
        four.close()

        x_loaded = sem("x_loaded")
        qk_loaded, vo_loaded = sem("qk_loaded"), sem("vo_loaded")
        small_loaded = sem("small_loaded")
        ffn0_loaded = sem("ffn0_loaded")
        ffn1_loaded = sem("ffn1_loaded")
        ctxT_loaded = [sem(f"ctxT_loaded{s}") for s in range(SLOTS)]
        ctxn_loaded = [sem(f"ctxn_loaded{s}") for s in range(SLOTS)]
        v_step = sem("v_step")
        pool_done = sem("pool_done")
        const_done = sem("const_done")
        var_done = sem("var_done")
        sd_done = sem("sd_done")
        xn_done = sem("xn_done")
        xnT_done = sem("xnT_done")
        xT_done = sem("xT_done")
        g_done, g_kept = sem("g_done"), sem("g_kept")
        m_done, m_kept = sem("m_done"), sem("m_kept")
        qk_done = sem("qk_done")
        qk_kept = [sem("qk_kept_even_heads"), sem("qk_kept_odd_heads")]
        qslot_done = sem("qslot_done")
        s0_done, max0_done, exp0_done, norm0_done = sem("s0_done"), sem("max0_done"), sem("exp0_done"), sem("norm0_done")
        recip0_done, order_done = sem("recip0_done"), sem("order_done")
        p0T_done, p0T_kept = sem("p0T_done"), sem("p0T_kept")
        ac_done, ac_bank_free = sem("ac_done"), sem("ac_bank_free")
        o_done = sem("o_done")
        x_new = sem("x_new")
        gate_done, gate_sub, gate_exp = sem("gate_done"), sem("gate_sub"), sem("gate_exp")
        cw_done, cwT_done, cwT_kept = sem("cw_done"), sem("cwT_done"), sem("cwT_kept")
        b3_done, b3_kept = sem("b3_done"), sem("b3_kept")
        l1_done, l1_kept = sem("l1_done"), sem("l1_kept")
        l2_done, l2_kept = sem("l2_done"), sem("l2_kept")
        l3_done, l3_kept = sem("l3_done"), sem("l3_kept")
        k12_stored = [sem(f"k12_stored{c}") for c in range(KC)]
        q_done, q1_kept, q2_kept = sem("q_done"), sem("q1_kept"), sem("q2_kept")
        mask_loaded, maskr_done, mask_stored = sem("mask_loaded"), sem("maskr_done"), sem("mask_stored")
        k_done, k1_kept, k2_kept = sem("k_done"), sem("k1_kept"), sem("k2_kept")
        v_done, v_kept = sem("v_done"), sem("v_kept")
        kst_loaded = [[sem(f"kst_loaded{s}_{c}") for c in range(KC)] for s in range(SLOTS)]
        qs_done, qm_done = sem("qs_done"), sem("qm_done")
        kones_done, vones_done = sem("kones_done"), sem("vones_done")
        m1_done, m1_kept = sem("m1_done"), sem("m1_kept")
        negm_done, negmT_done = sem("negm_done"), sem("negmT_done")
        c_loaded = [sem(f"c_loaded{s}") for s in range(SLOTS)]
        st_done, exp1_done = sem("st_done"), sem("exp1_done")
        pv_done, pv_bank_free = sem("pv_done"), sem("pv_bank_free")
        sums_done, rden_done, heads_done, oT_done = sem("sums_done"), sem("rden_done"), sem("heads_done"), sem("oT_done")
        xa_done, xa_kept = sem("xa_done"), sem("xa_kept")
        z_done, zsub_done, ez_done = sem("z_done"), sem("zsub_done"), sem("ez_done")
        C_done, c3T_done, c3T_kept = sem("C_done"), sem("c3T_done"), sem("c3T_kept")
        fb_done, fb_kept = sem("fb_done"), sem("fb_kept")
        mix_done, mix_added, mix_scaled = sem("mix_done"), sem("mix_added"), sem("mix_scaled")
        rest_pair, rest_done, y_done = sem("rest_pair"), sem("rest_done"), sem("y_done")
        hg_done, hT_done, hT_kept = sem("hg_done"), sem("hT_done"), sem("hT_kept")
        out_done = sem("out_done")

        NUNITS = B * NU
        NTILES = B * KT
        NM = PAIRS * KC
        KDMA = 4

        MIXB = (PS[4], PS[5], PS[6], PS[7], PS[2], PS[3])

        def last_add(m):
            which, n = divmod(m, len(MIX))
            t, e4 = MIX[n]
            tiles = next(tiles for tiles in MIX_TILES if t in tiles)
            return (which * NT + tiles[0]) * ON_DVE + (4 * e4 + 3) * len(tiles) + tiles.index(t) + 1

        def last_weighed(which, t):
            return (which * NT + t + 1) * (E1 - ON_DVE)

        mask_rows = nc.dram_tensor("mask_rows", (B, SKP), F32).ap()
        k12_rows = nc.dram_tensor("k12_rows", (B, P, 2, SKP), F32).ap()

        MB, MB3 = (PS[1], PS[2]), (PS[1], PS[2], PS[0])

        block = ctx.enter_context(nc.Block())

        @block.sync
        def _(sp):
            for name, t in (("wq0", wq0), ("wk0", wk0)):
                sp.dma_start(t[:, :, :], a[name]).then_inc(qk_loaded, 16)
            sp.dma_start(x[:, :, :], a["x"]).then_inc(x_loaded, 16)
            for name, t in (("wv0", wv0), ("wo0", wo0)):
                sp.dma_start(t[:, :, :], a[name]).then_inc(vo_loaded, 16)
            sp.dma_start(ident[:, :], a["ident"]).then_inc(x_loaded, 16)
            sp.dma_start(mask8[:, :], a["mask"]).then_inc(mask_loaded, 16)
            for s in range(SLOTS):
                sp.dma_start(ctxT[s][:, :], a["ctxT"][s]).then_inc(ctxT_loaded[s], 16)
                sp.dma_start(ctxn[s][:, :, :], a["ctxn"][s]).then_inc(ctxn_loaded[s], 16)
            for name, t in (("pick", pick_f[:, :]), ("block", block_f[:, :, :]), ("rows", rows[:, :]),
                            ("gates", gates[:, :]), ("wq1", wq1[:, :, :]), ("bq1", bq1[:, :]), ("own_head", own_head[:, :]), ("wk1", wk1[:, :]), ("wv1", wv1[:, :]),
                            ("wo1", wo1[:, :]), ("bcol", bcol[:, :]), ("pick_out", pick_out[:, :, :, :])):
                sp.dma_start(t, a[name]).then_inc(small_loaded, 16)
            sp.wait_ge(maskr_done, 1)
            sp.dma_start(mask_rows, raw(maskr[:, :])).then_inc(mask_stored, 16)
            for name, t in (("w1", w1[:, :, :]), ("w2", w2[:, :, :]), ("w3", w3[:, :, :]), ("gwT", gwT[:, :]),
                            ("b12", b12[:, :, :]), ("b3", b3[:, :])):
                sp.dma_start(t, a[name]).then_inc(ffn0_loaded, 16)

            with sp.Fori(0, B // SLOTS - 1) as i:
                for s in range(SLOTS):
                    b = i * SLOTS + s
                    sp.wait_ge(s0_done, (b + 1) * NU)
                    sp.dma_start(ctxT[s][:, :], a["ctxT"][bass.ds(b + SLOTS, 1)].rearrange("o p n -> (o p) n")).then_inc(ctxT_loaded[s], 16)
                    sp.wait_ge(ac_done, (b + 1) * NU)
                    sp.dma_start(ctxn[s][:, :, :], a["ctxn"][bass.ds(b + SLOTS, 1)].rearrange("o p c d -> (o p) c d")).then_inc(ctxn_loaded[s], 16)
            for s in range(SLOTS):
                sp.wait_ge(s0_done, (B - SLOTS + s + 1) * NU)
                sp.dma_start(ctxT[s][:, :], a["ctxT"][s]).then_inc(ctxT_loaded[s], 16)

            def stack_keys(b, s, c):
                cols = slice(c * 512, (c + 1) * 512)
                sp.dma_start(raw(kstack[s][MASK_ROW:MASK_ROW + 1, :, cols]),
                             mask_rows[bass.ds(b, 1), cols].unsqueeze(1).to_broadcast([1, HG, 512])).then_inc(kst_loaded[s][c], 16)
                sp.wait_ge(k12_stored[c], (b + 1) * 16)
                for part, src in enumerate((0, 0, 1)):
                    sp.dma_start(raw(kstack[s][part * GROWS:(part + 1) * GROWS, :, cols]),
                                 k12_rows[bass.ds(b, 1), :, src, cols].rearrange("o (g r) n -> r (o g) n", r=GROWS)).then_inc(kst_loaded[s][c], 16)

            def load_max(b, s):
                sp.wait_ge(negmT_done, b + 1)
                dst = qs[s][MAX_ROW:MAX_ROW + 1, :, :, :].rearrange("o g (k h) q -> o (g k) (h q)", k=2)
                for r in range(4):
                    n = min(32, PQ - 32 * r)
                    sp.dma_start(raw(dst[:, :, 32 * r:32 * r + n]), negmT[32 * r:32 * r + PAIRS, 0:n]).then_inc(c_loaded[s], 16)

            sp.wait_ge(mask_stored, 16)
            for s in range(SLOTS):
                sp.wait_ge(kones_done, s + 1)
                for c in range(KC):
                    stack_keys(s, s, c)
            sp.wait_ge(v_done, KC)
            sp.dma_start(ctxT[0][:, :], a["ctxT"][SLOTS]).then_inc(ctxT_loaded[0], 16)

            load_max(0, 0)

            def sample(i, s, last):
                b = i * SLOTS + s
                if not (last or (s == 1 and type(b) is int)):
                    sp.wait_ge(v_done, (b + 2) * KC)
                    sp.dma_start(ctxT[1 - s][:, :], a["ctxT"][bass.ds(b + 3, 1)].rearrange("o p n -> (o p) n")).then_inc(ctxT_loaded[1 - s], 16)
                for c in range(KC):
                    if c == 1 and not (last and s == 1):
                        load_max(b + 1, 1 - s)
                    if not last:
                        sp.wait_ge(st_done, b * KT + 4 * (c + 1))
                        stack_keys(b + SLOTS, s, c)

            with sp.Fori(0, B // SLOTS - 2) as i:
                for s in range(SLOTS):
                    sample(i, s, False)
            for s in range(SLOTS):
                sample(B // SLOTS - 2, s, False)
            for s in range(SLOTS):
                sample(B // SLOTS - 1, s, True)

            sp.wait_ge(st_done, NTILES - KT)
            for name, t in (("f1", f1[:, :, :]), ("f2", f2[:, :, :]), ("pwT", pwT[:, :]), ("uT", uT[:, :]), ("fb2", fb2[:, :])):
                sp.dma_start(t, a[name]).then_inc(ffn1_loaded, 16)
            for n, tiles in enumerate(MIX_TILES):
                sp.wait_ge(x_new, 3 * 2 + n + 1)
                sp.dma_start(out[:, tiles[0]:tiles[-1] + 1, :], x[:, tiles[0]:tiles[-1] + 1, :]).then_inc(out_done, 16)
            sp.wait_ge(out_done, 16 * len(MIX_TILES))

        def keep_v(copy, engine, b, s, c, psum):
            engine.wait_ge(v_done, b * KC + c + 1)
            copy(V[s][:, 4 * c:4 * c + 4, 0:H * VH].rearrange("p t (h e) -> p t h e", e=VH)[:, :, :, 0:DH1],
                 psum.rearrange("p (t h e) -> p t h e", t=4, e=DH1)).then_inc(v_kept, 1)

        @block.gpsimd
        def _(pool):
            for s in range(SLOTS):
                for m, buf in enumerate((qs[s], qm[s])):
                    nc.gpsimd.memset(buf[MASK_ROW:P, :, :, :].bitcast(F32), 0.0).then_inc(pool_done, 1)
                    pool.wait_ge(pool_done, 4 * s + 2 * m + 1)
                    nc.gpsimd.memset(buf[MASK_ROW:MASK_ROW + 1, :, :, :].bitcast(F32), 1.0).then_inc(pool_done, 1)
            for s in range(SLOTS):
                pool.wait_ge(pool_done, 4 * SLOTS + s)
                nc.gpsimd.memset(p0T[s][:, :, :, :], 0.0).then_inc(pool_done, 1)
            pool.wait_ge(pool_done, 5 * SLOTS)
            nc.gpsimd.iota(order_0[:, :, :], [[0, NT], [-1, E0]], base=E0, channel_multiplier=0,
                           allow_small_or_imprecise_dtypes=True).then_inc(order_done, 1)
            nc.gpsimd.iota(order_1[:, :, :], [[0, NT * 3], [-1, E1]], base=E1, channel_multiplier=0,
                           allow_small_or_imprecise_dtypes=True).then_inc(order_done, 1)

            for e in range(2):
                pool.wait_ge(qk_kept[e], H // 2)
            for s in range(SLOTS):
                nc.gpsimd.tensor_copy(qslot[s][:, :], qk[:, s * SQ * H:(s + 1) * SQ * H]).then_inc(qslot_done, 1)
            for e in range(2):
                pool.wait_ge(qk_kept[e], H)
            with pool.Fori(0, B // SLOTS - 1) as i:
                for s in range(SLOTS):
                    b = i * SLOTS + s
                    pool.wait_ge(s0_done, (b + 1) * NU)
                    nc.gpsimd.tensor_copy(qslot[s][:, :], qk[:, bass.ds((b + SLOTS) * (SQ * H), SQ * H)]).then_inc(qslot_done, 1)

            def store_keys(b, c):
                cols = slice(c * 512, (c + 1) * 512)
                pool.wait_ge(k2_kept, b * KC + c + 1)
                pool.dma_start(k12_rows[bass.ds(b, 1), :, :, cols].rearrange("o p k n -> (o p) k n"),
                               raw(k12[:, :, cols])).then_inc(k12_stored[c], 16)

            pool.wait_ge(x_new, 2)
            for s in range(SLOTS):
                nc.gpsimd.memset(kstack[s][MASK_ROW:P, :, :].bitcast(F32), 1.0).then_inc(kones_done, 1)
                pool.wait_ge(kones_done, s + 1)
                nc.gpsimd.memset(V[s][:, :, 0:H * VH].rearrange("p t (h e) -> p t h e", e=VH)[:, :, :, DH1:VH], 1.0).then_inc(vones_done, 1)
                pool.wait_ge(vones_done, 2 * s + 1)
                nc.gpsimd.memset(V[s][:, :, H * VH:VW], 1.0).then_inc(vones_done, 1)
                pool.wait_ge(vones_done, 2 * s + 2)
            for b in range(SLOTS):
                for c in range(KC):
                    store_keys(b, c)

            def expand(dst, b, signal):
                src = q96[:, :, bass.ds(b * SQ, SQ)].bitcast(F32)
                nc.gpsimd.tensor_tensor(dst[0:MASK_ROW, :, :, :], src.unsqueeze(2).to_broadcast([MASK_ROW, HG, GH, SQ]),
                                        own_head[:, :].unsqueeze(1).unsqueeze(3).to_broadcast([MASK_ROW, HG, GH, SQ]),
                                        ALU.mult).then_inc(signal, 1)

            pool.wait_ge(small_loaded, 192)
            pool.wait_ge(q1_kept, HG)
            pool.wait_ge(q2_kept, HG)
            expand(qm[0], 0, qm_done)
            expand(qs[0], 0, qs_done)
            expand(qm[1], 1, qm_done)
            pool.wait_ge(q1_kept, 2 * HG)
            pool.wait_ge(q2_kept, 2 * HG)
            with pool.Fori(0, B // SLOTS - 1) as i:
                for s in range(SLOTS):
                    b = i * SLOTS + s
                    store_keys(b + SLOTS, 0)
                    expand(qs[1 - s], b + 1, qs_done)
                    expand(qm[s], b + SLOTS, qm_done)
                    for c in range(1, KC):
                        store_keys(b + SLOTS, c)
            pool.wait_ge(st_done, (B - SLOTS) * KT)
            expand(qs[1], B - 1, qs_done)

            for n in range(2 * len(MIX_TILES)):
                tiles = MIX_TILES[n % 3]
                part = slice(tiles[0], tiles[-1] + 1)
                pool.wait_ge(mix_scaled, last_weighed(n // 3, tiles[-1]))
                nc.gpsimd.tensor_tensor(rest[:, part, 0:2, :], rest[:, part, 0:2, :], rest[:, part, 2:4, :], ALU.add).then_inc(rest_pair, 1)
                pool.wait_ge(rest_pair, n + 1)
                nc.gpsimd.tensor_tensor(rest[:, part, 0, :], rest[:, part, 0, :], rest[:, part, 1, :], ALU.add).then_inc(rest_done, 1)

        @block.tensor
        def _(pe):
            def transpose_x(n):
                for j, (t0, nt) in enumerate(HALVES):
                    pe.wait_ge(xn_done, 2 * n + j + 1)
                    for t in range(nt):
                        mm = pe.transpose(PS[4 + j][:, t * P:(t + 1) * P], xn[:, t0 + t, :], ident[:, :])
                    mm.then_inc(xnT_done, 1)

            def add_row(psum, row, n, stop=True):
                return pe.matmul(psum, ones_row[:, :], row, start=False, stop=stop)

            pe.wait_ge(qk_loaded, 32)
            for j in range(4):
                for h in range(4):
                    mm = pe.matmul(PS[j][:, h * D:(h + 1) * D], wq0[:, 4 * j + h, :], wk0[:, 4 * j + h, :], start=True, stop=True)
                mm.then_inc(g_done, 1)
            pe.wait_ge(vo_loaded, 32)
            for j in range(4):
                for h in range(4):
                    mm = pe.matmul(PS[4 + j][:, h * D:(h + 1) * D], wv0[:, 4 * j + h, :], wo0[:, 4 * j + h, :], start=True, stop=True)
                mm.then_inc(m_done, 1)
            pe.wait_ge(x_loaded, 32)
            pe.wait_ge(m_kept, 2)
            transpose_x(0)
            pe.wait_ge(g_kept, 4)
            pe.wait_ge(m_kept, 4)
            pe.wait_ge(xT_done, 2)
            for n in range(2 * H):
                half, h = divmod(n, H)
                if n >= 4:
                    pe.wait_ge(qk_kept[n % 2], n // 2 - 1)
                pe.matmul(PS[n % 4][:, 0:448], G[:, h, :], xT[:, half * 448:(half + 1) * 448], start=True, stop=True).then_inc(qk_done, 1)

            def scores0(par, u, s):
                first, cnt = UNITS[u]
                for g in range(cnt):
                    grp = first + g
                    i0 = grp * QG
                    kind = 0 if i0 + QG <= LASTQ else (1 if i0 < LASTQ else 2)
                    dst = PS[par][:, g * 256:g * 256 + GK]
                    keys = ctxT[s][:, 0:KPQ * SQ].rearrange("p (t i) -> p i t", i=SQ)[:, i0:i0 + QG, :]
                    pe.matmul(dst, qslot[s][:, i0 * H:(i0 + QG) * H], keys, start=True, stop=False)
                    mm = pe.matmul(dst, pick[:, :], blockm[:, kind, :], start=False, stop=True)
                mm.then_inc(s0_done, 1)

            def transposes0(u, par):
                first, cnt = UNITS[u]
                for g in range(cnt):
                    mm = pe.transpose(PS[2 + par][0:CK, g * P:(g + 1) * P], own[par][:, g, :], ident[:, :])
                mm.then_inc(p0T_done, 1)

            def values0(u, par, s):
                first, cnt = UNITS[u]
                for g in range(cnt):
                    for c in range(2):
                        mm = pe.matmul(PS[4 + 2 * par][:, g * P:(g + 1) * P], ctxn[s][:, 2 * (first + g) + c, :],
                                       p0T[par][:, g, c, :], start=(c == 0), stop=(c == 1))
                mm.then_inc(ac_done, 1)

            def next_sample(s, nxt):
                pe.wait_ge(ctxT_loaded[s], 16 * (nxt + 1))
                pe.wait_ge(qslot_done, nxt * SLOTS + s + 1)

            def body0(i, last):
                for k in range(SLOTS * NU):
                    n = i * (SLOTS * NU) + k
                    ahead, k1 = k + AHEAD, k + 1
                    if not (last and ahead >= SLOTS * NU):
                        s_, u_ = (ahead // NU) % SLOTS, ahead % NU
                        if u_ == 0:
                            next_sample(s_, i + ahead // (SLOTS * NU))
                        pe.wait_ge(exp0_done, n + 3)
                        scores0(ahead % 2, u_, s_)
                    if not (last and k1 >= SLOTS * NU):
                        pe.wait_ge(norm0_done, n + 2)
                        transposes0(k1 % NU, k1 % 2)
                    s0, u0 = k // NU, k % NU
                    if u0 == 0:
                        pe.wait_ge(ctxn_loaded[s0], 16 * (i + 1))
                    pe.wait_ge(p0T_kept, n + 1)
                    pe.wait_ge(ac_bank_free, n + 1)
                    values0(u0, k % 2, s0)

            pe.wait_ge(const_done, 1)
            pe.wait_ge(qk_kept[0], H)
            pe.wait_ge(qk_kept[1], H)
            next_sample(0, 0)
            scores0(0, 0, 0)
            scores0(1, 1, 0)
            pe.wait_ge(exp0_done, 1)
            scores0(0, 2, 0)
            pe.wait_ge(exp0_done, 2)
            scores0(1, 3, 0)
            pe.wait_ge(norm0_done, 1)
            transposes0(0, 0)
            with pe.Fori(0, B // SLOTS - 1) as i:
                body0(i, False)
            body0(B // SLOTS - 1, True)

            pe.wait_ge(ac_bank_free, NUNITS + 2)
            qk_v = qk[:, :].rearrange("p (t h) -> p h t", h=H)
            for j, (t0, nt) in enumerate(HALVES):
                for t in range(nt):
                    dst = PS[j][:, t * P:(t + 1) * P]
                    for h in range(H):
                        pe.matmul(dst, qk_v[:, h, (t0 + t) * P:(t0 + t + 1) * P], M[:, h, :], start=(h == 0), stop=False)
                    mm = add_row(dst, rows[:, 0:D], D)
                mm.then_inc(o_done, 1)

            transpose_x(1)
            pe.wait_ge(xT_done, 4)
            pe.wait_ge(ffn0_loaded, 96)
            for t in range(NT):
                pe.matmul(PS[6][:, t * E0:(t + 1) * E0], xT[:, t * P:(t + 1) * P], gwT[:, :], start=True, stop=False)
                mm = add_row(PS[6][:, t * E0:(t + 1) * E0], rows[:, 2 * D:2 * D + E0], E0)
            mm.then_inc(gate_done, 1)

            def width(s):
                return HALVES[s % 2][0] * P, HALVES[s % 2][1] * P

            def layer1(s):
                t0, w = width(s)
                if s >= 2:
                    pe.wait_ge(l1_kept, s - 1)
                pe.matmul(PS[s % 2][:, 0:w], w1[:, s // 2, :], xT[:, t0:t0 + w], start=True, stop=True).then_inc(l1_done, 1)

            def layer2(s):
                t0, w = width(s)
                pe.wait_ge(l1_kept, s + 1)
                if s >= 2:
                    pe.wait_ge(l2_kept, s - 1)
                pe.matmul(PS[2 + s % 2][:, 0:w], w2[:, s // 2, :], h1[s % 2][:, 0:w], start=True, stop=True).then_inc(l2_done, 1)

            def layer3(s):
                t0, w = width(s)
                pe.wait_ge(l2_kept, s + 1)
                if s >= 2:
                    pe.wait_ge(l3_kept, s - 1)
                for t in range(w // P):
                    mm = pe.matmul(PS[4 + s % 2][:, t * P:(t + 1) * P], h2[s % 2][:, t * P:(t + 1) * P], w3[:, s // 2, :], start=True, stop=True)
                mm.then_inc(l3_done, 1)

            def keys(b, s, c, psum):
                if c == 0:
                    if not (type(b) is int and b == 0):
                        pe.wait_ge(v_kept, b * KC)
                else:
                    pe.wait_ge(k2_kept, b * KC + c)
                pe.matmul(psum, wk1[:, :], ctxT[s][:, c * 512:(c + 1) * 512], start=True, stop=True).then_inc(k_done, 1)

            def values(b, s, c, psum):
                if c == 0:
                    pe.wait_ge(k2_kept, (b + 1) * KC)
                else:
                    pe.wait_ge(v_kept, b * KC + c)
                for t in range(4):
                    mm = pe.matmul(psum[:, t * P:(t + 1) * P], ctxT[s][:, (4 * c + t) * P:(4 * c + t + 1) * P], wv1[:, :], start=True, stop=True)
                mm.then_inc(v_done, 1)

            NS = 2 * E0
            pe.wait_ge(x_new, 2)
            layer1(0)
            layer1(1)
            layer2(0)
            pe.wait_ge(cw_done, 1)
            for j, (t0, nt) in enumerate(HALVES):
                for t in range(nt):
                    mm = pe.transpose(PS[6 + j][0:E0, t * P:(t + 1) * P], cw[:, t0 + t, :], ident[:, :])
                mm.then_inc(cwT_done, 1)
            pe.wait_ge(cwT_kept, 2)
            for j, (t0, nt) in enumerate(HALVES):
                for t in range(nt):
                    mm = pe.matmul(PS[6 + j][:, t * P:(t + 1) * P], cwT[:, (t0 + t) * P:(t0 + t + 1) * P], b3[:, :], start=True, stop=True)
                mm.then_inc(b3_done, 1)
            for s in range(NS):
                if s + 2 < NS:
                    layer1(s + 2)
                if s + 1 < NS:
                    layer2(s + 1)
                layer3(s)
                if s == 0:
                    pe.wait_ge(b3_kept, 2)
                    for b in range(SLOTS):
                        pe.wait_ge(ctxT_loaded[b], 16 * (B // SLOTS + 1))
                if 1 <= s <= SLOTS * 2 * KC:
                    b, piece = divmod(s - 1, 2 * KC)
                    (keys if piece < KC else values)(b, b, piece % KC, PS[7])

            transpose_x(2)
            pe.wait_ge(xT_done, 6)
            for m in range(2 * HG):
                j, g = divmod(m, HG)
                if m >= 4:
                    pe.wait_ge(q2_kept, m - 3)
                pe.matmul(PS[m % 4][0:MASK_ROW, 0:448], wq1[:, g, :], xT[:, j * 448:(j + 1) * 448], start=True, stop=True).then_inc(q_done, 1)
            pe.wait_ge(q2_kept, 2 * HG)

            PVB = PS[3]

            def maximum(b, s, n, m, first=None):
                c, pair = divmod(m, PAIRS)
                if m == 0:
                    pe.wait_ge(qm_done, b + 1)
                if pair == 0:
                    pe.wait_ge(kst_loaded[s][c], 16 * KDMA * (n + 1))
                if first is None:
                    psum = MB[m % 2]
                    pe.wait_ge(m1_kept, b * NM + (m - 1))
                else:
                    psum = MB3[first % 3]
                    if first >= 3:
                        pe.wait_ge(m1_kept, first - 2)
                q = qm[s][0:MAX_ROW, pair // 2, 2 * (pair % 2):2 * (pair % 2) + 2, :]
                pe.matmul(psum[0:PQ, :], q, kstack[s][0:MAX_ROW, pair // 2, c * 512:(c + 1) * 512],
                          start=True, stop=True).then_inc(m1_done, 1)

            def pick_rows(which, j, psum):
                t0, nt = HALVES[j]
                for c in range(PBLOCKS):
                    mm = pe.matmul(psum[:, 0:nt * P], pick_out[0:PROWS[c], which, c, :], pv[0:PROWS[c], c, t0 * P:(t0 + nt) * P],
                                   start=(c == 0), stop=(c == PBLOCKS - 1))
                return mm

            def scores1(s, t):
                for g in range(HG):
                    mm = pe.matmul(wide[t % 2][:, g // 2, (g % 2) * QCOLS:(g % 2 + 1) * QCOLS],
                                   kstack[s][:, g, t * P:(t + 1) * P], qs[s][:, g, :, :], start=True, stop=True)
                mm.then_inc(st_done, 1)

            def values1(s, t):
                p = p1[t % 3][:, :, :].rearrange("p a c -> p (a c)")
                for g, (head, cnt, row, col) in enumerate(PGROUPS):
                    mm = pe.matmul(PVB[row:row + 32, col:col + cnt * SQ], V[s][:, t, VH * head:VH * head + 32],
                                   p[:, head * SQ:(head + cnt) * SQ],
                                   start=(t == 0 and g < 4), stop=(t == KT - 1), skip_group_check=True)
                mm.then_inc(pv_done, 1)

            for m in range(NM):
                maximum(0, 0, 0, m, first=m)
            for m in range(PAIRS):
                maximum(1, 1, 0, m, first=NM + m)
            pe.wait_ge(v_kept, SLOTS * KC)
            pe.wait_ge(c_loaded[0], 64)
            pe.wait_ge(qs_done, 1)
            scores1(0, 0)
            scores1(0, 1)

            def body1(i, last):
                for s in range(SLOTS):
                    b = i * SLOTS + s
                    final = last and s == 1
                    for t in range(KT):
                        pe.wait_ge(exp1_done, b * KT + t + 1)
                        if t + 2 < KT:
                            scores1(s, t + 2)
                        elif t + 2 > KT and not final:
                            scores1(1 - s, t + 2 - KT)
                        for k in range(2):
                            if k == 1 and t == 0:
                                pe.wait_ge(v_kept, (b + 1) * KC)
                                pe.wait_ge(pv_bank_free, b + 1)
                            if k == 1:
                                values1(s, t)
                            if t < KT - 4 and not final:
                                maximum(b + 1, 1 - s, i + s, PAIRS + 2 * t + k)
                            if t >= KT - 4 and not last:
                                maximum(b + SLOTS, s, i + 1, 2 * t + k - 2 * (KT - 4))
                        if not last:
                            if t == 0:
                                pe.wait_ge(ctxT_loaded[s], 16 * (B // SLOTS + 2) + 16 * i)
                            if t in (1, 3, 5):
                                keys(b + SLOTS, s, (t - 1) // 2, PS[0])
                            if t in (7, 9, 10):
                                values(b + SLOTS, s, (7, 9, 10).index(t), PS[0])
                        if last and s == 0 and t + 2 == KT:
                            pe.wait_ge(v_kept, B * KC)
                            pick_rows(1, 0, PS[0]).then_inc(sums_done, 1)
                        if t + 2 == KT and not final:
                            pe.wait_ge(c_loaded[1 - s], 64 * (i + s + 1))
                            pe.wait_ge(qs_done, b + 2)
                            scores1(1 - s, 0)
                        if final and t == 1:
                            pe.wait_ge(rden_done, 1)
                            pick_rows(0, 0, PS[0]).then_inc(heads_done, 1)

            with pe.Fori(0, B // SLOTS - 1) as i:
                body1(i, False)
            body1(B // SLOTS - 1, True)

            pe.wait_ge(oT_done, 1)
            pe.wait_ge(pv_bank_free, B + 1)
            pick_rows(1, 1, PS[0]).then_inc(sums_done, 1)
            pick_rows(0, 1, PS[1]).then_inc(heads_done, 1)
            for j, (t0, nt) in enumerate(HALVES):
                pe.wait_ge(oT_done, j + 1)
                for t in range(nt):
                    dst = PS[2 + j][:, t * P:(t + 1) * P]
                    pe.matmul(dst, oT[:, (t0 + t) * P:(t0 + t + 1) * P], wo1[:, :], start=True, stop=False)
                    mm = add_row(dst, rows[:, D:2 * D], D)
                mm.then_inc(o_done, 1)

            transpose_x(3)
            pe.wait_ge(xT_done, 8)
            pe.wait_ge(ffn1_loaded, 80)
            pe.wait_ge(x_new, 6)
            for j in range(2):
                pe.matmul(PS[2 + j][0:PADDR, 0:448], pwT[:, :], xT[:, j * 448:(j + 1) * 448], start=True, stop=True).then_inc(xa_done, 1)
            pe.wait_ge(xa_kept, 2)
            for t in range(NT):
                mm = pe.matmul(PS[2][:, t * 3 * E1:(t + 1) * 3 * E1], xaT[:, t * P:(t + 1) * P], uT[:, :], start=True, stop=True)
            mm.then_inc(z_done, 1)

            def mixture(which, group, src, w):
                for n, (t, e4) in enumerate(MIX):
                    if t not in MIX_TILES[group]:
                        continue
                    m = which * len(MIX) + n
                    if m >= len(MIXB):
                        w_, n_ = divmod(m - len(MIXB), len(MIX))
                        if MIX[n_][1] == 2:
                            pe.wait_ge(mix_scaled, last_weighed(w_, MIX[n_][0]))
                        else:
                            pe.wait_ge(mix_added, last_add(m - len(MIXB)))
                    elif m == 4:
                        pe.wait_ge(zsub_done, 1)
                    pe.matmul(MIXB[m % len(MIXB)], src[:, t * P:(t + 1) * P],
                              w[:, 4 * e4:4 * e4 + 4, :].rearrange("p e d -> p (e d)"), start=True, stop=True).then_inc(mix_done, 1)

            def turn_hidden(group):
                tiles = MIX_TILES[group]
                pe.wait_ge(hg_done, group + 1)
                if group >= 2:
                    pe.wait_ge(hT_kept, group - 1)
                for i, t in enumerate(tiles):
                    mm = pe.transpose(PS[group % 2][:, i * P:(i + 1) * P], hg[:, t, :], ident[:, :])
                mm.then_inc(hT_done, 1)

            mixture(0, 0, xT, f1)
            pe.wait_ge(C_done, 1)
            for j, (t0, nt) in enumerate(HALVES):
                for t in range(nt):
                    mm = pe.transpose(PS[j][0:E1, t * P:(t + 1) * P], C[:, 3 * (t0 + t) + 2, :], ident[:, :])
                mm.then_inc(c3T_done, 1)
            mixture(0, 1, xT, f1)
            pe.wait_ge(c3T_kept, 2)
            for j, (t0, nt) in enumerate(HALVES):
                for t in range(nt):
                    mm = pe.matmul(PS[j][:, t * P:(t + 1) * P], c3T[:, (t0 + t) * P:(t0 + t + 1) * P], fb2[:, :], start=True, stop=True)
                mm.then_inc(fb_done, 1)
            mixture(0, 2, xT, f1)
            pe.wait_ge(fb_kept, 2)
            for group in range(len(MIX_TILES)):
                turn_hidden(group)
                pe.wait_ge(hT_kept, group + 1)
                mixture(1, group, hT, f2)

        @block.scalar
        def _(act):
            def norm_parts(n):
                for j, (t0, nt) in enumerate(HALVES):
                    act.wait_ge(var_done, 2 * n + j + 1)
                    nc.scalar.activation(sd[:, t0:t0 + nt], mv[:, t0:t0 + nt, 1], ACT.Sqrt, bias=eps[:, 0:1]).then_inc(sd_done, 1)
                act.wait_ge(xnT_done, 2 * n + 1)
                nc.scalar.copy(xT[:, 0:512], PS[4]).then_inc(xT_done, 1)

            for j in range(4):
                act.wait_ge(g_done, j + 1)
                nc.scalar.mul(G[:, 4 * j:4 * j + 4, :].rearrange("p h d -> p (h d)"), PS[j], DH0 ** -0.5).then_inc(g_kept, 1)
            norm_parts(0)
            act.wait_ge(small_loaded, 192)
            nc.scalar.activation(tg[:, 0:2], gates[:, 0:2], ACT.Tanh).then_inc(ac_bank_free, 1)
            nc.scalar.activation(tg[:, 2:4], gates[:, 2:4], ACT.Tanh).then_inc(ac_bank_free, 1)
            qk_t = qk[:, :].rearrange("p (t h) -> p h t", h=H)
            act.wait_ge(mask_stored, 16)
            for n in range(0, 2 * H, 2):
                half, h = divmod(n, H)
                act.wait_ge(qk_done, n + 1)
                nc.scalar.copy(qk_t[:, h, half * 448:(half + 1) * 448], PS[n % 4][:, 0:448]).then_inc(qk_kept[0], 1)

            def exp0(u, par, n):
                first, cnt = UNITS[u]
                act.wait_ge(max0_done, n + 1)
                for g in range(cnt):
                    ins = nc.scalar.activation(p0[par][:, g, :], PS[par][:, g * 256:g * 256 + GK], ACT.Exp,
                                               bias=nmax0[:, par, g:g + 1], accum_out=psum0[:, par, g:g + 1])
                ins.then_inc(exp0_done, 1)

            def body0(i, last):
                for k in range(SLOTS * NU):
                    n = i * (SLOTS * NU) + k
                    if not (last and k + AHEAD >= SLOTS * NU):
                        act.wait_ge(norm0_done, n + 3)
                        exp0((k + AHEAD) % NU, (k + AHEAD) % 2, n + AHEAD)
                    act.wait_ge(ac_done, n + 1)
                    first, cnt = UNITS[k % NU]
                    start = (i * SLOTS + k // NU) * (SQ * H) + first * P
                    nc.scalar.copy(qk[:, bass.ds(start, cnt * P)], PS[4 + 2 * (k % 2)][:, 0:cnt * P]).then_inc(ac_bank_free, 1)

            exp0(0, 0, 0)
            exp0(1, 1, 1)
            act.wait_ge(norm0_done, 1)
            exp0(2, 0, 2)
            act.wait_ge(norm0_done, 2)
            exp0(3, 1, 3)
            with act.Fori(0, B // SLOTS - 1) as i:
                body0(i, False)
            body0(B // SLOTS - 1, True)

            norm_parts(1)
            act.wait_ge(gate_sub, 1)
            nc.scalar.activation(left[:, :, :], probs[:, :, :], ACT.Exp).then_inc(gate_exp, 1)

            def relu1(s):
                w = HALVES[s % 2][1] * P
                act.wait_ge(l1_done, s + 1)
                if s >= 2:
                    act.wait_ge(l2_done, s - 1)
                nc.scalar.activation(h1[s % 2][:, 0:w], PS[s % 2][:, 0:w], ACT.Relu, bias=b12[:, 0, s // 2:s // 2 + 1]).then_inc(l1_kept, 1)

            def relu2(s):
                w = HALVES[s % 2][1] * P
                act.wait_ge(l2_done, s + 1)
                if s >= 2:
                    act.wait_ge(l3_done, s - 1)
                nc.scalar.activation(h2[s % 2][:, 0:w], PS[2 + s % 2][:, 0:w], ACT.Relu, bias=b12[:, 1, s // 2:s // 2 + 1]).then_inc(l2_kept, 1)

            def keep_k1(b, c, psum):
                act.wait_ge(k_done, b * KC + c + 1)
                if not (type(b) is int and b == 0):
                    act.wait_ge(k12_stored[c], b * 16)
                nc.scalar.activation(k12[:, 0, c * 512:(c + 1) * 512], psum, ACT.Identity, bias=bcol[:, 0:1]).then_inc(k1_kept, 1)

            NS = 2 * E0
            relu1(0)
            relu1(1)
            relu2(0)
            for s in range(NS):
                if s + 2 < NS:
                    relu1(s + 2)
                if s + 1 < NS:
                    relu2(s + 1)
                if 1 <= s <= SLOTS * 2 * KC and (s - 1) % (2 * KC) < KC:
                    keep_k1((s - 1) // (2 * KC), (s - 1) % (2 * KC), PS[7])

            norm_parts(2)
            for m in range(2 * HG):
                j, g = divmod(m, HG)
                act.wait_ge(q_done, m + 1)
                nc.scalar.activation(q96[:, g, j * 448:(j + 1) * 448], PS[m % 4][0:MASK_ROW, 0:448], ACT.Identity, bias=bq1[:, g:g + 1]).then_inc(q1_kept, 1)

            def body1(i, last):
                for s in range(SLOTS):
                    b = i * SLOTS + s
                    for t in range(KT):
                        act.wait_ge(st_done, b * KT + t + 1)
                        nc.scalar.activation(p1[t % 3][:, :, :], wide[t % 2][:, :, 0:2 * QCOLS], ACT.Exp, scale=SCALE1).then_inc(exp1_done, 1)
                        if not last and t in (3, 5, 7):
                            keep_k1(b + SLOTS, (t - 3) // 2, PS[0])
                        if not last and t in (9, 11):
                            keep_v(nc.scalar.copy, act, b + SLOTS, s, (t - 9) // 2, PS[0])

            with act.Fori(0, B // SLOTS - 1) as i:
                body1(i, False)
            body1(B // SLOTS - 1, True)

            norm_parts(3)
            for j in range(2):
                act.wait_ge(xa_done, j + 1)
                nc.scalar.copy(xaT[:, j * 448:(j + 1) * 448], PS[2 + j][0:PADDR, 0:448]).then_inc(xa_kept, 1)
            act.wait_ge(zsub_done, 1)
            nc.scalar.activation(ez[:, :, :], zl[:, :, :], ACT.Exp).then_inc(ez_done, 1)

            def weigh(which, group):
                for t in MIX_TILES[group]:
                    m = which * len(MIX) + MIX.index((t, 2))
                    act.wait_ge(mix_done, m + 1)
                    for e in range(ON_DVE, E1):
                        nc.scalar.activation(rest[:, t, e - ON_DVE, :], MIXB[m % len(MIXB)][:, (e - ON_DVE) * D:(e - ON_DVE + 1) * D],
                                             ACT.Copy, scale=C[:, 3 * t + which, e:e + 1]).then_inc(mix_scaled, 1)

            def gelu(group):
                act.wait_ge(y_done, group + 1)
                part = slice(MIX_TILES[group][0], MIX_TILES[group][-1] + 1)
                nc.scalar.activation(hg[:, part, :], y1[:, part, :], ACT.Gelu).then_inc(hg_done, 1)

            def keep_hT(group):
                tiles = MIX_TILES[group]
                act.wait_ge(hT_done, group + 1)
                nc.scalar.copy(hT[:, tiles[0] * P:(tiles[-1] + 1) * P], PS[group % 2][:, 0:len(tiles) * P]).then_inc(hT_kept, 1)

            act.wait_ge(C_done, 1)
            weigh(0, 0)
            for j, (t0, nt) in enumerate(HALVES):
                act.wait_ge(c3T_done, j + 1)
                nc.scalar.copy(c3T[:, t0 * P:(t0 + nt) * P], PS[j][0:E1, 0:nt * P]).then_inc(c3T_kept, 1)
            weigh(0, 1)
            for j, (t0, nt) in enumerate(HALVES):
                act.wait_ge(fb_done, j + 1)
                nc.scalar.copy(y2[:, t0:t0 + nt, :].rearrange("p t d -> p (t d)"), PS[j][:, 0:nt * P]).then_inc(fb_kept, 1)
            gelu(0)
            weigh(0, 2)
            keep_hT(0)
            gelu(1)
            weigh(1, 0)
            keep_hT(1)
            gelu(2)
            weigh(1, 1)
            keep_hT(2)
            weigh(1, 2)

        @block.vector
        def _(dve):
            steps = [0]

            def link(ins):
                steps[0] += 1
                ins.then_inc(v_step, 1)
                dve.wait_ge(v_step, steps[0])

            def layernorm(n, update=None):
                for j, (t0, nt) in enumerate(HALVES):
                    tiles = range(t0, t0 + nt)
                    if update is not None:
                        update(j).then_inc(x_new, 1)
                        dve.wait_ge(x_new, 2 * n + j - 1)
                    for t in tiles:
                        ins = nc.vector.bn_stats(stats[:, t, :], x[:, t, :])
                    link(ins)
                    for t in tiles:
                        ins = nc.vector.bn_aggr(mv[:, t, :], stats[:, t, :])
                    ins.then_inc(var_done, 1)
                    dve.wait_ge(sd_done, 2 * n + j + 1)
                    link(nc.vector.reciprocal(rstd[:, t0:t0 + nt], sd[:, t0:t0 + nt]))
                    for t in tiles:
                        ins = nc.vector.tensor_scalar(xn[:, t, :], x[:, t, :], mv[:, t, 0:1], rstd[:, t:t + 1], ALU.subtract, ALU.mult)
                    ins.then_inc(xn_done, 1)

            def keep_xT(n):
                dve.wait_ge(xnT_done, 2 * n + 2)
                nc.vector.tensor_copy(xT[:, 512:TOK], PS[5][:, 0:TOK - 512]).then_inc(xT_done, 1)

            def add_gated(src, j, gate):
                t0, nt = HALVES[j]
                part = x[:, t0:t0 + nt, :].rearrange("p t d -> p (t d)")
                return nc.vector.scalar_tensor_tensor(out=part, in0=src, scalar=tg[:, gate:gate + 1], in1=part,
                                                      op0=ALU.mult, op1=ALU.add)

            def bc(ap, n):
                return ap.unsqueeze(2).to_broadcast([P, ap.shape[1], n])

            link(nc.vector.memset(eps[:, :], EPS))
            nc.vector.memset(ones_row[:, :], 1.0)
            dve.wait_ge(x_loaded, 32)
            layernorm(0)
            dve.wait_ge(mask_loaded, 16)
            nc.vector.memset(maskr[:, SK:SKP].bitcast(F32), -BIG)
            nc.vector.tensor_scalar(maskr[:, 0:SK], mask8[:, :], -BIG, None, ALU.mult).then_inc(maskr_done, 1)
            for j in range(4):
                dve.wait_ge(m_done, j + 1)
                nc.vector.tensor_copy(M[:, 4 * j:4 * j + 4, :].rearrange("p h d -> p (h d)"), PS[4 + j]).then_inc(m_kept, 1)
            keep_xT(0)
            dve.wait_ge(small_loaded, 192)
            nc.vector.tensor_copy(pick[:, :], pick_f[:, :])
            nc.vector.tensor_copy(blockm[:, :, :], block_f[:, :, :]).then_inc(const_done, 1)
            qk_t = qk[:, :].rearrange("p (t h) -> p h t", h=H)
            dve.wait_ge(mask_stored, 16)
            for n in range(1, 2 * H, 2):
                half, h = divmod(n, H)
                dve.wait_ge(qk_done, n + 1)
                nc.vector.tensor_copy(qk_t[:, h, half * 448:(half + 1) * 448], PS[n % 4][:, 0:448]).then_inc(qk_kept[1], 1)

            def max0(u, par, n):
                cnt = UNITS[u][1]
                dve.wait_ge(s0_done, n + 1)
                nc.vector.tensor_reduce(nmax0[:, par, 0:cnt], PS[par].rearrange("p (g k) -> p g k", g=2)[:, 0:cnt, 0:GK],
                                        AX, ALU.max, negate=True).then_inc(max0_done, 1)

            def norm0(u, par, n):
                cnt = UNITS[u][1]
                dve.wait_ge(exp0_done, n + 1)
                nc.vector.reciprocal(rsum0[:, par, 0:cnt], psum0[:, par, 0:cnt]).then_inc(recip0_done, 1)
                dve.wait_ge(recip0_done, n + 1)
                for c in range(2):
                    half = slice(64 * c, 64 * c + 64)
                    ins = nc.vector.tensor_tensor(own[par][half, 0:cnt, :], p0[par][half, 0:cnt, c * CK:(c + 1) * CK],
                                                  rsum0[half, par, 0:cnt].unsqueeze(2).to_broadcast([64, cnt, CK]), ALU.mult)
                ins.then_inc(norm0_done, 1)

            def keep_p0T(u, par, n):
                cnt = UNITS[u][1]
                dve.wait_ge(p0T_done, n + 1)
                for c in range(2):
                    half = slice(64 * c, 64 * c + 64)
                    ins = nc.vector.tensor_copy(p0T[par][:, 0:cnt, c, half],
                                                PS[2 + par][0:CK, 0:cnt * P].rearrange("p (g q) -> p g q", g=cnt)[:, :, half])
                ins.then_inc(p0T_kept, 1)

            def body0(i, last):
                for k in range(SLOTS * NU):
                    n = i * (SLOTS * NU) + k
                    keep_p0T(k % NU, k % 2, n)
                    if not (last and k + AHEAD >= SLOTS * NU):
                        max0((k + AHEAD) % NU, (k + AHEAD) % 2, n + AHEAD)
                    if not (last and k + 3 >= SLOTS * NU):
                        dve.wait_ge(p0T_done, n + 2)
                        norm0((k + 3) % NU, (k + 3) % 2, n + 3)

            dve.wait_ge(pool_done, 5 * SLOTS)
            max0(0, 0, 0)
            max0(1, 1, 1)
            norm0(0, 0, 0)
            max0(2, 0, 2)
            norm0(1, 1, 1)
            max0(3, 1, 3)
            dve.wait_ge(p0T_done, 1)
            norm0(2, 0, 2)
            with dve.Fori(0, B // SLOTS - 1) as i:
                body0(i, False)
            body0(B // SLOTS - 1, True)

            dve.wait_ge(ac_bank_free, 2)

            def add_attention0(j):
                dve.wait_ge(o_done, j + 1)
                return add_gated(PS[j][:, 0:HALVES[j][1] * P], j, 0)

            layernorm(1, add_attention0)
            keep_xT(1)
            dve.wait_ge(gate_done, 1)
            logits = PS[6][:, 0:NT * E0].rearrange("p (t e) -> p t e", e=E0)
            link(nc.vector.tensor_reduce(top0[:, :], logits, AX, ALU.max))
            nc.vector.tensor_tensor(probs[:, :, :], logits, bc(top0[:, :], E0), ALU.subtract).then_inc(gate_sub, 1)
            dve.wait_ge(gate_exp, 1)
            link(nc.vector.tensor_reduce(top0[:, :], left[:, :, :], AX, ALU.add))
            link(nc.vector.reciprocal(top0[:, :], top0[:, :]))
            link(nc.vector.tensor_tensor(probs[:, :, :], left[:, :, :], bc(top0[:, :], E0), ALU.mult))
            link(nc.vector.tensor_copy(left[:, :, :], probs[:, :, :]))

            def first_largest(vals, pick_, top, n, order):
                link(nc.vector.tensor_reduce(top, vals, AX, ALU.max))
                link(nc.vector.tensor_tensor(pick_, vals, bc(top, n), ALU.is_equal))
                link(nc.vector.tensor_tensor(pick_, pick_, order, ALU.mult))
                link(nc.vector.tensor_reduce(top, pick_, AX, ALU.max))
                link(nc.vector.tensor_tensor(pick_, pick_, bc(top, n), ALU.is_equal))

            dve.wait_ge(order_done, 2)
            order0 = order_0[:, :, :]
            first_largest(left[:, :, :], pick0[:, :, :], top0[:, :], E0, order0)
            link(nc.vector.tensor_tensor(cw[:, :, :], pick0[:, :, :], probs[:, :, 0:1].to_broadcast([P, NT, E0]), ALU.mult))
            link(nc.vector.scalar_tensor_tensor(out=left[:, :, :], in0=pick0[:, :, :], scalar=-2.0, in1=left[:, :, :], op0=ALU.mult, op1=ALU.add))
            first_largest(left[:, :, :], pick0[:, :, :], top0[:, :], E0, order0)
            link(nc.vector.tensor_tensor(pick0[:, :, :], pick0[:, :, :], probs[:, :, 1:2].to_broadcast([P, NT, E0]), ALU.mult))
            nc.vector.tensor_tensor(cw[:, :, :], cw[:, :, :], pick0[:, :, :], ALU.add).then_inc(cw_done, 1)
            for j, (t0, nt) in enumerate(HALVES):
                dve.wait_ge(cwT_done, j + 1)
                nc.vector.tensor_copy(cwT[:, t0 * P:(t0 + nt) * P], PS[6 + j][0:E0, 0:nt * P]).then_inc(cwT_kept, 1)
            for j, (t0, nt) in enumerate(HALVES):
                dve.wait_ge(b3_done, j + 1)
                nc.vector.tensor_copy(acc0[:, t0:t0 + nt, :].rearrange("p t d -> p (t d)"), PS[6 + j][:, 0:nt * P]).then_inc(b3_kept, 1)
            dve.wait_ge(b3_kept, 2)
            def keep_k2(b, c, psum):
                dve.wait_ge(k1_kept, b * KC + c + 1)
                cols = slice(c * 512, (c + 1) * 512)
                nc.vector.scalar_tensor_tensor(out=k12[:, 1, cols], in0=psum, scalar=bcol[:, 0:1], in1=k12[:, 0, cols].bitcast(F32),
                                               op0=ALU.add, op1=ALU.subtract).then_inc(k2_kept, 1)

            for s in range(2 * E0):
                t0, nt = HALVES[s % 2]
                dve.wait_ge(l3_done, s + 1)
                if s >= 2:
                    dve.wait_ge(l3_kept, s - 1)
                for t in range(nt):
                    ins = nc.vector.scalar_tensor_tensor(out=acc0[:, t0 + t, :], in0=PS[4 + s % 2][:, t * P:(t + 1) * P],
                                                         scalar=cw[:, t0 + t, s // 2:s // 2 + 1], in1=acc0[:, t0 + t, :],
                                                         op0=ALU.mult, op1=ALU.add)
                ins.then_inc(l3_kept, 1)
                if 1 <= s <= SLOTS * 2 * KC:
                    b, piece = divmod(s - 1, 2 * KC)
                    if piece == KC:
                        dve.wait_ge(vones_done, 2 * b + 2)
                    if piece < KC:
                        keep_k2(b, piece, PS[7])
                    else:
                        keep_v(nc.vector.tensor_copy, dve, b, b, piece - KC, PS[7])

            def add_experts0(j):
                t0, nt = HALVES[j]
                dve.wait_ge(l3_kept, 2 * E0 - 1 + j)
                return add_gated(acc0[:, t0:t0 + nt, :].rearrange("p t d -> p (t d)"), j, 1)

            layernorm(2, add_experts0)
            nc.vector.memset(negm[:, :], 0.0).then_inc(const_done, 1)
            nc.vector.memset(negmT[:, :], 0.0).then_inc(pv_bank_free, 1)
            keep_xT(2)
            for m in range(2 * HG):
                j, g = divmod(m, HG)
                dve.wait_ge(q1_kept, m + 1)
                part = q96[GROWS:2 * GROWS, g, j * 448:(j + 1) * 448]
                nc.vector.scalar_tensor_tensor(out=part, in0=PS[m % 4][GROWS:2 * GROWS, 0:448], scalar=bq1[GROWS:2 * GROWS, g:g + 1],
                                               in1=part.bitcast(F32), op0=ALU.add, op1=ALU.subtract).then_inc(q2_kept, 1)

            def keep_max(b, m, first=None):
                c, pair = divmod(m, PAIRS)
                dve.wait_ge(m1_done, b * NM + m + 1)
                psum = MB[m % 2] if first is None else MB3[first % 3]
                nc.vector.tensor_reduce(mx3[:, pair, c:c + 1], psum[0:PQ, :], AX, ALU.max).then_inc(m1_kept, 1)

            def turn_max(b):
                dve.wait_ge(m1_kept, (b + 1) * NM)
                nc.vector.tensor_reduce(negm[0:PQ, 0:PAIRS].bitcast(F32R), mx3[:, :, :], AX, ALU.max, negate=True).then_inc(negm_done, 1)
                dve.wait_ge(negm_done, b + 1)
                nc.vector.transpose(negmT[:, :], negm[:, :]).then_inc(negmT_done, 1)

            def keep_pv(b):
                dve.wait_ge(pv_done, (b + 1) * KT)
                toks = bass.ds(b * SQ, SQ)
                nc.vector.tensor_copy(pv[:, 0:3, toks], PS[3][:, 0:3 * SQ].rearrange("p (c q) -> p c q", c=3))
                nc.vector.tensor_copy(pv[0:64, 3:5, toks], PS[3][0:64, 3 * SQ:5 * SQ].rearrange("p (c q) -> p c q", c=2)).then_inc(pv_bank_free, 1)

            def invert_sums(j, psum):
                t0, nt = HALVES[j]
                dve.wait_ge(sums_done, j + 1)
                nc.vector.reciprocal(rden[:, t0 * P:(t0 + nt) * P], psum[:, 0:nt * P]).then_inc(rden_done, 1)

            def divide(j, psum):
                t0, nt = HALVES[j]
                toks = slice(t0 * P, (t0 + nt) * P)
                dve.wait_ge(heads_done, j + 1)
                dve.wait_ge(rden_done, j + 1)
                link(nc.vector.tensor_tensor(oT[:, toks], psum[:, 0:nt * P], rden[:, toks], ALU.mult))
                nc.vector.tensor_scalar(oT[:, toks], oT[:, toks], bcol[:, 1:2], None, ALU.add).then_inc(oT_done, 1)

            for m in range(NM):
                keep_max(0, m, first=m)
            turn_max(0)
            for m in range(PAIRS):
                keep_max(1, m, first=NM + m)

            def body1(i, last):
                for s in range(SLOTS):
                    b = i * SLOTS + s
                    final = last and s == 1
                    for t in range(KT):
                        for m in (2 * t, 2 * t + 1):
                            if t < KT - 4 and not final:
                                keep_max(b + 1, PAIRS + m)
                            if t >= KT - 4 and not last:
                                keep_max(b + SLOTS, m - 2 * (KT - 4))
                            if m % 2 == 0:
                                if not last and t in (2, 4, 6):
                                    keep_k2(b + SLOTS, (t - 2) // 2, PS[0])
                                if t == KT - 1:
                                    keep_pv(b)
                        if t == KT - 5 and not final:
                            turn_max(b + 1)
                        if last and s == 0 and t == KT - 1:
                            invert_sums(0, PS[0])
                        if final and t == 1:
                            divide(0, PS[0])
                    if not last:
                        keep_v(nc.vector.tensor_copy, dve, b + SLOTS, s, 2, PS[0])

            with dve.Fori(0, B // SLOTS - 1) as i:
                body1(i, False)
            body1(B // SLOTS - 1, True)

            invert_sums(1, PS[0])
            divide(1, PS[1])

            def add_attention1(j):
                dve.wait_ge(o_done, 2 + j + 1)
                return add_gated(PS[2 + j][:, 0:HALVES[j][1] * P], j, 2)

            layernorm(3, add_attention1)
            keep_xT(3)
            dve.wait_ge(z_done, 1)
            link(nc.vector.tensor_copy(z[:, :, :].rearrange("p a e -> p (a e)"), PS[2][:, 0:NT * 3 * E1]))
            link(nc.vector.tensor_reduce(top2[:, :], z[:, :, :], AX, ALU.max))
            nc.vector.tensor_tensor(zl[:, :, :], z[:, :, :], bc(top2[:, :], E1), ALU.subtract).then_inc(zsub_done, 1)
            for k in range(TOPK1):
                first_largest(z[:, :, :], pk[:, :, :], top1[:, :], E1, order_1[:, :, :])
                if k == 0:
                    link(nc.vector.tensor_copy(sel[:, :, :], pk[:, :, :]))
                else:
                    link(nc.vector.tensor_tensor(sel[:, :, :], sel[:, :, :], pk[:, :, :], ALU.add))
                if k < TOPK1 - 1:
                    link(nc.vector.scalar_tensor_tensor(out=z[:, :, :], in0=pk[:, :, :], scalar=-BIG, in1=z[:, :, :], op0=ALU.mult, op1=ALU.add))
            dve.wait_ge(ez_done, 1)
            link(nc.vector.tensor_tensor(C[:, :, :], ez[:, :, :], sel[:, :, :], ALU.mult))
            link(nc.vector.tensor_reduce(top1[:, :], C[:, :, :], AX, ALU.add))
            link(nc.vector.reciprocal(top1[:, :], top1[:, :]))
            nc.vector.tensor_tensor(C[:, :, :], C[:, :, :], bc(top1[:, :], E1), ALU.mult).then_inc(C_done, 1)
            dve.wait_ge(C_done, 1)

            def add_experts(which, group, dst):
                tiles = MIX_TILES[group]
                count = (which * NT + tiles[0]) * ON_DVE
                for e in range(ON_DVE):
                    for t in tiles:
                        m = which * len(MIX) + MIX.index((t, e // 4))
                        if e % 4 == 0:
                            dve.wait_ge(mix_done, m + 1)
                        coef = C[:, 3 * t + which, e:e + 1]
                        src = MIXB[m % len(MIXB)][:, (e % 4) * D:(e % 4 + 1) * D]
                        if which == 0 and e == 0:
                            ins = nc.vector.tensor_scalar(dst[:, t, :], src, coef, None, ALU.mult)
                        else:
                            if e > 0:
                                dve.wait_ge(mix_added, count - len(tiles) + 1)
                            ins = nc.vector.scalar_tensor_tensor(out=dst[:, t, :], in0=src, scalar=coef, in1=dst[:, t, :],
                                                                 op0=ALU.mult, op1=ALU.add)
                        ins.then_inc(mix_added, 1)
                        count += 1

            def add_rest(which, group, dst):
                tiles = MIX_TILES[group]
                part = slice(tiles[0], tiles[-1] + 1)
                dve.wait_ge(rest_done, which * len(MIX_TILES) + group + 1)
                dve.wait_ge(mix_added, last_add(which * len(MIX) + MIX.index((tiles[-1], 1))))
                nc.vector.tensor_tensor(dst[:, part, :], dst[:, part, :], rest[:, part, 0, :], ALU.add).then_inc(y_done, 1)

            def update(group):
                tiles = MIX_TILES[group]
                part = slice(tiles[0], tiles[-1] + 1)
                add_rest(1, group, y2)
                dve.wait_ge(y_done, len(MIX_TILES) + group + 1)
                nc.vector.scalar_tensor_tensor(out=x[:, part, :], in0=y2[:, part, :], scalar=tg[:, 3:4], in1=x[:, part, :],
                                               op0=ALU.mult, op1=ALU.add).then_inc(x_new, 1)

            add_experts(0, 0, y1)
            add_experts(0, 1, y1)
            add_rest(0, 0, y1)
            add_experts(0, 2, y1)
            add_rest(0, 1, y1)
            dve.wait_ge(fb_kept, 2)
            add_experts(1, 0, y2)
            add_rest(0, 2, y1)
            add_experts(1, 1, y2)
            update(0)
            add_experts(1, 2, y2)
            update(1)
            update(2)


def kernel(**inputs):
    import numpy as np
    import concourse.bacc as bacc
    from concourse.bass_utils import run_bass_kernel_spmd

    v = {k: np.asarray(t) for k, t in inputs.items()}
    ctx = v["ctx_1024"]
    ctxT = np.zeros((B, P, SKP), ctx.dtype)
    ctxT[:, :, :SK] = ctx.transpose(0, 2, 1)
    ctxn = np.zeros((B, KPQ * SQ, D), ctx.dtype)
    ctxn[:, :SK] = ctx
    ctxn = ctxn.reshape(B, KPQ, 2 * NG, 4, D).transpose(0, 3, 1, 2, 4).reshape(B, CK, 2 * NG, D)
    pick = np.zeros((QG, QG, H), np.float32)
    block = np.full((QG, 3, QG, KPQ), -BIG, np.float32)
    for i in range(QG):
        pick[i, i] = 1
        for kind, whole in enumerate((QG, LASTQ % QG, 0)):
            block[i, kind, i, :KPQ - (i >= whole)] = 0

    pick_out = np.zeros((P, 2, PBLOCKS, P), np.float32)
    for first, cnt, row, col in PGROUPS:
        for i in range(cnt):
            for e in range(DH1):
                feature = (first + i) * DH1 + e
                pick_out[row + i * VH + e, 0, col // SQ + i, feature] = 1
                pick_out[row + i * VH + DH1, 1, col // SQ + i, feature] = 1

    def heads(w, transposed):
        w = w.T if transposed else w
        return w.reshape(H, DH0, D).transpose(1, 0, 2)

    wkv0, wkv1 = v["L0_xattn_Wkv"], v["L1_xattn_Wkv"]
    inner = H * DH0
    arrays = {
        "x": v["x"].reshape(NT, P, D).transpose(1, 0, 2),
        "ident": np.eye(P, dtype=np.float32),
        "wq0": heads(v["L0_xattn_Wq"], True),
        "wk0": heads(wkv0[:, :inner], True),
        "wv0": heads(wkv0[:, inner:], True),
        "wo0": heads(v["L0_xattn_Wout"], False),
        "ctxT": ctxT,
        "ctxn": ctxn,
        "pick": pick.reshape(QG, P),
        "block": block.reshape(QG, 3, GK),
        "rows": np.concatenate([v["L0_xattn_bout"], v["L1_xattn_bout"], v["L0_ffn_gate_b"]])[None],
        "gates": np.broadcast_to(np.stack([v["g_xattn"][0], v["g_ffn"][0], v["g_xattn"][1], v["g_ffn"][1]])[None], (P, 4)),
        "wq1": np.tile(v["L1_xattn_Wq"].reshape(D, HG, 1, GROWS), (1, 1, 3, 1)).reshape(D, HG, MASK_ROW),
        "bq1": np.tile(v["L1_xattn_bq"].reshape(HG, GROWS).T, (3, 1)),
        "own_head": np.tile(np.repeat(np.eye(GH, dtype=np.float32), DH1, axis=0), (3, 1)),
        "wk1": wkv1[:, :D],
        "wv1": wkv1[:, D:],
        "wo1": v["L1_xattn_Wout"],
        "bcol": np.stack([v["L1_xattn_bkv"][:D], v["L1_xattn_bkv"][D:]], 1),
        "pick_out": pick_out,
        "mask": v["mask_BxS2_bf0"],
        "w1": v["L0_ffn_w1"].transpose(1, 0, 2),
        "w2": v["L0_ffn_w2"].transpose(1, 0, 2),
        "w3": v["L0_ffn_w3"].transpose(1, 0, 2),
        "gwT": v["L0_ffn_gate_w"].T,
        "b12": np.stack([v["L0_ffn_b1"].T, v["L0_ffn_b2"].T], 1),
        "b3": v["L0_ffn_b3"],
        "f1": v["L1_ffn_W1"].transpose(2, 0, 1),
        "f2": v["L1_ffn_W2"].transpose(2, 0, 1),
        "pwT": v["L1_ffn_P_w"].T,
        "uT": np.concatenate([v["L1_ffn_U1"], v["L1_ffn_U2"], v["L1_ffn_U3"]]).T,
        "fb2": v["L1_ffn_b2"],
    }
    arrays = {k: np.ascontiguousarray(t) for k, t in arrays.items()}
    nc = bacc.Bacc("TRN2", target_bir_lowering=False, num_devices=1)
    aps = {k: nc.dram_tensor(f"in_{k}", t.shape, mybir.dt.from_np(t.dtype), kind="ExternalInput").ap()
           for k, t in arrays.items()}
    out = nc.dram_tensor("out", (TOK, D), F32, kind="ExternalOutput").ap()
    build(nc, aps, out.rearrange("(n p) d -> p n d", p=P))
    got = run_bass_kernel_spmd(nc, [{f"in_{k}": t for k, t in arrays.items()}], core_ids=[0])
    return got.results[0]["out"].reshape(B, SQ, D)
```
